# Optimizing a Trainium2 kernel written in Bass

```python
import numpy as np
import jax
import jax.numpy as jnp

def _softmax(x, axis=-1):
    return jax.nn.softmax(x, axis=axis)

def _gelu(x):
    return jax.nn.gelu(x, approximate=True)

def _silu(x):
    return jax.nn.silu(x)

def _sigmoid(x):
    return jax.nn.sigmoid(x)

def _layernorm(x, axis=-1, eps=1e-05):
    m = jnp.mean(x, axis=axis, keepdims=True)
    v = jnp.var(x, axis=axis, keepdims=True)
    return (x - m) / jnp.sqrt(v + eps)

def _scatter_add(tgt, idx, src, axis=0):
    return tgt.at[idx].add(src)

def _segment_sum(src, seg, n):
    return jax.ops.segment_sum(src, seg, n)
kernel_name = 'mk_decoder_preln_d4_seqx_r8_30cd80'

def setup_inputs(seed: int=0):
    np.random.seed(seed)
    _w = jnp.asarray

    def _rec_inputs():
        import jax
        import jax.numpy as jnp
        _rk = jax.random.key(seed)
        x = 0.0001212 + 1 * jax.random.normal(jax.random.fold_in(_rk, 1), (8, 128, 256), jnp.float32)
        _lenS = 128 - jax.random.randint(jax.random.fold_in(_rk, 7), (8,), 0, max(1, 128 // 4) + 1, jnp.int32)
        _lenS2 = 128 - jax.random.randint(jax.random.fold_in(_rk, 8), (8,), 0, max(1, 128 // 4) + 1, jnp.int32)
        _ctx_2048P = jax.random.normal(jax.random.fold_in(_rk, 11), (8, 16, 256), jnp.float32)
        _ctx_2048c = jax.random.dirichlet(jax.random.fold_in(_rk, 511), 0.3 * jnp.ones((16,), jnp.float32), (8, 128))
        _ctx_2048t = jnp.einsum('bsk,bkd->bsd', _ctx_2048c, _ctx_2048P)
        _ctx_2048t = _ctx_2048t * jax.lax.rsqrt(jnp.mean(jnp.square(_ctx_2048t)) + 1e-12) * 0.953939
        ctx_2048 = 0.000173663 + 1.0001 * (_ctx_2048t + 0.3 * jax.random.normal(jax.random.fold_in(_rk, 611), (8, 128, 256), jnp.float32))
        _validS = jnp.arange(128)[None, :] < _lenS[:, None]
        _validS2 = jnp.arange(128)[None, :] < _lenS2[:, None]
        _causal = jnp.tril(jnp.ones((128, 128), dtype=bool))
        mask_BxS2_if1 = jnp.where(jnp.ones((8, 128), dtype=bool), 1, 0).astype(jnp.int32)
        mask_BxS2_bk0 = jnp.logical_not(jnp.broadcast_to(_validS2[:, :], (8, 128)))
        return (x, ctx_2048, mask_BxS2_if1, mask_BxS2_bk0)
    x, ctx_2048, mask_BxS2_if1, mask_BxS2_bk0 = _rec_inputs()

    def _L0_attn_setup():
        import jax, jax.numpy as jnp
        import numpy as np
        from jax import lax
        B, L, D = (4, 256, 256)
        R = 256
        DH = D // 4
        key = jax.random.key(seed)
        ks = jax.random.split(key, 12)
        s = 0.02
        x = jax.random.normal(ks[0], (B, L, D), dtype=jnp.float32)
        Wu = jax.random.normal(ks[1], (R, D), dtype=jnp.float32) * s
        bu = jnp.zeros((R,), dtype=jnp.float32)
        Wv = jax.random.normal(ks[2], (R, D), dtype=jnp.float32) * s
        bv = jnp.zeros((R,), dtype=jnp.float32)
        Wg1 = jax.random.normal(ks[3], (DH, D), dtype=jnp.float32) * s
        bg1 = jnp.zeros((DH,), dtype=jnp.float32)
        Wg2 = jax.random.normal(ks[4], (R, DH), dtype=jnp.float32) * s
        bg2 = jnp.zeros((R,), dtype=jnp.float32)
        conv_w = jax.random.normal(ks[5], (D, 1, 3), dtype=jnp.float32) * s
        conv_b = jnp.zeros((D,), dtype=jnp.float32)
        return {'x': x, 'Wu': Wu, 'bu': bu, 'Wv': Wv, 'bv': bv, 'Wg1': Wg1, 'bg1': bg1, 'Wg2': Wg2, 'bg2': bg2, 'conv_w': conv_w, 'conv_b': conv_b}
    _L0_attn_all = _L0_attn_setup()
    _L0_attn_in = {k: v for k, v in _L0_attn_all.items() if k in ('Wu', 'bu', 'Wv', 'bv', 'Wg1', 'bg1', 'Wg2', 'bg2', 'conv_w', 'conv_b')}
    del _L0_attn_all

    def _L0_xattn_setup():
        import jax, jax.numpy as jnp
        import numpy as np
        B_DIM, T_DIM, C_DIM = (16, 128, 256)

        def _wkv(w, u, k, v):
            Bn, Tn, Cn = k.shape
            NEG_INF = jnp.float32(-1e+38)

            def step(carry, kv_t):
                p, q, o = carry
                kt, vt = kv_t
                no = jnp.maximum(o, u + kt)
                A = jnp.exp(o - no)
                E = jnp.exp(u + kt - no)
                y = (A * p + E * vt) / (A * q + E)
                no2 = jnp.maximum(w + o, kt)
                A2 = jnp.exp(w + o - no2)
                E2 = jnp.exp(kt - no2)
                return ((A2 * p + E2 * vt, A2 * q + E2, no2), y)
            init = (jnp.zeros((Bn, Cn), k.dtype), jnp.zeros((Bn, Cn), k.dtype), jnp.full((Bn, Cn), NEG_INF, k.dtype))
            kT = jnp.moveaxis(k, 1, 0)
            vT = jnp.moveaxis(v, 1, 0)
            _, yT = jax.lax.scan(step, init, (kT, vT))
            return jnp.moveaxis(yT, 0, 1)
        key = jax.random.key(seed)
        k1, k2, k3, k4 = jax.random.split(key, 4)
        w = -jnp.exp(jax.random.normal(k1, (C_DIM,), jnp.float32))
        u = jax.random.normal(k2, (C_DIM,), jnp.float32)
        k = jax.random.normal(k3, (B_DIM, T_DIM, C_DIM), jnp.float32)
        v = jax.random.normal(k4, (B_DIM, T_DIM, C_DIM), jnp.float32)
        return {'B': B_DIM, 'T': T_DIM, 'C': C_DIM, 'w': w, 'u': u, 'k': k, 'v': v}
    _L0_xattn_all = _L0_xattn_setup()
    _L0_xattn_in = {k: v for k, v in _L0_xattn_all.items() if k in ('w', 'u')}
    del _L0_xattn_all

    def _L0_ffn_setup():
        import jax, jax.numpy as jnp
        import numpy as np
        TOP_K = 4
        key = jax.random.key(seed)
        ks = jax.random.split(key, 5)
        H, I, E = (256, 96, 32)
        s = 0.02
        return {'hidden_states': jax.random.normal(ks[0], (1, 128, H), jnp.float32), 'router_w': jax.random.normal(ks[1], (E, H), jnp.float32) * s, 'gate_w': jax.random.normal(ks[2], (E, I, H), jnp.float32) * s, 'up_w': jax.random.normal(ks[3], (E, I, H), jnp.float32) * s, 'down_w': jax.random.normal(ks[4], (E, H, I), jnp.float32) * s}
    _L0_ffn_all = _L0_ffn_setup()
    _L0_ffn_in = {k: v for k, v in _L0_ffn_all.items() if k in ('router_w', 'gate_w', 'up_w', 'down_w')}
    del _L0_ffn_all

    def _L1_attn_setup():
        import jax, jax.numpy as jnp
        import numpy as np
        H = 32
        HKV = 8

        def _rope(t):
            B, h, S, dk = t.shape
            P = dk // 2
            theta = 1.0 / 10000.0 ** (2.0 * jnp.arange(P, dtype=jnp.float32) / dk)
            m_theta = jnp.arange(S, dtype=jnp.float32)[:, None] * theta[None, :]
            cos, sin = (jnp.cos(m_theta), jnp.sin(m_theta))
            tp = t.reshape(B, h, S, P, 2)
            t0, t1 = (tp[..., 0], tp[..., 1])
            rot = jnp.stack([t0 * cos - t1 * sin, t0 * sin + t1 * cos], axis=-1)
            return rot.reshape(B, h, S, dk)
        key = jax.random.key(seed)
        ks = jax.random.split(key, 5)
        B, S, D = (2, 128, 256)
        dk = D // H
        scale = 0.02
        x = jax.random.normal(ks[0], (B, S, D), dtype=jnp.float32)
        Wq = jax.random.normal(ks[1], (D, D), dtype=jnp.float32) * scale
        Wk = jax.random.normal(ks[2], (D, HKV * dk), dtype=jnp.float32) * scale
        Wv = jax.random.normal(ks[3], (D, HKV * dk), dtype=jnp.float32) * scale
        Wo = jax.random.normal(ks[4], (D, D), dtype=jnp.float32) * scale
        return {'x': x, 'Wq': Wq, 'Wk': Wk, 'Wv': Wv, 'Wo': Wo}
    _L1_attn_all = _L1_attn_setup()
    _L1_attn_in = {k: v for k, v in _L1_attn_all.items() if k in ('Wq', 'Wk', 'Wv', 'Wo')}
    del _L1_attn_all

    def _L1_xattn_setup():
        import jax, jax.numpy as jnp
        import numpy as np
        HIDDEN = 256
        NUM_HEADS = 16
        NUM_KV_HEADS = 4
        HEAD_DIM = 128
        ROPE_THETA = 10000.0
        EPS = 1e-06

        def rms_norm(x, w, eps=EPS):
            var = jnp.mean(jnp.square(x), axis=-1, keepdims=True)
            return x * jax.lax.rsqrt(var + eps) * w

        def rope_cache(L, head_dim, theta, dtype):
            inv_freq = 1.0 / theta ** (jnp.arange(0, head_dim, 2, dtype=jnp.float32) / head_dim)
            t = jnp.arange(L, dtype=jnp.float32)
            freqs = jnp.outer(t, inv_freq)
            emb = jnp.concatenate([freqs, freqs], -1)
            cos = jnp.cos(emb).astype(dtype)[None, :, None, :]
            sin = jnp.sin(emb).astype(dtype)[None, :, None, :]
            return (cos, sin)

        def rotate_half(x):
            x1, x2 = jnp.split(x, 2, axis=-1)
            return jnp.concatenate([-x2, x1], axis=-1)
        key = jax.random.key(seed)
        ks = jax.random.split(key, 10)
        B, L, T = (2, 256, 64)
        q_out = NUM_HEADS * HEAD_DIM
        kv_out = NUM_KV_HEADS * HEAD_DIM
        s = lambda fan_in: 1.0 / np.sqrt(fan_in)
        return {'x': jax.random.normal(ks[0], (B, L, HIDDEN), jnp.float32), 'h_ctx_kv': jax.random.normal(ks[1], (B, T, HIDDEN), jnp.float32), 'wq': jax.random.normal(ks[2], (HIDDEN, q_out), jnp.float32) * s(HIDDEN), 'wk': jax.random.normal(ks[3], (HIDDEN, kv_out), jnp.float32) * s(HIDDEN), 'wv': jax.random.normal(ks[4], (HIDDEN, kv_out), jnp.float32) * s(HIDDEN), 'wo': jax.random.normal(ks[5], (q_out, HIDDEN), jnp.float32) * s(q_out), 'wk_ctx': jax.random.normal(ks[6], (HIDDEN, kv_out), jnp.float32) * s(HIDDEN), 'wv_ctx': jax.random.normal(ks[7], (HIDDEN, kv_out), jnp.float32) * s(HIDDEN), 'q_norm_w': jnp.ones((HEAD_DIM,), jnp.float32), 'k_norm_w': jnp.ones((HEAD_DIM,), jnp.float32)}
    _L1_xattn_all = _L1_xattn_setup()
    _L1_xattn_in = {k: v for k, v in _L1_xattn_all.items() if k in ('wq', 'wk', 'wv', 'wo', 'wk_ctx', 'wv_ctx', 'q_norm_w', 'k_norm_w')}
    del _L1_xattn_all

    def _L1_ffn_setup():
        import jax, jax.numpy as jnp
        import numpy as np
        N, S, D = (8, 256, 256)
        O = 256
        E = 8
        K = 2
        key = jax.random.key(seed)
        ks = jax.random.split(key, 5)
        scale_in = 1.0 / np.sqrt(D)
        x = jax.random.normal(ks[0], (N, S, D), dtype=jnp.float32)
        gate_w = jax.random.uniform(ks[1], (D, E), dtype=jnp.float32, minval=-scale_in, maxval=scale_in)
        gate_b = jax.random.uniform(ks[2], (E,), dtype=jnp.float32, minval=-scale_in, maxval=scale_in)
        expert_w = jax.random.uniform(ks[3], (E, D, O), dtype=jnp.float32, minval=-scale_in, maxval=scale_in)
        expert_b = jax.random.uniform(ks[4], (E, O), dtype=jnp.float32, minval=-scale_in, maxval=scale_in)
        return {'x': x, 'gate_w': gate_w, 'gate_b': gate_b, 'expert_w': expert_w, 'expert_b': expert_b}
    _L1_ffn_all = _L1_ffn_setup()
    _L1_ffn_in = {k: v for k, v in _L1_ffn_all.items() if k in ('gate_w', 'gate_b', 'expert_w', 'expert_b')}
    del _L1_ffn_all

    def _L2_attn_setup():
        import jax, jax.numpy as jnp
        import numpy as np
        D_MODEL = 256
        D_STATE = 128
        D_CONV = 4
        EXPAND = 2
        HEADDIM = 64
        CHUNK = 64
        D_INNER = EXPAND * D_MODEL
        NHEADS = D_INNER // HEADDIM
        CONV_DIM = D_INNER + 2 * D_STATE
        D_IN_PROJ = 2 * D_INNER + 2 * D_STATE + NHEADS
        BATCH, SEQLEN = (2, 256)

        def segsum(x):
            T = x.shape[-1]
            xx = jnp.broadcast_to(x[..., :, None], x.shape + (T,))
            mask_lower = jnp.tril(jnp.ones((T, T), dtype=bool), -1)
            s = jnp.cumsum(jnp.where(mask_lower, xx, 0.0), axis=-2)
            mask_diag = jnp.tril(jnp.ones((T, T), dtype=bool), 0)
            return jnp.where(mask_diag, s, -jnp.inf)

        def ssd(x, A, Bm, Cm, chunk):
            b, L, h, p = x.shape
            c = L // chunk
            x = x.reshape(b, c, chunk, h, p)
            A = A.reshape(b, c, chunk, h).transpose(0, 3, 1, 2)
            Bm = Bm.reshape(b, c, chunk, -1)
            Cm = Cm.reshape(b, c, chunk, -1)
            A_cum = jnp.cumsum(A, axis=-1)
            Lmat = jnp.exp(segsum(A))
            Y_diag = jnp.einsum('bcln,bcsn,bhcls,bcshp->bclhp', Cm, Bm, Lmat, x)
            decay_states = jnp.exp(A_cum[..., -1:] - A_cum)
            states = jnp.einsum('bcln,bhcl,bclhp->bchpn', Bm, decay_states, x)
            init = jnp.zeros_like(states[:, :1])
            states = jnp.concatenate([init, states], axis=1)
            A_last = jnp.pad(A_cum[..., -1], ((0, 0), (0, 0), (1, 0)))
            decay_chunk = jnp.exp(segsum(A_last))
            new_states = jnp.einsum('bhzc,bchpn->bzhpn', decay_chunk, states)
            states, final_state = (new_states[:, :-1], new_states[:, -1])
            out_decay = jnp.exp(A_cum)
            Y_off = jnp.einsum('bcln,bchpn,bhcl->bclhp', Cm, states, out_decay)
            return ((Y_diag + Y_off).reshape(b, L, h, p), final_state)
        key = jax.random.key(seed)
        ks = jax.random.split(key, 8)
        u = jax.random.normal(ks[0], (BATCH, SEQLEN, D_MODEL), jnp.float32)
        W_in = jax.random.normal(ks[1], (D_MODEL, D_IN_PROJ), jnp.float32) / np.sqrt(D_MODEL).astype(np.float32)
        conv_w = jax.random.normal(ks[2], (CONV_DIM, D_CONV), jnp.float32) * np.sqrt(2.0 / D_CONV).astype(np.float32)
        conv_b = jnp.zeros((CONV_DIM,), jnp.float32)
        dt_bias = jax.random.uniform(ks[3], (NHEADS,), jnp.float32, minval=-2.0, maxval=2.0)
        A_log = jax.random.normal(ks[4], (NHEADS,), jnp.float32) * 0.1
        D_param = jnp.ones((NHEADS,), jnp.float32)
        norm_w = jnp.ones((D_INNER,), jnp.float32)
        W_out = jax.random.normal(ks[5], (D_INNER, D_MODEL), jnp.float32) / np.sqrt(D_INNER).astype(np.float32)
        return {'u': u, 'W_in': W_in, 'conv_w': conv_w, 'conv_b': conv_b, 'dt_bias': dt_bias, 'A_log': A_log, 'D_param': D_param, 'norm_w': norm_w, 'W_out': W_out}
    _L2_attn_all = _L2_attn_setup()
    _L2_attn_in = {k: v for k, v in _L2_attn_all.items() if k in ('W_in', 'conv_w', 'conv_b', 'dt_bias', 'A_log', 'D_param', 'norm_w', 'W_out')}
    del _L2_attn_all

    def _L2_xattn_setup():
        import jax, jax.numpy as jnp
        import numpy as np
        D_MODEL = 256
        N_HEADS = 32
        N_GROUPS = 8
        HEAD_DIM = D_MODEL // N_HEADS
        BATCH, SEQ = (2, 128)
        NEG_INF = float('-inf')
        key = jax.random.key(seed)
        ks = jax.random.split(key, 9)
        s = 0.02
        return {'Q': jax.random.normal(ks[0], (BATCH, SEQ, D_MODEL), jnp.float32), 'K': jax.random.normal(ks[1], (BATCH, SEQ, D_MODEL), jnp.float32), 'V': jax.random.normal(ks[2], (BATCH, SEQ, D_MODEL), jnp.float32), 'attention_mask': jnp.ones((BATCH, SEQ), jnp.int32), 'w_q': jax.random.normal(ks[3], (D_MODEL, D_MODEL), jnp.float32) * s, 'w_k': jax.random.normal(ks[4], (HEAD_DIM * N_GROUPS, D_MODEL), jnp.float32) * s, 'w_v': jax.random.normal(ks[5], (HEAD_DIM * N_GROUPS, D_MODEL), jnp.float32) * s, 'w_o': jax.random.normal(ks[6], (D_MODEL, D_MODEL), jnp.float32) * s, 'b_o': jnp.zeros((D_MODEL,), jnp.float32)}
    _L2_xattn_all = _L2_xattn_setup()
    _L2_xattn_in = {k: v for k, v in _L2_xattn_all.items() if k in ('w_q', 'w_k', 'w_v', 'w_o', 'b_o')}
    del _L2_xattn_all

    def _L2_ffn_setup():
        import jax, jax.numpy as jnp
        import numpy as np
        EPS = 1e-05
        RMS_EPS = 1e-06

        def _rmsnorm(x):
            return x * jax.lax.rsqrt(jnp.mean(x * x, axis=-1, keepdims=True) + RMS_EPS)

        def _act_quant(x):
            scale = 127.0 / jnp.clip(jnp.max(jnp.abs(x), axis=-1, keepdims=True), EPS)
            q = jnp.round(jnp.clip(x * scale, -128.0, 127.0)) / scale
            return x + jax.lax.stop_gradient(q - x)

        def _weight_quant(w):
            scale = 1.0 / jnp.clip(jnp.mean(jnp.abs(w)), EPS)
            q = jnp.round(jnp.clip(w * scale, -1.0, 1.0)) / scale
            return w + jax.lax.stop_gradient(q - w)

        def _bitlinear(x, w):
            xq = _act_quant(_rmsnorm(x))
            wq = _weight_quant(w)
            return jnp.einsum('bsi,oi->bso', xq, wq)
        key = jax.random.key(seed)
        k1, k2, k3, k4 = jax.random.split(key, 4)
        B, S, D, F = (2, 256, 256, 1024)
        x = jax.random.normal(k1, (B, S, D), dtype=jnp.float32)
        w_gate = jax.random.normal(k2, (F, D), dtype=jnp.float32) * 0.02
        w_up = jax.random.normal(k3, (F, D), dtype=jnp.float32) * 0.02
        w_down = jax.random.normal(k4, (D, F), dtype=jnp.float32) * 0.02
        return {'x': x, 'w_gate': w_gate, 'w_up': w_up, 'w_down': w_down}
    _L2_ffn_all = _L2_ffn_setup()
    _L2_ffn_in = {k: v for k, v in _L2_ffn_all.items() if k in ('w_gate', 'w_up', 'w_down')}
    del _L2_ffn_all

    def _L3_attn_setup():
        import jax, jax.numpy as jnp
        import numpy as np
        D_MODEL = 256
        D_INNER = 512
        D_STATE = 64
        N_QK_HEADS = 8
        N_V_HEADS = 64
        CHUNK = 128
        KSIZE = 4
        CONV_DIM = D_INNER + 2 * N_QK_HEADS * D_STATE
        PROJ_DIM = CONV_DIM + D_INNER + N_V_HEADS

        def segsum(x):
            T = x.shape[-1]
            xe = jnp.broadcast_to(x[..., None], x.shape + (T,))
            strict_lower = jnp.tril(jnp.ones((T, T), dtype=bool), -1)
            xe = jnp.where(strict_lower, xe, 0.0)
            s = jnp.cumsum(xe, axis=-2)
            lower = jnp.tril(jnp.ones((T, T), dtype=bool), 0)
            return jnp.where(lower, s, -jnp.inf)

        def ssd_chunk_scan(X, dA, Bm, Cm, chunk):
            b, l, h, p = X.shape
            g = Bm.shape[2]
            rep = h // g
            Bm = jnp.repeat(Bm, rep, axis=2)
            Cm = jnp.repeat(Cm, rep, axis=2)
            c = l // chunk
            X = X.reshape(b, c, chunk, h, p)
            Bm = Bm.reshape(b, c, chunk, h, -1)
            Cm = Cm.reshape(b, c, chunk, h, -1)
            A = jnp.transpose(dA.reshape(b, c, chunk, h), (0, 3, 1, 2))
            A_cum = jnp.cumsum(A, axis=-1)
            Lm = jnp.exp(segsum(A))
            Y_diag = jnp.einsum('bcshn,bczhn,bhcsz,bczhp->bcshp', Cm, Bm, Lm, X)
            decay_states = jnp.exp(A_cum[..., -1:] - A_cum)
            states = jnp.einsum('bcshn,bhcs,bcshp->bchpn', Bm, decay_states, X)
            states = jnp.concatenate([jnp.zeros_like(states[:, :1]), states], axis=1)
            chunk_sums = jnp.pad(A_cum[..., -1], ((0, 0), (0, 0), (1, 0)))
            decay_chunk = jnp.exp(segsum(chunk_sums))
            new_states = jnp.einsum('bhzc,bchpn->bzhpn', decay_chunk, states)
            states = new_states[:, :-1]
            state_decay_out = jnp.exp(A_cum)
            Y_off = jnp.einsum('bcshn,bchpn,bhcs->bcshp', Cm, states, state_decay_out)
            return (Y_diag + Y_off).reshape(b, l, h, p)
        key = jax.random.key(seed)
        ks = jax.random.split(key, 6)
        input_ = jax.random.normal(ks[0], (2, 512, D_MODEL), dtype=jnp.float32)
        in_proj_w = jax.random.normal(ks[1], (PROJ_DIM, D_MODEL), dtype=jnp.float32) * (2.0 / D_MODEL) ** 0.5
        cb = (CONV_DIM * KSIZE) ** (-0.5)
        conv1d_weight = jax.random.uniform(ks[2], (CONV_DIM, 1, KSIZE), dtype=jnp.float32, minval=-cb, maxval=cb)
        conv1d_bias = jax.random.uniform(ks[3], (CONV_DIM,), dtype=jnp.float32, minval=-0.5, maxval=0.5)
        z_bias = jnp.zeros((D_INNER,), dtype=jnp.float32)
        D = jnp.ones((N_V_HEADS,), dtype=jnp.float32)
        out_proj_w = jax.random.normal(ks[4], (D_MODEL, D_INNER), dtype=jnp.float32) * (2.0 / D_INNER) ** 0.5
        return {'input_': input_, 'in_proj_w': in_proj_w, 'conv1d_weight': conv1d_weight, 'conv1d_bias': conv1d_bias, 'z_bias': z_bias, 'D': D, 'out_proj_w': out_proj_w}
    _L3_attn_all = _L3_attn_setup()
    _L3_attn_in = {k: v for k, v in _L3_attn_all.items() if k in ('in_proj_w', 'conv1d_weight', 'conv1d_bias', 'z_bias', 'D', 'out_proj_w')}
    del _L3_attn_all

    def _L3_xattn_setup():
        import jax, jax.numpy as jnp
        import numpy as np
        key = jax.random.key(seed)
        k1, k2, k3 = jax.random.split(key, 3)
        B, S, D, M = (8, 256, 256, 128)
        hidden_states = jax.random.normal(k1, (B, S, D), dtype=jnp.float32)
        memory_tokens = jax.random.normal(k2, (B, M, D), dtype=jnp.float32)
        memory_mask = jax.random.randint(k3, (B, M), 0, 2).astype(jnp.bool_)
        return {'hidden_states': hidden_states, 'memory_tokens': memory_tokens, 'memory_mask': memory_mask}
    _L3_xattn_all = _L3_xattn_setup()
    _L3_xattn_in = {k: v for k, v in _L3_xattn_all.items() if k in ()}
    del _L3_xattn_all

    def _L3_ffn_setup():
        import jax, jax.numpy as jnp
        import numpy as np
        N_BLOCKS = 16
        BLOCK_SIZE = 64
        TOP_K = N_BLOCKS // 4
        key = jax.random.key(seed)
        k1, k2, k3, k4, k5 = jax.random.split(key, 5)
        in_f, out_f = (256, 1024)
        x = jax.random.normal(k1, (2, 512, in_f), dtype=jnp.float32)
        Wr = jax.random.normal(k2, (N_BLOCKS, in_f), dtype=jnp.float32) * in_f ** (-0.5)
        br = jnp.zeros((N_BLOCKS,), dtype=jnp.float32)
        W1 = jax.random.normal(k3, (out_f, in_f), dtype=jnp.float32) * in_f ** (-0.5)
        W2 = jax.random.normal(k4, (in_f, out_f), dtype=jnp.float32) * out_f ** (-0.5)
        return {'x': x, 'Wr': Wr, 'br': br, 'W1': W1, 'W2': W2}
    _L3_ffn_all = _L3_ffn_setup()
    _L3_ffn_in = {k: v for k, v in _L3_ffn_all.items() if k in ('Wr', 'br', 'W1', 'W2')}
    del _L3_ffn_all
    return {'x': x, 'ctx_2048': ctx_2048, 'mask_BxS2_if1': mask_BxS2_if1, 'mask_BxS2_bk0': mask_BxS2_bk0, 'L0_attn_Wu': _L0_attn_in['Wu'], 'L0_attn_bu': _L0_attn_in['bu'], 'L0_attn_Wv': _L0_attn_in['Wv'], 'L0_attn_bv': _L0_attn_in['bv'], 'L0_attn_Wg1': _L0_attn_in['Wg1'], 'L0_attn_bg1': _L0_attn_in['bg1'], 'L0_attn_Wg2': _L0_attn_in['Wg2'], 'L0_attn_bg2': _L0_attn_in['bg2'], 'L0_attn_conv_w': _L0_attn_in['conv_w'], 'L0_attn_conv_b': _L0_attn_in['conv_b'], 'L0_xattn_w': _L0_xattn_in['w'], 'L0_xattn_u': _L0_xattn_in['u'], 'L0_ffn_router_w': _L0_ffn_in['router_w'], 'L0_ffn_gate_w': _L0_ffn_in['gate_w'], 'L0_ffn_up_w': _L0_ffn_in['up_w'], 'L0_ffn_down_w': _L0_ffn_in['down_w'], 'L1_attn_Wq': _L1_attn_in['Wq'], 'L1_attn_Wk': _L1_attn_in['Wk'], 'L1_attn_Wv': _L1_attn_in['Wv'], 'L1_attn_Wo': _L1_attn_in['Wo'], 'L1_xattn_wq': _L1_xattn_in['wq'], 'L1_xattn_wk': _L1_xattn_in['wk'], 'L1_xattn_wv': _L1_xattn_in['wv'], 'L1_xattn_wo': _L1_xattn_in['wo'], 'L1_xattn_wk_ctx': _L1_xattn_in['wk_ctx'], 'L1_xattn_wv_ctx': _L1_xattn_in['wv_ctx'], 'L1_xattn_q_norm_w': _L1_xattn_in['q_norm_w'], 'L1_xattn_k_norm_w': _L1_xattn_in['k_norm_w'], 'L1_ffn_gate_w': _L1_ffn_in['gate_w'], 'L1_ffn_gate_b': _L1_ffn_in['gate_b'], 'L1_ffn_expert_w': _L1_ffn_in['expert_w'], 'L1_ffn_expert_b': _L1_ffn_in['expert_b'], 'L2_attn_W_in': _L2_attn_in['W_in'], 'L2_attn_conv_w': _L2_attn_in['conv_w'], 'L2_attn_conv_b': _L2_attn_in['conv_b'], 'L2_attn_dt_bias': _L2_attn_in['dt_bias'], 'L2_attn_A_log': _L2_attn_in['A_log'], 'L2_attn_D_param': _L2_attn_in['D_param'], 'L2_attn_norm_w': _L2_attn_in['norm_w'], 'L2_attn_W_out': _L2_attn_in['W_out'], 'L2_xattn_w_q': _L2_xattn_in['w_q'], 'L2_xattn_w_k': _L2_xattn_in['w_k'], 'L2_xattn_w_v': _L2_xattn_in['w_v'], 'L2_xattn_w_o': _L2_xattn_in['w_o'], 'L2_xattn_b_o': _L2_xattn_in['b_o'], 'L2_ffn_w_gate': _L2_ffn_in['w_gate'], 'L2_ffn_w_up': _L2_ffn_in['w_up'], 'L2_ffn_w_down': _L2_ffn_in['w_down'], 'L3_attn_in_proj_w': _L3_attn_in['in_proj_w'], 'L3_attn_conv1d_weight': _L3_attn_in['conv1d_weight'], 'L3_attn_conv1d_bias': _L3_attn_in['conv1d_bias'], 'L3_attn_z_bias': _L3_attn_in['z_bias'], 'L3_attn_D': _L3_attn_in['D'], 'L3_attn_out_proj_w': _L3_attn_in['out_proj_w'], 'L3_ffn_Wr': _L3_ffn_in['Wr'], 'L3_ffn_br': _L3_ffn_in['br'], 'L3_ffn_W1': _L3_ffn_in['W1'], 'L3_ffn_W2': _L3_ffn_in['W2']}

def reference(x, ctx_2048, mask_BxS2_if1, mask_BxS2_bk0, L0_attn_Wu, L0_attn_bu, L0_attn_Wv, L0_attn_bv, L0_attn_Wg1, L0_attn_bg1, L0_attn_Wg2, L0_attn_bg2, L0_attn_conv_w, L0_attn_conv_b, L0_xattn_w, L0_xattn_u, L0_ffn_router_w, L0_ffn_gate_w, L0_ffn_up_w, L0_ffn_down_w, L1_attn_Wq, L1_attn_Wk, L1_attn_Wv, L1_attn_Wo, L1_xattn_wq, L1_xattn_wk, L1_xattn_wv, L1_xattn_wo, L1_xattn_wk_ctx, L1_xattn_wv_ctx, L1_xattn_q_norm_w, L1_xattn_k_norm_w, L1_ffn_gate_w, L1_ffn_gate_b, L1_ffn_expert_w, L1_ffn_expert_b, L2_attn_W_in, L2_attn_conv_w, L2_attn_conv_b, L2_attn_dt_bias, L2_attn_A_log, L2_attn_D_param, L2_attn_norm_w, L2_attn_W_out, L2_xattn_w_q, L2_xattn_w_k, L2_xattn_w_v, L2_xattn_w_o, L2_xattn_b_o, L2_ffn_w_gate, L2_ffn_w_up, L2_ffn_w_down, L3_attn_in_proj_w, L3_attn_conv1d_weight, L3_attn_conv1d_bias, L3_attn_z_bias, L3_attn_D, L3_attn_out_proj_w, L3_ffn_Wr, L3_ffn_br, L3_ffn_W1, L3_ffn_W2):
    import jax
    import jax.numpy as jnp

    def _L0_attn_ref(x, Wu, bu, Wv, bv, Wg1, bg1, Wg2, bg2, conv_w, conv_b):
        import jax, jax.numpy as jnp
        import numpy as np
        from jax import lax
        B, L, D = (4, 256, 256)
        R = 256
        DH = D // 4
        xc = jnp.transpose(x, (0, 2, 1))
        t = lax.conv_general_dilated(xc, conv_w, window_strides=(1,), padding=[(1, 1)], dimension_numbers=('NCH', 'OIH', 'NCH'), feature_group_count=D)
        t_out = jnp.transpose(t + conv_b[None, :, None], (0, 2, 1))
        u = jnp.einsum('bld,rd->blr', x, Wu) + bu
        v = jnp.einsum('bld,rd->blr', x, Wv) + bv
        h = jax.nn.relu(jnp.einsum('bld,hd->blh', x, Wg1) + bg1)
        gates = jax.nn.sigmoid(jnp.einsum('blh,rh->blr', h, Wg2) + bg2)
        u_gated = u * gates
        v_gated = v * gates
        k_cumsum = jnp.cumsum(u_gated, axis=1)
        global_out = k_cumsum * v_gated
        uv_term = jnp.einsum('blr,rd->bld', global_out, Wu.T[:R, :])
        return t_out + uv_term

    def _L0_xattn_ref(B, T, C, w, u, k, v):
        import jax, jax.numpy as jnp
        import numpy as np
        B_DIM, T_DIM, C_DIM = (16, 128, 256)

        def _wkv(w, u, k, v):
            Bn, Tn, Cn = k.shape
            NEG_INF = jnp.float32(-1e+38)

            def step(carry, kv_t):
                p, q, o = carry
                kt, vt = kv_t
                no = jnp.maximum(o, u + kt)
                A = jnp.exp(o - no)
                E = jnp.exp(u + kt - no)
                y = (A * p + E * vt) / (A * q + E)
                no2 = jnp.maximum(w + o, kt)
                A2 = jnp.exp(w + o - no2)
                E2 = jnp.exp(kt - no2)
                return ((A2 * p + E2 * vt, A2 * q + E2, no2), y)
            init = (jnp.zeros((Bn, Cn), k.dtype), jnp.zeros((Bn, Cn), k.dtype), jnp.full((Bn, Cn), NEG_INF, k.dtype))
            kT = jnp.moveaxis(k, 1, 0)
            vT = jnp.moveaxis(v, 1, 0)
            _, yT = jax.lax.scan(step, init, (kT, vT))
            return jnp.moveaxis(yT, 0, 1)
        return _wkv(w, u, k, v)

    def _L0_ffn_ref(hidden_states, router_w, gate_w, up_w, down_w):
        import jax, jax.numpy as jnp
        import numpy as np
        TOP_K = 4
        B, S, H = hidden_states.shape
        E = router_w.shape[0]
        x = hidden_states.reshape(-1, H)
        logits = x @ router_w.T
        probs = jax.nn.softmax(logits.astype(jnp.float32), axis=-1)
        rw, sel = jax.lax.top_k(probs, TOP_K)
        rw = rw / jnp.sum(rw, axis=-1, keepdims=True)
        rw = rw.astype(x.dtype)

        def body(acc, expert):
            gw, uw, dw, e = expert
            w_tok = jnp.sum(jnp.where(sel == e, rw, 0.0), axis=-1)
            h = jax.nn.silu(x @ gw.T) * (x @ uw.T)
            y = h @ dw.T
            return (acc + w_tok[:, None] * y, None)
        acc0 = jnp.zeros_like(x)
        out, _ = jax.lax.scan(body, acc0, (gate_w, up_w, down_w, jnp.arange(E)))
        return out.reshape(B, S, H)

    def _L1_attn_ref(x, Wq, Wk, Wv, Wo):
        import jax, jax.numpy as jnp
        import numpy as np
        H = 32
        HKV = 8

        def _rope(t):
            B, h, S, dk = t.shape
            P = dk // 2
            theta = 1.0 / 10000.0 ** (2.0 * jnp.arange(P, dtype=jnp.float32) / dk)
            m_theta = jnp.arange(S, dtype=jnp.float32)[:, None] * theta[None, :]
            cos, sin = (jnp.cos(m_theta), jnp.sin(m_theta))
            tp = t.reshape(B, h, S, P, 2)
            t0, t1 = (tp[..., 0], tp[..., 1])
            rot = jnp.stack([t0 * cos - t1 * sin, t0 * sin + t1 * cos], axis=-1)
            return rot.reshape(B, h, S, dk)
        B, S, D = x.shape
        dk = D // H
        G = H // HKV
        q = (x @ Wq).reshape(B, S, H, dk).transpose(0, 2, 1, 3)
        k = (x @ Wk).reshape(B, S, HKV, dk).transpose(0, 2, 1, 3)
        v = (x @ Wv).reshape(B, S, HKV, dk).transpose(0, 2, 1, 3)
        q = _rope(q)
        k = _rope(k)
        qg = q.reshape(B, HKV, G, S, dk)
        scores = jnp.einsum('bhgqd,bhkd->bhgqk', qg, k) / jnp.sqrt(jnp.float32(dk))
        mask = jnp.triu(jnp.full((S, S), jnp.finfo(jnp.float32).min, dtype=jnp.float32), 1)
        attn = jax.nn.softmax(scores + mask, axis=-1)
        out = jnp.einsum('bhgqk,bhkd->bhgqd', attn, v)
        out = out.reshape(B, H, S, dk).transpose(0, 2, 1, 3).reshape(B, S, D)
        return out @ Wo

    def _L1_xattn_ref(x, h_ctx_kv, wq, wk, wv, wo, wk_ctx, wv_ctx, q_norm_w, k_norm_w):
        import jax, jax.numpy as jnp
        import numpy as np
        HIDDEN = 256
        NUM_HEADS = 16
        NUM_KV_HEADS = 4
        HEAD_DIM = 128
        ROPE_THETA = 10000.0
        EPS = 1e-06

        def rms_norm(x, w, eps=EPS):
            var = jnp.mean(jnp.square(x), axis=-1, keepdims=True)
            return x * jax.lax.rsqrt(var + eps) * w

        def rope_cache(L, head_dim, theta, dtype):
            inv_freq = 1.0 / theta ** (jnp.arange(0, head_dim, 2, dtype=jnp.float32) / head_dim)
            t = jnp.arange(L, dtype=jnp.float32)
            freqs = jnp.outer(t, inv_freq)
            emb = jnp.concatenate([freqs, freqs], -1)
            cos = jnp.cos(emb).astype(dtype)[None, :, None, :]
            sin = jnp.sin(emb).astype(dtype)[None, :, None, :]
            return (cos, sin)

        def rotate_half(x):
            x1, x2 = jnp.split(x, 2, axis=-1)
            return jnp.concatenate([-x2, x1], axis=-1)
        B, L, _ = x.shape
        T = h_ctx_kv.shape[1]
        rep = NUM_HEADS // NUM_KV_HEADS
        q = (x @ wq).reshape(B, L, NUM_HEADS, HEAD_DIM)
        k = (x @ wk).reshape(B, L, NUM_KV_HEADS, HEAD_DIM)
        v = (x @ wv).reshape(B, L, NUM_KV_HEADS, HEAD_DIM)
        q = rms_norm(q, q_norm_w)
        k = rms_norm(k, k_norm_w)
        k_ctx = (h_ctx_kv @ wk_ctx).reshape(B, T, NUM_KV_HEADS, HEAD_DIM)
        v_ctx = (h_ctx_kv @ wv_ctx).reshape(B, T, NUM_KV_HEADS, HEAD_DIM)
        k_ctx = rms_norm(k_ctx, k_norm_w)
        cos, sin = rope_cache(L, HEAD_DIM, ROPE_THETA, x.dtype)
        q = q * cos + rotate_half(q) * sin
        k = k * cos + rotate_half(k) * sin
        k_full = jnp.concatenate([k_ctx, k], axis=1)
        v_full = jnp.concatenate([v_ctx, v], axis=1)
        k_full = jnp.repeat(k_full, rep, axis=2)
        v_full = jnpp_repeat = jnp.repeat(v_full, rep, axis=2)
        i = jnp.arange(L)[:, None]
        j = jnp.arange(L)[None, :]
        causal = jnp.where(j > i, -jnp.inf, 0.0).astype(x.dtype)
        mask = jnp.concatenate([jnp.zeros((L, T), x.dtype), causal], axis=1)
        scale = 1.0 / np.sqrt(HEAD_DIM)
        scores = jnp.einsum('blhd,bmhd->bhlm', q, k_full) * scale + mask
        probs = jax.nn.softmax(scores, axis=-1)
        out = jnp.einsum('bhlm,bmhd->blhd', probs, v_full)
        out = out.reshape(B, L, NUM_HEADS * HEAD_DIM)
        return out @ wo

    def _L1_ffn_ref(x, gate_w, gate_b, expert_w, expert_b):
        import jax, jax.numpy as jnp
        import numpy as np
        N, S, D = (8, 256, 256)
        O = 256
        E = 8
        K = 2
        gate_logits = jnp.einsum('nsd,de->nse', x, gate_w) + gate_b
        _, top_idx = jax.lax.top_k(gate_logits, K)
        all_out = jax.nn.relu(jnp.einsum('nsd,edo->nseo', x, expert_w) + expert_b)
        sel = jnp.take_along_axis(all_out, top_idx[..., None], axis=2)
        return sel.mean(axis=2)

    def _L2_attn_ref(u, W_in, conv_w, conv_b, dt_bias, A_log, D_param, norm_w, W_out):
        import jax, jax.numpy as jnp
        import numpy as np
        D_MODEL = 256
        D_STATE = 128
        D_CONV = 4
        EXPAND = 2
        HEADDIM = 64
        CHUNK = 64
        D_INNER = EXPAND * D_MODEL
        NHEADS = D_INNER // HEADDIM
        CONV_DIM = D_INNER + 2 * D_STATE
        D_IN_PROJ = 2 * D_INNER + 2 * D_STATE + NHEADS
        BATCH, SEQLEN = (2, 256)

        def segsum(x):
            T = x.shape[-1]
            xx = jnp.broadcast_to(x[..., :, None], x.shape + (T,))
            mask_lower = jnp.tril(jnp.ones((T, T), dtype=bool), -1)
            s = jnp.cumsum(jnp.where(mask_lower, xx, 0.0), axis=-2)
            mask_diag = jnp.tril(jnp.ones((T, T), dtype=bool), 0)
            return jnp.where(mask_diag, s, -jnp.inf)

        def ssd(x, A, Bm, Cm, chunk):
            b, L, h, p = x.shape
            c = L // chunk
            x = x.reshape(b, c, chunk, h, p)
            A = A.reshape(b, c, chunk, h).transpose(0, 3, 1, 2)
            Bm = Bm.reshape(b, c, chunk, -1)
            Cm = Cm.reshape(b, c, chunk, -1)
            A_cum = jnp.cumsum(A, axis=-1)
            Lmat = jnp.exp(segsum(A))
            Y_diag = jnp.einsum('bcln,bcsn,bhcls,bcshp->bclhp', Cm, Bm, Lmat, x)
            decay_states = jnp.exp(A_cum[..., -1:] - A_cum)
            states = jnp.einsum('bcln,bhcl,bclhp->bchpn', Bm, decay_states, x)
            init = jnp.zeros_like(states[:, :1])
            states = jnp.concatenate([init, states], axis=1)
            A_last = jnp.pad(A_cum[..., -1], ((0, 0), (0, 0), (1, 0)))
            decay_chunk = jnp.exp(segsum(A_last))
            new_states = jnp.einsum('bhzc,bchpn->bzhpn', decay_chunk, states)
            states, final_state = (new_states[:, :-1], new_states[:, -1])
            out_decay = jnp.exp(A_cum)
            Y_off = jnp.einsum('bcln,bchpn,bhcl->bclhp', Cm, states, out_decay)
            return ((Y_diag + Y_off).reshape(b, L, h, p), final_state)
        b, L, _ = u.shape
        zxbcdt = u @ W_in
        z = zxbcdt[..., :D_INNER]
        xBC = zxbcdt[..., D_INNER:D_INNER + CONV_DIM]
        dt = zxbcdt[..., D_INNER + CONV_DIM:]
        dt = jax.nn.softplus(dt + dt_bias)
        xp = jnp.pad(xBC, ((0, 0), (D_CONV - 1, 0), (0, 0)))
        xBC = sum((xp[:, w:w + L, :] * conv_w[:, w] for w in range(D_CONV))) + conv_b
        xBC = jax.nn.silu(xBC)
        x = xBC[..., :D_INNER]
        Bm = xBC[..., D_INNER:D_INNER + D_STATE]
        Cm = xBC[..., D_INNER + D_STATE:]
        x = x.reshape(b, L, NHEADS, HEADDIM)
        A = -jnp.exp(A_log)
        y, final_state = ssd(x * dt[..., None], A * dt, Bm, Cm, CHUNK)
        y = y + x * D_param[:, None]
        y = y.reshape(b, L, D_INNER)
        yf = y * jax.nn.silu(z)
        rrms = jax.lax.rsqrt(jnp.mean(yf * yf, axis=-1, keepdims=True) + 1e-05)
        y = yf * rrms * norm_w
        return y @ W_out

    def _L2_xattn_ref(Q, K, V, attention_mask, w_q, w_k, w_v, w_o, b_o):
        import jax, jax.numpy as jnp
        import numpy as np
        D_MODEL = 256
        N_HEADS = 32
        N_GROUPS = 8
        HEAD_DIM = D_MODEL // N_HEADS
        BATCH, SEQ = (2, 128)
        NEG_INF = float('-inf')
        B, S, D = Q.shape
        G, HG, HD = (N_GROUPS, N_HEADS // N_GROUPS, HEAD_DIM)
        q = (Q @ w_q.T).reshape(B, S, G, HG, HD)
        k = (K @ w_k.T).reshape(B, S, G, HD)
        v = (V @ w_v.T).reshape(B, S, G, HD)
        scale = jnp.sqrt(jnp.float32(HD))
        scores = jnp.einsum('bnghd,bmgd->bnghm', q, k) / scale
        pad = (attention_mask == 0)[:, None, None, None, :]
        scores = jnp.where(pad, NEG_INF, scores)
        causal = jnp.tril(jnp.ones((S, S), bool))[None, :, None, None, :]
        scores = jnp.where(causal, scores, NEG_INF)
        attn = jax.nn.softmax(scores, axis=-1)
        out = jnp.einsum('bnghm,bmgd->bnghd', attn, v).reshape(B, S, D)
        return out @ w_o.T + b_o

    def _L2_ffn_ref(x, w_gate, w_up, w_down):
        import jax, jax.numpy as jnp
        import numpy as np
        EPS = 1e-05
        RMS_EPS = 1e-06

        def _rmsnorm(x):
            return x * jax.lax.rsqrt(jnp.mean(x * x, axis=-1, keepdims=True) + RMS_EPS)

        def _act_quant(x):
            scale = 127.0 / jnp.clip(jnp.max(jnp.abs(x), axis=-1, keepdims=True), EPS)
            q = jnp.round(jnp.clip(x * scale, -128.0, 127.0)) / scale
            return x + jax.lax.stop_gradient(q - x)

        def _weight_quant(w):
            scale = 1.0 / jnp.clip(jnp.mean(jnp.abs(w)), EPS)
            q = jnp.round(jnp.clip(w * scale, -1.0, 1.0)) / scale
            return w + jax.lax.stop_gradient(q - w)

        def _bitlinear(x, w):
            xq = _act_quant(_rmsnorm(x))
            wq = _weight_quant(w)
            return jnp.einsum('bsi,oi->bso', xq, wq)
        gate = jax.nn.silu(_bitlinear(x, w_gate))
        up = _bitlinear(x, w_up)
        return _bitlinear(gate * up, w_down)

    def _L3_attn_ref(input_, in_proj_w, conv1d_weight, conv1d_bias, z_bias, D, out_proj_w):
        import jax, jax.numpy as jnp
        import numpy as np
        D_MODEL = 256
        D_INNER = 512
        D_STATE = 64
        N_QK_HEADS = 8
        N_V_HEADS = 64
        CHUNK = 128
        KSIZE = 4
        CONV_DIM = D_INNER + 2 * N_QK_HEADS * D_STATE
        PROJ_DIM = CONV_DIM + D_INNER + N_V_HEADS

        def segsum(x):
            T = x.shape[-1]
            xe = jnp.broadcast_to(x[..., None], x.shape + (T,))
            strict_lower = jnp.tril(jnp.ones((T, T), dtype=bool), -1)
            xe = jnp.where(strict_lower, xe, 0.0)
            s = jnp.cumsum(xe, axis=-2)
            lower = jnp.tril(jnp.ones((T, T), dtype=bool), 0)
            return jnp.where(lower, s, -jnp.inf)

        def ssd_chunk_scan(X, dA, Bm, Cm, chunk):
            b, l, h, p = X.shape
            g = Bm.shape[2]
            rep = h // g
            Bm = jnp.repeat(Bm, rep, axis=2)
            Cm = jnp.repeat(Cm, rep, axis=2)
            c = l // chunk
            X = X.reshape(b, c, chunk, h, p)
            Bm = Bm.reshape(b, c, chunk, h, -1)
            Cm = Cm.reshape(b, c, chunk, h, -1)
            A = jnp.transpose(dA.reshape(b, c, chunk, h), (0, 3, 1, 2))
            A_cum = jnp.cumsum(A, axis=-1)
            Lm = jnp.exp(segsum(A))
            Y_diag = jnp.einsum('bcshn,bczhn,bhcsz,bczhp->bcshp', Cm, Bm, Lm, X)
            decay_states = jnp.exp(A_cum[..., -1:] - A_cum)
            states = jnp.einsum('bcshn,bhcs,bcshp->bchpn', Bm, decay_states, X)
            states = jnp.concatenate([jnp.zeros_like(states[:, :1]), states], axis=1)
            chunk_sums = jnp.pad(A_cum[..., -1], ((0, 0), (0, 0), (1, 0)))
            decay_chunk = jnp.exp(segsum(chunk_sums))
            new_states = jnp.einsum('bhzc,bchpn->bzhpn', decay_chunk, states)
            states = new_states[:, :-1]
            state_decay_out = jnp.exp(A_cum)
            Y_off = jnp.einsum('bcshn,bchpn,bhcs->bcshp', Cm, states, state_decay_out)
            return (Y_diag + Y_off).reshape(b, l, h, p)
        b, L, _ = input_.shape
        xBCzA = jnp.einsum('bld,ed->ble', input_, in_proj_w)
        xBC = xBCzA[..., :CONV_DIM]
        z = xBCzA[..., CONV_DIM:CONV_DIM + D_INNER]
        A_log = xBCzA[..., CONV_DIM + D_INNER:]
        xt = jnp.transpose(xBC, (0, 2, 1))
        y = jax.lax.conv_general_dilated(xt, conv1d_weight, (1,), [(KSIZE - 1, 0)], feature_group_count=CONV_DIM, dimension_numbers=('NCH', 'OIH', 'NCH'))
        xBC = jax.nn.silu(jnp.transpose(y + conv1d_bias[None, :, None], (0, 2, 1)))
        x = xBC[..., :D_INNER].reshape(b, L, N_V_HEADS, D_INNER // N_V_HEADS)
        Bm = xBC[..., D_INNER:D_INNER + N_QK_HEADS * D_STATE].reshape(b, L, N_QK_HEADS, D_STATE)
        Cm = xBC[..., D_INNER + N_QK_HEADS * D_STATE:].reshape(b, L, N_QK_HEADS, D_STATE)
        dt = jax.nn.softplus(A_log)
        x_in = x / dt[..., None]
        y_ssm = ssd_chunk_scan(x_in * dt[..., None], -dt, Bm, Cm, CHUNK)
        Du = D[None, None, :, None] * x_in
        yf = (y_ssm + Du).reshape(b, L, D_INNER)
        out = jnp.einsum('bld,ed->ble', yf * jax.nn.silu(z + z_bias), out_proj_w)
        return out

    def _L3_xattn_ref(hidden_states, memory_tokens, memory_mask):
        import jax, jax.numpy as jnp
        import numpy as np
        B, S, D = hidden_states.shape
        scale = 1.0 / jnp.sqrt(jnp.asarray(D, hidden_states.dtype))
        scores = jnp.einsum('bsd,bmd->bsm', hidden_states, memory_tokens) * scale
        neg_inf = jnp.asarray(-1e+30, scores.dtype)
        scores = jnp.where(memory_mask[:, None, :], scores, neg_inf)
        attn = jax.nn.softmax(scores, axis=-1)
        readout = jnp.einsum('bsm,bmd->bsd', attn, memory_tokens)
        valid_b = jnp.any(memory_mask, axis=-1)
        out = jnp.where(valid_b[:, None, None], readout, jnp.zeros_like(readout))
        return out

    def _L3_ffn_ref(x, Wr, br, W1, W2):
        import jax, jax.numpy as jnp
        import numpy as np
        N_BLOCKS = 16
        BLOCK_SIZE = 64
        TOP_K = N_BLOCKS // 4
        x_shape = x.shape
        in_f = x_shape[-1]
        xf = x.reshape(-1, in_f)
        n = xf.shape[0]
        prob = jax.nn.softmax(xf @ Wr.T + br, axis=-1)
        _, idx = jax.lax.top_k(prob, TOP_K)
        mask = jnp.zeros((n, N_BLOCKS), dtype=xf.dtype)
        mask = mask.at[jnp.arange(n)[:, None], idx].set(1.0)
        W1b = W1.reshape(N_BLOCKS, BLOCK_SIZE, in_f)
        h = jnp.einsum('nf,ibf->nib', xf, W1b)
        h = jax.nn.gelu(h, approximate=False) * mask[:, :, None]
        W2b = W2.reshape(in_f, N_BLOCKS, BLOCK_SIZE)
        y = jnp.einsum('nib,fib->nf', h, W2b)
        return y.reshape(x_shape)
    x = x + _L0_attn_ref(_layernorm(x, axis=-1), L0_attn_Wu, L0_attn_bu, L0_attn_Wv, L0_attn_bv, L0_attn_Wg1, L0_attn_bg1, L0_attn_Wg2, L0_attn_bg2, L0_attn_conv_w, L0_attn_conv_b)
    x = x + _L0_xattn_ref(8, 128, 256, L0_xattn_w, L0_xattn_u, _layernorm(x, axis=-1), ctx_2048)
    x = x + _L0_ffn_ref(_layernorm(x, axis=-1), L0_ffn_router_w, L0_ffn_gate_w, L0_ffn_up_w, L0_ffn_down_w)
    x = x + _L1_attn_ref(_layernorm(x, axis=-1), L1_attn_Wq, L1_attn_Wk, L1_attn_Wv, L1_attn_Wo)
    x = x + _L1_xattn_ref(_layernorm(x, axis=-1), ctx_2048, L1_xattn_wq, L1_xattn_wk, L1_xattn_wv, L1_xattn_wo, L1_xattn_wk_ctx, L1_xattn_wv_ctx, L1_xattn_q_norm_w, L1_xattn_k_norm_w)
    x = x + _L1_ffn_ref(_layernorm(x, axis=-1), L1_ffn_gate_w, L1_ffn_gate_b, L1_ffn_expert_w, L1_ffn_expert_b)
    x = x + _L2_attn_ref(_layernorm(x, axis=-1), L2_attn_W_in, L2_attn_conv_w, L2_attn_conv_b, L2_attn_dt_bias, L2_attn_A_log, L2_attn_D_param, L2_attn_norm_w, L2_attn_W_out)
    x = x + _L2_xattn_ref(_layernorm(x, axis=-1), ctx_2048, ctx_2048, mask_BxS2_if1, L2_xattn_w_q, L2_xattn_w_k, L2_xattn_w_v, L2_xattn_w_o, L2_xattn_b_o)
    x = x + _L2_ffn_ref(_layernorm(x, axis=-1), L2_ffn_w_gate, L2_ffn_w_up, L2_ffn_w_down)
    x = x + _L3_attn_ref(_layernorm(x, axis=-1), L3_attn_in_proj_w, L3_attn_conv1d_weight, L3_attn_conv1d_bias, L3_attn_z_bias, L3_attn_D, L3_attn_out_proj_w)
    x = x + _L3_xattn_ref(_layernorm(x, axis=-1), ctx_2048, mask_BxS2_bk0)
    x = x + _L3_ffn_ref(_layernorm(x, axis=-1), L3_ffn_Wr, L3_ffn_br, L3_ffn_W1, L3_ffn_W2)
    return x

_drawn_inputs = setup_inputs


def setup_inputs(seed=0):
    import zlib

    import numpy as np

    out = dict(_drawn_inputs(seed))
    spreads = {'L0_attn_bu': (0.0, 0.1),
     'L0_attn_bv': (0.0, 0.1),
     'L0_attn_bg1': (0.0, 0.55),
     'L0_attn_bg2': (0.0, 0.1),
     'L0_attn_conv_b': (0.0, 0.1),
     'L1_xattn_q_norm_w': (1.0, 0.2),
     'L1_xattn_k_norm_w': (1.0, 0.2),
     'L2_attn_conv_b': (0.0, 0.1),
     'L2_attn_D_param': (1.0, 0.6),
     'L2_attn_norm_w': (1.0, 0.2),
     'L2_xattn_b_o': (0.0, 0.1),
     'L3_attn_z_bias': (0.0, 0.1),
     'L3_attn_D': (1.0, 0.2),
     'L3_ffn_br': (0.0, 0.1)}
    factors = {'L0_attn_Wg1': 3.331,
     'L0_attn_Wg2': 3.967,
     'L0_ffn_gate_w': 2.981,
     'L0_ffn_up_w': 2.758,
     'L1_attn_Wq': 4.339,
     'L1_attn_Wk': 3.811,
     'L2_xattn_w_q': 6.192,
     'L2_xattn_w_k': 5.631}
    for name, (base, spread) in spreads.items():
        noise = np.random.default_rng([zlib.crc32(name.encode()), seed]).standard_normal(out[name].shape)
        drawn = base * np.exp(spread * noise) if base else spread * noise
        out[name] = jnp.asarray(drawn.astype(out[name].dtype))
    for name, factor in factors.items():
        out[name] = (out[name] * factor).astype(out[name].dtype)
    return out
```

```python
from contextlib import ExitStack

import numpy as np
import concourse.bass as bass
from concourse import mybir

P = 128
NB = 8
D = 256
N = NB * P
G = 512
BANKS = 8
NEG = -1e30
LOW, IMM = -3.0e38, -3.3e38

ALU = mybir.AluOpType
ACT = mybir.ActivationFunctionType
AX = mybir.AxisListType
F32 = mybir.dt.float32
BF16 = mybir.dt.bfloat16

CST = dict(ident=128, tri=128, strict=128, ones=128, causal=128, cos1=128, sin1=128,
           cosx=128, sinx=128, nf=512, first=128, blk=4)
VEC = dict(bu=2, bv=2, bg1=1, bg2=2, cw0=6, cb0=2, w=2, u=2, rw0=64, qn=1, kn=1, qns=1, kns=1,
           cw2=24, cb2=6, nw2=4, cw3=48, cb3=12, gate_b=8, dt_bias=8, A_log=8, D2=8, D3=64,
           br=16, z_bias=4, b_o=256, eps5=1, eps6=1, one=1, zero=1)
W_L0A = dict(WuT=512, WvT=512, g1T=128, g2T=256)
W_EXP = dict(gate=192, up=192, down=256)
W_L1A = dict(q=512, qs=512, k=512, ks=512, v=128, o=512)
W_L1X = dict(q=4096, k=1024, v=1024, kc=1024, vc=1024, o=4096)
W_L1F = dict(gate=16, e=4096)
W_L2A = dict(inp=2 * 1288, out=1024)
W_L2X = dict(q=512, k=512, v=128, o=512)
W_L2F = dict(gate=2048, up=2048, down=2048)
W_L3A = dict(inp=2 * 2112, out=1024)
W_L3F = dict(r=32, w1=2048, w2=2048)
NE = 32
EI = 96
EXP_COLS = sum(W_EXP.values())
KV, XH = 4, 16
EXP_CHUNK = 4
EXP_SLOTS = 4
ARENA_A = 5632
ARENA_B = 12288
V_WINDOWS = sum(W_L1A.values())


def offsets(sizes):
    at, out = 0, {}
    for name, n in sizes.items():
        out[name] = (at, at + n)
        at += n
    return out, at


def plans():
    ln = [("ln", g, c) for g in range(2) for c in range(2)]
    out = [("o", bp) for bp in range(4)]
    p = {}
    p["pre"] = [("ctx", g, c) for g in range(2) for c in range(2)]
    p["l0a"] = ln + [("h", g) for g in range(2)] + \
        [(k, rc, g) for rc in range(2) for g in range(2) for k in ("gate", "u", "v")] + out
    p["l0x"] = ln + out
    l = list(ln) + [("r",)]
    for e in range(NE + 1):
        if e < NE:
            l += [(k, e, g) for g in range(2) for k in ("gate", "up")]
        if e >= 1:
            l += [("down", e - 1, bp) for bp in range(4)]
    p["l0f"] = l
    p["l1a"] = ln + [(k, c, g) for c in range(2) for g in range(2) for k in ("q", "qs", "k", "ks")] + \
        [("v",)] + heads_plan()
    l = list(ln)
    for g in range(2):
        for kv in range(KV + 1):
            if kv < KV:
                l += [(k, g, kv) for k in ("k", "kc")]
            if kv >= 1:
                l += [(k, g, kv - 1) for k in ("k2", "kc2")]
        l += [(k, g, i) for i in range(4) for k in ("v", "vc")]
        for h2 in range(9):
            if h2 < 8:
                l += [("q", g, 2 * h2), ("q", g, 2 * h2 + 1)]
            if h2 >= 1:
                l += [("rq", g, h2 - 1)]
        for u in range(18):
            if u < 16:
                l += [("s", g, u, 0), ("s", g, u, 1)]
            if 1 <= u <= 16:
                l += [("t", g, u - 1, 0), ("t", g, u - 1, 1)]
            if u >= 2:
                l += [("pv", g, u - 2)]
                if (u - 2) % 4 == 3:
                    l += [("o", 4 * g + (u - 2) // 4)]
    p["l1x"] = l
    p["l1f"] = ln + [("r",)] + [("e", e, bp) for e in range(8) for bp in range(4)]
    l = ln + [("dt",)] + [("c", cc, g) for g in range(2) for cc in range(6)] + [("z", b) for b in range(NB)] + \
        [("x", b) for b in range(NB)]
    for b in range(NB + 1):
        if b < NB:
            l += [("seg", b, 0), ("seg", b, 1), ("cb", b)]
        if b >= 1:
            l += [("y", b - 1)]
    for b in range(NB + 1):
        if b < NB:
            l += [("yt", b)]
        if b >= 1:
            l += [("o", b - 1)]
    p["l2a"] = l
    p["l2x"] = ln + [(k, c, g) for c in range(2) for g in range(2) for k in ("q", "k")] + [("v",)] + heads_plan()
    l = [("ws",)] + [("qt", g, c) for g in range(2) for c in range(2)] + \
        [(k, b, h) for b in range(NB) for h in range(2) for k in ("gate", "up")]
    for b in range(NB + 1):
        if b < NB:
            l += [("ht", b)]
        if b >= 1:
            l += [("o", b - 1)]
    p["l2f"] = l
    l = ln + [("dt",)]
    for g in range(2):
        l += [("c", cc, g) for cc in range(12)] + [("z", 4 * g + i) for i in range(4)] + [("x", 4 * g + i) for i in range(4)]
        for t in range(18):
            if t < 16:
                if t % 4 == 0:
                    l += [("cb", g, t // 4, 0), ("cb", g, t // 4, 1)]
                l += [("seg", g, u, hh) for u in (2 * t, 2 * t + 1) for hh in range(2)]
            if 1 <= t < 17:
                l += [("y", g, t - 1)]
            if t >= 5 and (t - 5) % 4 == 0:
                l += [("o", 4 * g + (t - 5) // 4)]
    p["l3a"] = l
    p["l3x"] = ln + [("val",), ("s", 0), ("s", 1), ("t", 0), ("t", 1)] + out
    p["l3f"] = ln + [("r",), ("mt",)] + [(k, m, g) for m in range(8) for g in range(2) for k in ("h", "m")] + \
        [("o", bp) for bp in range(4)]
    return p


def heads_plan():
    l = []
    for u in range(NB * 8 + 4):
        if u < NB * 8:
            l += [("s", u)]
        if 2 <= u < NB * 8 + 2:
            l += [("t", u - 2)]
        if u >= 7 and (u - 7) % 4 == 0:
            l += [("pv", (u - 7) // 4)]
        if u >= 20 and (u - 20) % 16 == 0:
            l += [("o", (u - 20) // 16)]
    return l + [("o", 3)]


def build(nc, a, out):
    plan = plans()
    job_of, at = {}, 0
    for layer, keys in plan.items():
        for key in keys:
            job_of[(layer,) + key] = at
            at += 1

    with ExitStack() as ctx:
        def sb(name, cols, dt=F32):
            return ctx.enter_context(nc.sbuf_tensor(name, [P, cols], dt))

        def sem(name):
            return ctx.enter_context(nc.semaphore(name))

        cst_at, ncst = offsets(CST)
        vec_at, nvec = offsets(VEC)
        cst_t, vec_t = sb("cst", ncst), sb("vec", nvec)
        X = sb("X", NB * D)
        XN = sb("XN", NB * D)
        XT = sb("XT", 2 * N)
        C = sb("C", NB * D)
        CT = sb("CT", 2 * N)
        WA, WB = sb("WA", ARENA_A), sb("WB", ARENA_B)
        identb, causalb, onesb = sb("identb", P, BF16), sb("causalb", 4 * P, BF16), sb("onesb", P, BF16)
        small = sb("small", 832)
        WORK = 18432
        work = sb("work", WORK)
        PS = ctx.enter_context(nc.psum_tensor("PS", [P, BANKS * G], F32))

        def cst(name, p0=0, p1=P):
            return cst_t[p0:p1, slice(*cst_at[name])]

        def vec(name, i=None, n=1, p0=0, p1=P):
            lo, hi = vec_at[name]
            return vec_t[p0:p1, lo:hi] if i is None else vec_t[p0:p1, lo + i:lo + i + n]

        mk1 = ctx.enter_context(nc.sbuf_tensor("mk1", [1, N], mybir.dt.int32))
        mk0 = ctx.enter_context(nc.sbuf_tensor("mk0", [1, N // 4], mybir.dt.int32))
        pad1 = ctx.enter_context(nc.sbuf_tensor("pad1", [P, N], BF16))
        pad0 = ctx.enter_context(nc.sbuf_tensor("pad0", [P, N], BF16))
        valid = ctx.enter_context(nc.sbuf_tensor("valid", [1, NB], F32))

        bank_full = [sem(f"bank_full{i}") for i in range(BANKS)]
        bank_free = [sem(f"bank_free{i}") for i in range(BANKS)]
        cst_in, x_in, ctx_in = sem("cst_in"), sem("x_in"), sem("ctx_in")
        windows_zero = sem("windows_zero")
        expert_b, eb_in = WB[:, 8192:8192 + 8 * D], sem("eb_in")
        wa_in, wb_in = sem("wa_in"), sem("wb_in")
        exp_in = [sem(f"exp_in{i}") for i in range(EXP_SLOTS)]
        y_out = sem("y_out")
        x_final = sem("x_final")

        class Handoff:
            def __init__(self, name):
                self.sem, self.given, self.taken = sem(name), 0, 0

            def give(self):
                self.given += 1
                return 1

            def next(self):
                self.taken += 1
                return self.taken

        act_to_pe, dve_to_pe = Handoff("act_to_pe"), Handoff("dve_to_pe")
        act_to_dve, dve_to_act = Handoff("act_to_dve"), Handoff("dve_to_act")
        decay_steps, decayed_scores, gated_y = Handoff("decay_steps"), Handoff("decayed_scores"), Handoff("gated_y")

        def stepper(name):
            own, latest = Handoff(name), []

            def step(to=own):
                if isinstance(to, int):
                    latest[:] = [bank_free[to % BANKS], to // BANKS + 1]
                else:
                    to.give()
                    latest[:] = [to.sem, to.given]
                return latest[0], 1

            return step, lambda: tuple(latest)

        dve_step, dve_last = stepper("dve_own")
        act_step, act_last = stepper("act_own")

        def bank(j, rows=P, cols=G):
            return PS[0:rows, (j % BANKS) * G:(j % BANKS) * G + cols]

        def full(j):
            return bank_full[j % BANKS], j // BANKS + 1

        def freed(j):
            return bank_free[j % BANKS], j // BANKS + 1

        block = ctx.enter_context(nc.Block())

        def r3(ap, b):
            return ap.rearrange("p (a b) -> p a b", b=b)

        def xt(c, lo, hi, T=None):
            return (T or XT)[:, c * N + lo:c * N + hi]

        sm = lambda lo, n: small[:, lo:lo + n]

        def W(arena, sizes, name, lo=0, hi=None, p1=P, base=0):
            a0, a1 = offsets(sizes)[0][name]
            hi = a1 - a0 if hi is None else hi
            return arena[0:p1, base + a0 + lo:base + a0 + hi]

        def wk(lo, n, p0=0, p1=P):
            return work[p0:p1, lo:lo + n]

        def wkb(lo, n, p0=0, p1=P):
            return work[p0:p1, lo:lo + n // 2].bitcast(BF16)

        def ew(e, name, lo, hi, p1=P):
            return W(WB, W_EXP, name, lo, hi, p1, base=(e % (EXP_CHUNK * EXP_SLOTS)) * EXP_COLS)

        v_windows, ones_window = WA[:, V_WINDOWS:V_WINDOWS + 2072], WA[:, V_WINDOWS + 2072:V_WINDOWS + 2128]

        def l3a_x(i):
            return wk(6144, 2048) if i == 3 else WB[:, 4128 + i * 2048:4128 + (i + 1) * 2048]

        def l1x_p(u):
            return wk(16384, 1024) if u % 2 == 0 else XN[:, 0:1024]

        def l1x_pt(u):
            return wk(17408, 1024) if u % 2 == 0 else XN[:, 1024:2048]

        @block.sync
        def _(sp):
            J = lambda *k: job_of[k]
            last = lambda layer: job_of[(layer,) + plan[layer][-1]]
            sp.dma_start(r3(X[:, :], D), a["x"].rearrange("b t d -> t b d")).then_inc(x_in, 16)
            sp.dma_start(cst_t[:, :], a["cst"]).then_inc(cst_in, 16)
            sp.dma_start(vec_t[:, :], a["vec"]).then_inc(cst_in, 16)
            sp.dma_start(r3(C[:, :], D), a["ctx"].rearrange("b t d -> t b d")).then_inc(ctx_in, 16)

            def load(arena, name, s):
                sp.dma_start(arena[:, 0:a[name].shape[1]], a[name]).then_inc(s, 16)

            def experts(c):
                s = c % EXP_SLOTS
                n = EXP_CHUNK * EXP_COLS
                sp.dma_start(WB[:, s * n:(s + 1) * n], a["l0f"][:, c * n:(c + 1) * n]).then_inc(exp_in[s], 16)

            sp.dma_start(mk1[:, :], a["m1"]).then_inc(cst_in, 16)
            sp.dma_start(mk0[:, :], a["m0"]).then_inc(cst_in, 16)
            load(WA, "l0a", wa_in)
            for c in range(EXP_SLOTS):
                experts(c)
            for c in range(EXP_SLOTS, NE // EXP_CHUNK):
                sp.wait_ge(*full(J("l0f", "down", (c - EXP_SLOTS + 1) * EXP_CHUNK - 1, 3)))
                experts(c)
                if c == EXP_SLOTS:
                    load(WA, "l1a", wa_in)
            sp.wait_ge(*full(last("l0f")))
            load(WB, "l1x", wb_in)
            sp.wait_ge(*full(last("l1a")))
            load(WA, "l1f", wa_in)
            sp.wait_ge(*full(last("l1x")))
            sp.dma_start(expert_b, a["eb"]).then_inc(eb_in, 16)
            load(WB, "l2a", wb_in)
            sp.dma_start(r3(C[:, :], D), a["ctx"].rearrange("b t d -> t b d")).then_inc(ctx_in, 16)
            for layer, free_by, arena, s in (("l2x", "l1f", WA, wa_in), ("l2f", "l2a", WB, wb_in),
                                             ("l3a", "l2x", WA, wa_in), ("l3f", "l2f", WB, wb_in)):
                sp.wait_ge(*full(last(free_by)))
                load(arena, layer, s)
            sp.wait_ge(x_final, 1)
            sp.dma_start(out.rearrange("b t d -> t b d"), r3(X[:, :], D)).then_inc(y_out, 16)
            sp.wait_ge(y_out, 16)

        @block.gpsimd
        def _(pool):
            both = WA[:, V_WINDOWS:V_WINDOWS + 2072 + 56]
            nc.gpsimd.memset(both, 0.0).then_inc(windows_zero, 1)
            pool.wait_ge(*full(job_of[("l1f",) + plan["l1f"][-1]]))
            nc.gpsimd.memset(both, 0.0).then_inc(windows_zero, 1)
            pool.wait_ge(*freed(job_of[("l2f",) + plan["l2f"][-1]]))
            for i in range(4):
                nc.gpsimd.memset(l3a_x(i), 0.0).then_inc(windows_zero, 1)

        @block.tensor
        def _(pe):
            opened = [0]

            def begin(*key):
                j = opened[0]
                assert job_of[key] == j, (key, job_of[key], j)
                if j >= BANKS:
                    pe.wait_ge(bank_free[j % BANKS], j // BANKS)
                return bank(j)

            def end(ins):
                ins.then_inc(bank_full[opened[0] % BANKS], 1)
                opened[0] += 1

            mm = lambda o, l, r, s, e: nc.tensor.matmul(o, l, r, start=s, stop=e)
            J = lambda *k: job_of[k]

            def transposes(layer, tag, source, ready):
                for g in range(2):
                    for c in range(2):
                        o = begin(layer, tag, g, c)
                        for i in range(4):
                            b = 4 * g + i
                            if ready and c == 0:
                                pe.wait_ge(dve_to_pe.sem, dve_to_pe.next())
                            ins = nc.tensor.transpose(o[:, i * P:(i + 1) * P],
                                                      source[:, b * D + c * P:b * D + (c + 1) * P], cst("ident"))
                        end(ins)

            def ln(layer):
                transposes(layer, "ln", XN, True)

            def need_xt(layer, g):
                pe.wait_ge(*freed(J(layer, "ln", g, 0)))
                pe.wait_ge(*freed(J(layer, "ln", g, 1)))

            def from_xt(o, cols, g, w, T=None):
                for c in range(2):
                    ins = mm(o, w(c), xt(c, g * G, (g + 1) * G, T), c == 0, c == 1)
                return ins

            pe.wait_ge(cst_in, 64)
            pe.wait_ge(ctx_in, 16)
            transposes("pre", "ctx", C, False)

            def heads(layer, wo, pad):
                kbd = r3(wk(0, 8 * N), N)
                for key in heads_plan():
                    o = begin(layer, *key)
                    if key[0] == "s":
                        b, kv = key[1] // 8, key[1] % 8
                        c, r = kv // 4, 32 * (kv % 4)
                        if pad is not None:
                            mm(r3(o, P), onesb[:, :], pad[:, b * P:(b + 1) * P].unsqueeze(1).to_broadcast([P, 4, P]), True, False)
                        mm(o, identb[:, :], causalb[:, :], pad is None, False)
                        end(mm(r3(o, P), XN[r:r + 32, c * N + b * P:c * N + (b + 1) * P],
                               kbd[r:r + 32, 4 * c:4 * c + 4, b * P:(b + 1) * P], False, True))
                    elif key[0] == "t":
                        pe.wait_ge(act_to_pe.sem, act_to_pe.next())
                        for i in range(4):
                            ins = nc.tensor.transpose(o[:, i * P:(i + 1) * P],
                                                      wk(16384 + (key[1] % 3) * G + i * P, P), cst("ident"))
                        end(ins)
                    elif key[0] == "pv":
                        x = key[1]
                        pe.wait_ge(*freed(J(layer, "t", 4 * x + 3)))
                        for part in range(2):
                            for k in range(4):
                                u = 4 * x + k
                                for h in range(4):
                                    window = v_windows[:, u * 32 + 24 - 8 * h:u * 32 + 56 - 8 * h] if part == 0 else ones_window[:, 24 - 8 * h:56 - 8 * h]
                                    ins = mm(o[32 * k:32 * k + 32, part * P:(part + 1) * P], window,
                                             wk(8192 + (u % 16) * G + h * P, P), h == 0, h == 3)
                        end(ins)
                    else:
                        bp = key[1]
                        for x in range(4):
                            pe.wait_ge(*freed(J(layer, "pv", 4 * bp + x)))
                        for i in range(2):
                            for c in range(2):
                                lo = (bp % 2) * G + (2 * i + c) * P
                                ins = mm(o[:, i * D:(i + 1) * D], XT[:, lo:lo + P],
                                         wo[:, c * D:(c + 1) * D], c == 0, c == 1)
                        end(ins)

            def values(layer, wv, T):
                o = begin(layer, "v")
                for b in range(NB):
                    for c in range(2):
                        ins = mm(o[:, b * 64:(b + 1) * 64], xt(c, b * P, (b + 1) * P, T), wv[:, c * 64:(c + 1) * 64], c == 0, c == 1)
                end(ins)

            ln("l0a")
            pe.wait_ge(wa_in, 16)
            w = lambda n, *k, **kw: W(WA, W_L0A, n, *k, **kw)
            for g in range(2):
                o = begin("l0a", "h", g)
                need_xt("l0a", g)
                end(from_xt(o[0:64, :], 64, g, lambda c: w("g1T", c * 64, c * 64 + 64)))
            for rc in range(2):
                for g in range(2):
                    o = begin("l0a", "gate", rc, g)
                    pe.wait_ge(*freed(J("l0a", "h", g)))
                    end(mm(o, w("g2T", rc * P, rc * P + P, p1=64), wk(0 + g * G, G, 0, 64), True, True))
                    for n in ("u", "v"):
                        o = begin("l0a", n, rc, g)
                        end(from_xt(o, P, g, lambda c: w("WuT" if n == "u" else "WvT", c * D + rc * P, c * D + rc * P + P)))
            for bp in range(4):
                o = begin("l0a", "o", bp)
                if bp == 0:
                    pe.wait_ge(dve_to_pe.sem, dve_to_pe.next())
                for i in range(2):
                    b = 2 * bp + i
                    oo = o[:, i * D:(i + 1) * D]
                    for rc in range(2):
                        mm(oo, wk(5120 + rc * N + b * P, P), w("WuT", rc * D, rc * D + D), rc == 0, False)
                    for c in range(2):
                        ins = mm(oo[:, c * P:(c + 1) * P], wk(7168 + c * N + b * P, P), cst("ident"), False, c == 1)
                end(ins)

            ln("l0x")
            for bp in range(4):
                o = begin("l0x", "o", bp)
                if bp == 0:
                    pe.wait_ge(dve_to_pe.sem, dve_to_pe.next())
                for i in range(2):
                    for c in range(2):
                        b = 2 * bp + i
                        ins = nc.tensor.transpose(o[:, i * D + c * P:i * D + (c + 1) * P],
                                                  wk(c * N + b * P, P), cst("ident"))
                end(ins)

            ln("l0f")
            o = begin("l0f", "r")
            pe.wait_ge(cst_in, 64)
            need_xt("l0f", 0)
            need_xt("l0f", 1)
            for b in range(NB):
                for c in range(2):
                    ins = mm(o[:, b * NE:(b + 1) * NE], xt(c, b * P, (b + 1) * P), vec("rw0", c * NE, NE), c == 0, c == 1)
            end(ins)
            for e in range(NE + 1):
                if e < NE:
                    ch = e // EXP_CHUNK
                    if e % EXP_CHUNK == 0:
                        pe.wait_ge(exp_in[ch % EXP_SLOTS], 16 * (ch // EXP_SLOTS + 1))
                    for g in range(2):
                        for n in ("gate", "up"):
                            o = begin("l0f", n, e, g)
                            end(from_xt(o[0:EI, :], EI, g, lambda c: ew(e, n, c * EI, (c + 1) * EI)))
                if e >= 1:
                    f = e - 1
                    for bp in range(4):
                        o = begin("l0f", "down", f, bp)
                        pe.wait_ge(*freed(J("l0f", "up", f, bp // 2)))
                        for i in range(2):
                            b = 2 * bp + i
                            ins = mm(o[:, i * D:(i + 1) * D], wk((f % 2) * N + b * P, P, 0, EI),
                                     ew(f, "down", 0, D, EI), True, True)
                        end(ins)

            ln("l1a")
            pe.wait_ge(wa_in, 32)
            w1 = lambda n, *k, **kw: W(WA, W_L1A, n, *k, **kw)
            for c in range(2):
                for g in range(2):
                    for n in ("q", "qs", "k", "ks"):
                        o = begin("l1a", n, c, g)
                        need_xt("l1a", g)
                        end(from_xt(o, P, g, lambda cc: w1(n, cc * D + c * P, cc * D + c * P + P)))
            values("l1a", w1("v"), XT)
            pe.wait_ge(act_to_pe.sem, act_to_pe.next())
            pe.wait_ge(act_to_pe.sem, act_to_pe.next())
            heads("l1a", w1("o"), None)

            ln("l1x")
            pe.wait_ge(wb_in, 16)
            wx = lambda n, *k, **kw: W(WB, W_L1X, n, *k, **kw)
            for g in range(2):
                need_xt("l1x", g)
                for kv in range(KV + 1):
                    if kv < KV:
                        for n, T in (("k", XT), ("kc", CT)):
                            o = begin("l1x", n, g, kv)
                            end(from_xt(o, P, g, lambda c: wx(n, c * G + kv * P, c * G + kv * P + P), T))
                    if kv >= 1:
                        for i, n in enumerate(("k", "kc")):
                            o = begin("l1x", n + "2", g, kv - 1)
                            pe.wait_ge(*freed(J("l1x", n, g, kv - 1)))
                            end(mm(o, cst("ones"), XN[:, (((kv - 1) % 2) * 2 + i) * G:(((kv - 1) % 2) * 2 + i + 1) * G], True, True))
                for i in range(4):
                    b = 4 * g + i
                    for n, T in (("v", XT), ("vc", CT)):
                        o = begin("l1x", n, g, i)
                        for c in range(2):
                            ins = mm(o, xt(c, b * P, (b + 1) * P, T), wx(n, c * G, c * G + G), c == 0, c == 1)
                        end(ins)
                for h2 in range(9):
                    if h2 < 8:
                        for h in (2 * h2, 2 * h2 + 1):
                            o = begin("l1x", "q", g, h)
                            end(from_xt(o, P, g, lambda c: wx("q", c * 2048 + h * P, c * 2048 + h * P + P)))
                    if h2 >= 1:
                        o = begin("l1x", "rq", g, h2 - 1)
                        for i in range(2):
                            pe.wait_ge(*freed(J("l1x", "q", g, 2 * h2 - 2 + i)))
                            for b in range(4):
                                ins = mm(o[:, b * 2 + i:b * 2 + i + 1],
                                         XN[:, ((2 * h2 - 2 + i) % 4) * G + b * P:((2 * h2 - 2 + i) % 4) * G + (b + 1) * P],
                                         cst("ones")[:, 0:1], True, True)
                        end(ins)
                pe.wait_ge(dve_to_pe.sem, dve_to_pe.next())
                for u in range(18):
                    if u < 16:
                        b, kv = u // 4, u % 4
                        for s_ in range(2):
                            o = begin("l1x", "s", g, u, s_)
                            for i in range(2):
                                h = 4 * kv + 2 * s_ + i
                                mm(o[:, i * D:(i + 1) * D], wk(h * G + b * P, P), wk(8192 + (kv * 4 + b) * D, D), True, False)
                                ins = mm(o[:, i * D + P:(i + 1) * D], identb[:, :], causalb[:, 0:P], False, True)
                            end(ins)
                    if 1 <= u <= 16:
                        x = u - 1
                        pe.wait_ge(dve_to_pe.sem, dve_to_pe.next())
                        for kc in range(2):
                            o = begin("l1x", "t", g, x, kc)
                            for j in range(4):
                                ins = nc.tensor.transpose(o[:, j * P:(j + 1) * P],
                                                          l1x_p(x)[:, j * D + kc * P:j * D + (kc + 1) * P], cst("ident"))
                            end(ins)
                    if u >= 2:
                        x = u - 2
                        b, kv = x // 4, x % 4
                        o = begin("l1x", "pv", g, x)
                        for kc in range(2):
                            pe.wait_ge(*freed(J("l1x", "t", g, x, kc)))
                            ins = mm(o, wk(12288 + (b * 2 + kc) * G + kv * P, P), l1x_pt(x)[:, kc * G:(kc + 1) * G], kc == 0, kc == 1)
                        end(ins)
                        if kv == 3:
                            o = begin("l1x", "o", 4 * g + b)
                            for m in range(4):
                                pe.wait_ge(*freed(J("l1x", "pv", g, 4 * b + m)))
                            for h in range(XH):
                                ins = mm(o[:, 0:D], C[:, h * P:(h + 1) * P], wx("o", h * D, h * D + D), h == 0, h == XH - 1)
                            end(ins)

            ln("l1f")
            pe.wait_ge(wa_in, 48)
            wf_ = lambda n, *k, **kw: W(WA, W_L1F, n, *k, **kw)
            o = begin("l1f", "r")
            need_xt("l1f", 0)
            need_xt("l1f", 1)
            for b in range(NB):
                for c in range(2):
                    ins = mm(o[:, b * 8:(b + 1) * 8], xt(c, b * P, (b + 1) * P), wf_("gate", c * 8, c * 8 + 8), c == 0, c == 1)
            end(ins)
            for e in range(8):
                for bp in range(4):
                    o = begin("l1f", "e", e, bp)
                    for i in range(2):
                        b = 2 * bp + i
                        for c in range(2):
                            ins = mm(o[:, i * D:(i + 1) * D], xt(c, b * P, (b + 1) * P),
                                     wf_("e", (2 * e + c) * D, (2 * e + c) * D + D), c == 0, c == 1)
                    end(ins)

            def project(layer, n, wt_, stride, lo, rows, b):
                o = begin(layer, n, b)
                for c in range(2):
                    ins = mm(o, xt(c, b * P, (b + 1) * P), wt_[:, c * stride + lo:c * stride + lo + rows], c == 0, c == 1)
                end(ins)

            ln("l2a")
            pe.wait_ge(wb_in, 32)
            wi, wo = W(WB, W_L2A, "inp"), W(WB, W_L2A, "out")
            o = begin("l2a", "dt")
            need_xt("l2a", 0)
            need_xt("l2a", 1)
            for b in range(NB):
                for c in range(2):
                    ins = mm(o[:, b * 8:(b + 1) * 8], xt(c, b * P, (b + 1) * P), wi[:, c * 1288 + 1280:c * 1288 + 1288], c == 0, c == 1)
            end(ins)
            for g in range(2):
                for cc in range(6):
                    o = begin("l2a", "c", cc, g)
                    end(from_xt(o, P, g, lambda c: wi[:, c * 1288 + 512 + cc * P:c * 1288 + 512 + (cc + 1) * P]))
            for b in range(NB):
                project("l2a", "z", wi, 1288, 0, 512, b)
            for b in range(NB):
                o = begin("l2a", "x", b)
                if b % 4 == 0:
                    pe.wait_ge(act_to_pe.sem, act_to_pe.next())
                for cc in range(4):
                    ins = nc.tensor.transpose(o[:, cc * P:(cc + 1) * P], wk(cc * N + b * P, P), cst("ident"))
                end(ins)
            for b in range(NB + 1):
                if b < NB:
                    pe.wait_ge(decay_steps.sem, decay_steps.next())
                    for hh in range(2):
                        o = begin("l2a", "seg", b, hh)
                        end(mm(o, cst("strict"), XN[:, (b % 2) * 1024 + hh * G:(b % 2) * 1024 + (hh + 1) * G], True, True))
                    o = begin("l2a", "cb", b)
                    end(mm(o[:, 0:P], wk(4 * N + b * P, P), wk(5 * N + b * P, P), True, True))
                if b >= 1:
                    x = b - 1
                    pe.wait_ge(decayed_scores.sem, decayed_scores.next())
                    o = begin("l2a", "y", x)
                    for h in range(8):
                        ins = mm(o[:, h * 64:(h + 1) * 64], wk(14336 + (x % 2) * 1024 + h * P, P),
                                 wk(16384 + (x % 2) * G + h * 64, 64), True, True)
                    end(ins)
            for b in range(NB + 1):
                if b < NB:
                    pe.wait_ge(gated_y.sem, gated_y.next())
                    o = begin("l2a", "yt", b)
                    for cc in range(4):
                        ins = nc.tensor.transpose(o[:, cc * P:(cc + 1) * P], wk(10240 + b * G + cc * P, P), cst("ident"))
                    end(ins)
                if b >= 1:
                    o = begin("l2a", "o", b - 1)
                    pe.wait_ge(*freed(J("l2a", "yt", b - 1)))
                    for cc in range(4):
                        ins = mm(o[:, 0:D], XT[:, ((b - 1) % 4) * G + cc * P:((b - 1) % 4) * G + (cc + 1) * P],
                                 wo[:, cc * D:(cc + 1) * D], cc == 0, cc == 3)
                    end(ins)

            ln("l2x")
            pe.wait_ge(wa_in, 64)
            w2 = lambda n, *k, **kw: W(WA, W_L2X, n, *k, **kw)
            for c in range(2):
                for g in range(2):
                    need_xt("l2x", g)
                    for n, T in (("q", XT), ("k", CT)):
                        o = begin("l2x", n, c, g)
                        end(from_xt(o, P, g, lambda cc: w2(n, cc * D + c * P, cc * D + c * P + P), T))
            values("l2x", w2("v"), CT)
            pe.wait_ge(act_to_pe.sem, act_to_pe.next())
            pe.wait_ge(act_to_pe.sem, act_to_pe.next())
            heads("l2x", w2("o"), pad1)

            o = begin("l2f", "ws")
            pe.wait_ge(act_to_pe.sem, act_to_pe.next())
            end(mm(o[:, 0:3], cst("ones"), sm(128, 3), True, True))
            for _ in range(NB):
                pe.wait_ge(dve_to_pe.sem, dve_to_pe.next())
            pe.wait_ge(dve_to_pe.sem, dve_to_pe.next())
            for g in range(2):
                for c in range(2):
                    o = begin("l2f", "qt", g, c).bitcast(BF16)
                    for i in range(4):
                        b = 4 * g + i
                        ins = nc.tensor.transpose(o[:, i * P:(i + 1) * P],
                                                  wkb(8192, 2048)[:, b * D + c * P:b * D + (c + 1) * P], identb[:, :])
                    end(ins)
            pe.wait_ge(dve_to_pe.sem, dve_to_pe.next())
            wq = wkb(11264, 6144)
            for b in range(NB):
                for h in range(2):
                    for i, n in enumerate(("gate", "up")):
                        o = begin("l2f", n, b, h)
                        for c in range(2):
                            pe.wait_ge(*freed(J("l2f", "qt", b // 4, c)))
                            ins = mm(o, wkb(9216, 2048)[:, c * N + b * P:c * N + (b + 1) * P],
                                     wq[:, i * 2048 + c * 1024 + h * G:i * 2048 + c * 1024 + (h + 1) * G], c == 0, c == 1)
                        end(ins)
            for b in range(NB + 1):
                if b < NB:
                    pe.wait_ge(dve_to_pe.sem, dve_to_pe.next())
                    o = begin("l2f", "ht", b).bitcast(BF16)
                    for m in range(8):
                        ins = nc.tensor.transpose(o[:, m * P:(m + 1) * P], wkb(14336, 8192)[:, b * 1024 + m * P:b * 1024 + (m + 1) * P],
                                                  identb[:, :])
                    end(ins)
                if b >= 1:
                    o = begin("l2f", "o", b - 1)
                    pe.wait_ge(*freed(J("l2f", "ht", b - 1)))
                    ht = XT[:, :].bitcast(BF16)
                    for m in range(8):
                        ins = mm(o[:, 0:D], ht[:, ((b - 1) % 4) * 1024 + m * P:((b - 1) % 4) * 1024 + (m + 1) * P],
                                 wq[:, 4096 + m * D:4096 + (m + 1) * D], m == 0, m == 7)
                    end(ins)

            ln("l3a")
            pe.wait_ge(wa_in, 80)
            wi, wo = W(WA, W_L3A, "inp"), W(WA, W_L3A, "out")
            o = begin("l3a", "dt")
            need_xt("l3a", 0)
            need_xt("l3a", 1)
            for b in range(NB):
                for c in range(2):
                    ins = mm(o[:, b * 64:(b + 1) * 64], xt(c, b * P, (b + 1) * P), wi[:, c * 2112 + 2048:c * 2112 + 2112], c == 0, c == 1)
            end(ins)
            for g in range(2):
                for cc in range(12):
                    o = begin("l3a", "c", cc, g)
                    end(from_xt(o, P, g, lambda c: wi[:, c * 2112 + cc * P:c * 2112 + (cc + 1) * P]))
                for cc in range(4):
                    o = begin("l3a", "z", 4 * g + cc)
                    end(from_xt(o, P, g, lambda c: wi[:, c * 2112 + 1536 + cc * P:c * 2112 + 1536 + (cc + 1) * P]))
                pe.wait_ge(act_to_pe.sem, act_to_pe.next())
                for i in range(4):
                    o = begin("l3a", "x", 4 * g + i)
                    for cc in range(4):
                        ins = nc.tensor.transpose(o[:, cc * P:(cc + 1) * P], wk(cc * G + i * P, P), cst("ident"))
                    end(ins)

                for t in range(18):
                    if t < 16:
                        i = t // 4
                        for par in range(2 if t % 4 == 0 else 0):
                            o = begin("l3a", "cb", g, i, par)
                            for m in range(4):
                                src = lambda part: work[64 * par:64 * par + 64, (part + m) * G + i * P:(part + m) * G + (i + 1) * P]
                                ins = mm(o[:, m * P:(m + 1) * P], src(4), src(8), True, True)
                            end(ins)
                        for u in (2 * t, 2 * t + 1):
                            pe.wait_ge(decay_steps.sem, decay_steps.next())
                            for hh in range(2):
                                o = begin("l3a", "seg", g, u, hh)
                                end(mm(o, cst("strict"), XN[:, (u % 2) * 1024 + hh * G:(u % 2) * 1024 + (hh + 1) * G], True, True))
                    if 1 <= t < 17:
                        i, cc = (t - 1) // 4, (t - 1) % 4
                        if t == 1:
                            pe.wait_ge(dve_to_pe.sem, dve_to_pe.next())
                            pe.wait_ge(*freed(J("l3a", "x", 4 * g + 3)))
                        o = begin("l3a", "y", g, t - 1)
                        mm(o[:, 0:P], wk(i * G + cc * P, P), cst("ident"), True, False)
                        for x in (2 * t - 2, 2 * t - 1):
                            pe.wait_ge(decayed_scores.sem, decayed_scores.next())
                            for h in range(8):
                                q = 32 * (2 * (x % 2) + h // 4)
                                ins = mm(o[q:q + 32, 0:P], l3a_x(i)[:, ((x % 8) * 8 + h) * 32:((x % 8) * 8 + h + 1) * 32],
                                         wk(10240 + (x % 4) * 1024 + h * P, P), False, h % 4 == 3)
                        end(ins)
                    if t >= 5 and (t - 5) % 4 == 0:
                        i = (t - 5) // 4
                        b = 4 * g + i
                        o = begin("l3a", "o", b)
                        for cc in range(4):
                            pe.wait_ge(*freed(J("l3a", "y", g, 4 * i + cc)))
                            ins = mm(o[:, 0:D], wk(17408 + (b % 2) * G + cc * P, P), wo[:, cc * D:(cc + 1) * D], cc == 0, cc == 3)
                        end(ins)

            ln("l3x")
            o = begin("l3x", "val")
            end(mm(o[:, 0:NB], cst("ones", 0, 1), valid[:, :], True, True))
            for g in range(2):
                o = begin("l3x", "s", g)
                need_xt("l3x", g)
                for i in range(4):
                    b = 4 * g + i
                    oo = o[:, i * P:(i + 1) * P]
                    for c in range(2):
                        mm(oo, xt(c, b * P, (b + 1) * P), xt(c, b * P, (b + 1) * P, CT), c == 0, False)
                    ins = mm(oo, onesb[:, :], pad0[:, b * P:(b + 1) * P], False, True)
                end(ins)
            pe.wait_ge(ctx_in, 32)
            for g in range(2):
                pe.wait_ge(act_to_pe.sem, act_to_pe.next())
                o = begin("l3x", "t", g)
                for i in range(4):
                    ins = nc.tensor.transpose(o[:, i * P:(i + 1) * P], wk(g * G + i * P, P), cst("ident"))
                end(ins)
            for bp in range(4):
                o = begin("l3x", "o", bp)
                pe.wait_ge(*freed(J("l3x", "t", bp // 2)))
                for i in range(2):
                    b = 2 * bp + i
                    ins = mm(o[:, i * D:(i + 1) * D], wk(1024 + b * P, P), C[:, b * D:(b + 1) * D], True, True)
                end(ins)

            ln("l3f")
            pe.wait_ge(wb_in, 64)
            w3 = lambda n, *k, **kw: W(WB, W_L3F, n, *k, **kw)
            o = begin("l3f", "r")
            need_xt("l3f", 0)
            need_xt("l3f", 1)
            for b in range(NB):
                for c in range(2):
                    ins = mm(o[:, b * 16:(b + 1) * 16], xt(c, b * P, (b + 1) * P), w3("r", c * 16, c * 16 + 16), c == 0, c == 1)
            end(ins)
            o = begin("l3f", "mt").bitcast(BF16)
            pe.wait_ge(dve_to_pe.sem, dve_to_pe.next())
            for b in range(NB):
                ins = nc.tensor.transpose(o[0:16, b * P:(b + 1) * P], wkb(8192, 128)[:, b * 16:(b + 1) * 16], identb[:, :])
            end(ins)
            for m in range(8):
                for g in range(2):
                    o = begin("l3f", "h", m, g)
                    end(from_xt(o, P, g, lambda c: w3("w1", c * 1024 + m * P, c * 1024 + m * P + P)))
                    o = begin("l3f", "m", m, g)
                    pe.wait_ge(*freed(J("l3f", "mt")))
                    end(mm(o, wkb(8768, 1024, 0, 16)[:, 2 * m * 64:(2 * m + 2) * 64], wkb(8256, 1024, 0, 16)[:, g * G:(g + 1) * G], True, True))
            for bp in range(4):
                o = begin("l3f", "o", bp)
                for i in range(2):
                    b = 2 * bp + i
                    for m in range(8):
                        pe.wait_ge(*freed(J("l3f", "m", m, b // 4)))
                        ins = mm(o[:, i * D:(i + 1) * D], wk(m * N + b * P, P), w3("w2", m * D, m * D + D), m == 0, m == 7)
                end(ins)

        @block.scalar
        def _(act):
            J = lambda *k: job_of[k]
            f = nc.scalar.activation

            def evac(layer, tag, T, *to):
                for g in range(2):
                    for c in range(2):
                        j = J(layer, tag, g, c)
                        act.wait_ge(*full(j))
                        f(xt(c, g * G, (g + 1) * G, T), bank(j), ACT.Copy).then_inc(*act_step(j))

            def ln(layer, *to):
                act.wait_ge(dve_to_act.sem, dve_to_act.next())
                f(sm(80, 8), sm(64, 16).rearrange("p (b s) -> p b s", s=2)[:, :, 1], ACT.Sqrt,
                  bias=vec("eps5")).then_inc(*act_step(act_to_dve))
                evac(layer, "ln", XT, *to)

            act.wait_ge(cst_in, 64)
            evac("pre", "ctx", CT)

            ln("l0a")
            for g in range(2):
                j = J("l0a", "h", g)
                act.wait_ge(*full(j))
                f(wk(g * G, G, 0, 64), bank(j, 64), ACT.Relu, bias=vec("bg1", 0, p1=64)).then_inc(*act_step(j))
            for rc in range(2):
                for g in range(2):
                    j = J("l0a", "gate", rc, g)
                    act.wait_ge(*full(j))
                    f(wk(1024 + rc * N + g * G, G), bank(j), ACT.Sigmoid, bias=vec("bg2", rc)).then_inc(*act_step(act_to_dve))
                    act.wait_ge(*act_last())
                    act.sem_inc(bank_free[j % BANKS], 1)

            ln("l0x")
            for c in range(2):
                for i in range(2):
                    for k in range(2):
                        act.wait_ge(dve_to_act.sem, dve_to_act.next())
                        t = wk(4096 + (c * 4 + i * 2 + k) * N, N)
                        f(t, t, ACT.Exp).then_inc(*act_step(act_to_dve))

            ln("l0f")
            act.wait_ge(dve_to_act.sem, dve_to_act.next())
            f(wk(4096, 256), wk(4096, 256), ACT.Exp).then_inc(*act_step(act_to_dve))
            for e in range(NE):
                for g in range(2):
                    j = J("l0f", "gate", e, g)
                    act.wait_ge(*full(j))
                    if e >= 2:
                        act.wait_ge(*freed(J("l0f", "up", e - 2, g)))
                    f(wk(2048 + (e % 2) * N + g * G, G, 0, EI), bank(j, EI), ACT.Silu).then_inc(*act_step(act_to_dve))
                    act.wait_ge(*act_last())
                    act.sem_inc(bank_free[j % BANKS], 1)

            def values(layer):
                j = J(layer, "v")
                act.wait_ge(windows_zero, 1 if layer == "l1a" else 2)
                act.wait_ge(*full(j))
                f(ones_window[:, 24:32], cst("ones")[:, 0:8], ACT.Copy).then_inc(*act_step())
                act.wait_ge(*act_last())
                f(r3(v_windows[:, 24:24 + 2048], 32)[:, :, 0:8], r3(bank(j), 8), ACT.Copy).then_inc(*act_step(act_to_pe))
                act.wait_ge(*act_last())
                act.sem_inc(bank_free[j % BANKS], 1)

            def block_keys(layer, c, g, src, *to):
                for i in range(4):
                    f(wk((4 * c + i) * N + g * G, G), src, ACT.Copy, scale=cst("blk")[:, i:i + 1]).then_inc(*act_step(*(to if i == 3 else ())))

            def heads(layer):
                for key in heads_plan():
                    if key[0] == "t":
                        u = key[1]
                        j = J(layer, "t", u)
                        act.wait_ge(*full(j))
                        if u >= 16:
                            act.wait_ge(*full(J(layer, "pv", (u - 16) // 4)))
                        f(wk(8192 + (u % 16) * G, G), bank(j), ACT.Copy).then_inc(*act_step(j))
                    elif key[0] == "s":
                        act.wait_ge(dve_to_act.sem, dve_to_act.next())
                        t = wk(16384 + (key[1] % 3) * G, G)
                        f(t, t, ACT.Exp, scale=float(8 ** -0.5)).then_inc(*act_step(act_to_pe))

            ln("l1a")
            for c in range(2):
                for g in range(2):
                    act.wait_ge(dve_to_act.sem, dve_to_act.next())
                    block_keys("l1a", c, g, wk(8192 + (2 * c + g) * G, G))
            values("l1a")
            act.sem_inc(act_to_pe.sem, act_to_pe.give())
            heads("l1a")

            ln("l1x")
            for g in range(2):
                for kv in range(KV + 1):
                    if kv < KV:
                        for i, n in enumerate(("k", "kc")):
                            j = J("l1x", n, g, kv)
                            act.wait_ge(*full(j))
                            if kv == 0 and g == 1 and i == 0:
                                act.wait_ge(dve_to_act.sem, dve_to_act.next())
                            if kv >= 2:
                                act.wait_ge(*full(J("l1x", n + "2", g, kv - 2)))
                            dst = wk(8192 + kv * 4 * D, 4 * D).rearrange("p (b t) -> p b t", t=D)[:, :, (1 - i) * P:(2 - i) * P]
                            f(dst, r3(bank(j), P), ACT.Copy).then_inc(*act_step())
                            f(XN[:, ((kv % 2) * 2 + i) * G:((kv % 2) * 2 + i + 1) * G], bank(j), ACT.Square).then_inc(*act_step(act_to_dve))
                            act.wait_ge(*act_last())
                            act.sem_inc(bank_free[j % BANKS], 1)
                    if kv >= 1:
                        for i, n in enumerate(("k2", "kc2")):
                            j = J("l1x", n, g, kv - 1)
                            act.wait_ge(*full(j))
                            if (kv - 1, i) != (0, 0):
                                act.wait_ge(dve_to_act.sem, dve_to_act.next())
                            f(WA[:, 4400:4400 + G], bank(j), ACT.Sqrt, bias=vec("eps6"), scale=1.0 / P).then_inc(*act_step(act_to_dve))
                            act.wait_ge(*act_last())
                            act.sem_inc(bank_free[j % BANKS], 1)
                for i in range(4):
                    for n in ("v", "vc"):
                        j = J("l1x", n, g, i)
                        act.wait_ge(*full(j))
                        f(wk(12288 + (i * 2 + (n == "v")) * G, G), bank(j), ACT.Copy).then_inc(*act_step(j))
                for h2 in range(9):
                    if h2 < 8:
                        for h in (2 * h2, 2 * h2 + 1):
                            j = J("l1x", "q", g, h)
                            act.wait_ge(*full(j))
                            if h2 >= 2:
                                act.wait_ge(*full(J("l1x", "rq", g, h2 - 2)))
                            elif h2 == 0 and h == 0:
                                act.wait_ge(*full(J("l1x", "kc2", g, KV - 1)))
                            f(wk(h * G, G), bank(j), ACT.Copy).then_inc(*act_step())
                            f(XN[:, (h % 4) * G:(h % 4 + 1) * G], bank(j), ACT.Square).then_inc(*act_step(act_to_dve))
                            act.wait_ge(*act_last())
                            act.sem_inc(bank_free[j % BANKS], 1)
                    if h2 >= 1:
                        j = J("l1x", "rq", g, h2 - 1)
                        act.wait_ge(*full(j))
                        f(sm(640 + (h2 - 1) * 8, 8), bank(j, P, 8), ACT.Sqrt, bias=vec("eps6"), scale=1.0 / P).then_inc(*act_step(j))
                        if h2 == 8:
                            act.wait_ge(*act_last())
                            act.sem_inc(act_to_dve.sem, act_to_dve.give())
                for u in range(18):
                    if u < 16:
                        for s_ in range(2):
                            j = J("l1x", "s", g, u, s_)
                            act.wait_ge(dve_to_act.sem, dve_to_act.next())
                            if s_ == 0 and u >= 2:
                                act.wait_ge(*full(J("l1x", "t", g, u - 2, 1)))
                            for i in range(2):
                                q = 2 * s_ + i
                                last_ = i == 1
                                f(l1x_p(u)[:, q * D:(q + 1) * D], bank(j)[:, i * D:(i + 1) * D], ACT.Exp,
                                  bias=sm(704 + (u % 4) * 16 + 4 + q, 1), scale=sm(640 + ((2 * (u % 4) + s_) * 8 + (u // 4) * 2 + i), 1),
                                  accum_out=sm(704 + (u % 4) * 16 + 8 + q, 1)).then_inc(*act_step(*([act_to_dve] if last_ else [])))
                            act.wait_ge(*act_last())
                            act.sem_inc(bank_free[j % BANKS], 1)
                    if 1 <= u <= 16:
                        x = u - 1
                        j = J("l1x", "t", g, x, 1)
                        act.wait_ge(*full(j))
                        if x >= 2:
                            act.wait_ge(*full(J("l1x", "pv", g, x - 2)))
                        f(l1x_pt(x)[:, G:2 * G], bank(j), ACT.Copy).then_inc(*act_step(j))
                    if u >= 2:
                        x = u - 2
                        j = J("l1x", "pv", g, x)
                        act.wait_ge(*full(j))
                        if x % 4 == 0 and (g or x):
                            act.wait_ge(*full(J("l1x", "o", 4 * g + x // 4 - 1)))
                        f(C[:, (x % 4) * G:(x % 4 + 1) * G], bank(j), ACT.Copy).then_inc(*act_step(j))

            ln("l1f")
            for e in range(8):
                for bp in range(4):
                    t = wk(((4 * e + bp) % 4) * G, G)
                    act.wait_ge(dve_to_act.sem, dve_to_act.next())
                    for i in range(2):
                        f(t[:, i * D:(i + 1) * D], t[:, i * D:(i + 1) * D], ACT.Relu,
                          scale=wk(5376, 64)[:, (2 * bp + i) * 8 + e:(2 * bp + i) * 8 + e + 1]).then_inc(*act_step(*([act_to_dve] if i else [])))

            def softplus(lo, n):
                act.wait_ge(dve_to_act.sem, dve_to_act.next())
                f(wk(lo + n, n), wk(lo, n), ACT.Abs).then_inc(*act_step())
                act.wait_ge(*act_last())
                f(wk(lo + n, n), wk(lo + n, n), ACT.Exp, scale=-1.0).then_inc(*act_step())
                act.wait_ge(*act_last())
                f(wk(lo + n, n), wk(lo + n, n), ACT.Ln, bias=vec("one")).then_inc(*act_step(act_to_dve))

            ln("l2a")
            softplus(14336, 64)
            act.wait_ge(*act_last())
            f(sm(128, 8), vec("A_log"), ACT.Exp).then_inc(*act_step(act_to_dve))
            for g in range(2):
                for cc in range(6):
                    act.wait_ge(dve_to_act.sem, dve_to_act.next())
                    t = wk(cc * N + g * G, G)
                    f(t, t, ACT.Silu).then_inc(*act_step(*([act_to_pe] if cc == 5 else [])))
            for b in range(NB):
                j = J("l2a", "z", b)
                act.wait_ge(*full(j))
                f(wk(10240 + b * G, G), bank(j), ACT.Silu).then_inc(*act_step(j))
            for b in range(NB):
                j = J("l2a", "x", b)
                act.wait_ge(*full(j))
                f(wk(6144 + b * G, G), bank(j), ACT.Copy).then_inc(*act_step(j))
            for b in range(NB):
                for hh in range(2):
                    j = J("l2a", "seg", b, hh)
                    act.wait_ge(*full(j))
                    if b >= 2:
                        act.wait_ge(*full(J("l2a", "y", b - 2)))
                    f(wk(14336 + (b % 2) * 1024 + hh * G, G), bank(j), ACT.Exp).then_inc(*act_step(j))
            for b in range(NB):
                act.wait_ge(dve_to_act.sem, dve_to_act.next())
                if b == 0:
                    act.wait_ge(*full(J("l2a", "y", NB - 1)))
                act.wait_ge(*act_last())
                f(wk(14336 + (b % 2) * G, G), wk(10240 + b * G, G), ACT.Square, accum_out=sm(144 + b, 1)).then_inc(*act_step())
            act.wait_ge(*act_last())
            f(sm(152, 8), sm(144, 8), ACT.Sqrt, bias=vec("eps5"), scale=1.0 / 512).then_inc(*act_step(act_to_dve))
            for b in range(NB):
                j = J("l2a", "yt", b)
                act.wait_ge(*full(j))
                if b >= 4:
                    act.wait_ge(*full(J("l2a", "o", b - 4)))
                f(XT[:, (b % 4) * G:(b % 4 + 1) * G], bank(j), ACT.Copy).then_inc(*act_step(j))

            ln("l2x")
            for c in range(2):
                for g in range(2):
                    j = J("l2x", "q", c, g)
                    act.wait_ge(*full(j))
                    f(XN[:, c * N + g * G:c * N + (g + 1) * G], bank(j), ACT.Copy).then_inc(*act_step(j))
                    j = J("l2x", "k", c, g)
                    act.wait_ge(*full(j))
                    block_keys("l2x", c, g, bank(j), j)
            values("l2x")
            act.sem_inc(act_to_pe.sem, act_to_pe.give())
            heads("l2x")

            act.wait_ge(wb_in, 48)
            for i, n in enumerate(("gate", "up", "down")):
                f(wk(0, 2048), W(WB, W_L2F, n), ACT.Abs, accum_out=sm(128 + i, 1)).then_inc(*act_step(*([act_to_pe] if i == 2 else [])))
                act.wait_ge(*act_last())
            act.wait_ge(dve_to_act.sem, dve_to_act.next())
            f(sm(80, 8), sm(64, 16).rearrange("p (b s) -> p b s", s=2)[:, :, 1], ACT.Sqrt,
              bias=vec("eps5")).then_inc(*act_step(act_to_dve))
            act.wait_ge(dve_to_act.sem, dve_to_act.next())
            for b in range(NB):
                f(wk(b * D, D), XN[:, b * D:(b + 1) * D], ACT.Square, accum_out=sm(144 + b, 1)).then_inc(*act_step())
            act.wait_ge(*act_last())
            f(sm(152, 8), sm(144, 8), ACT.Sqrt, bias=vec("eps6"), scale=1.0 / D).then_inc(*act_step(act_to_dve))
            for g in range(2):
                for c in range(2):
                    j = J("l2f", "qt", g, c)
                    act.wait_ge(*full(j))
                    f(wkb(9216, 2048)[:, c * N + g * G:c * N + (g + 1) * G], bank(j).bitcast(BF16)[:, 0:G], ACT.Copy).then_inc(*act_step(j))
            act.wait_ge(dve_to_act.sem, dve_to_act.next())
            for b in range(NB):
                for h in range(2):
                    j = J("l2f", "gate", b, h)
                    act.wait_ge(*full(j))
                    if b >= 1:
                        act.wait_ge(*freed(J("l2f", "up", b - 1, h)))
                    f(wk(10240 + h * G, G), bank(j), ACT.Silu, scale=sm(184 + b, 1)).then_inc(*act_step(act_to_dve))
                    act.wait_ge(*act_last())
                    act.sem_inc(bank_free[j % BANKS], 1)
            act.wait_ge(dve_to_act.sem, dve_to_act.next())
            for b in range(NB):
                f(wk(8192, 1024), wk(b * 1024, 1024), ACT.Square, accum_out=sm(144 + b, 1)).then_inc(*act_step())
                act.wait_ge(*act_last())
            f(sm(152, 8), sm(144, 8), ACT.Sqrt, bias=vec("eps6"), scale=1.0 / 1024).then_inc(*act_step(act_to_dve))
            for b in range(NB):
                j = J("l2f", "ht", b)
                act.wait_ge(*full(j))
                if b >= 4:
                    act.wait_ge(*full(J("l2f", "o", b - 4)))
                f(XT[:, (b % 4) * G:(b % 4 + 1) * G].bitcast(BF16), bank(j).bitcast(BF16), ACT.Copy).then_inc(*act_step(j))

            ln("l3a")
            softplus(13312, 512)
            for g in range(2):
                for cc in range(12):
                    act.wait_ge(dve_to_act.sem, dve_to_act.next())
                    t = wk(cc * G, G)
                    f(t, t, ACT.Silu).then_inc(*act_step(*([act_to_pe] if cc == 11 else [])))
                for cc in range(4):
                    j = J("l3a", "z", 4 * g + cc)
                    act.wait_ge(*full(j))
                    f(wk(8192 + cc * G, G), bank(j), ACT.Silu, bias=vec("z_bias", cc)).then_inc(*act_step(j))
                if g == 0:
                    act.wait_ge(windows_zero, 6)
                for i in range(4):
                    j = J("l3a", "x", 4 * g + i)
                    act.wait_ge(dve_to_act.sem, dve_to_act.next())
                    for c in range(4):
                        f(l3a_x(i).rearrange("p (a c w) -> p a c w", c=4, w=32)[:, :, c, c * 8:c * 8 + 8],
                          bank(j).rearrange("p (a c w) -> p a c w", c=4, w=8)[:, :, c, :], ACT.Copy).then_inc(*act_step(*([j] if c == 3 else [])))
                for u in range(32):
                    for hh in range(2):
                        j = J("l3a", "seg", g, u, hh)
                        act.wait_ge(*full(j))
                        if u >= 4:
                            act.wait_ge(*full(J("l3a", "y", g, (u - 4) // 2)))
                        f(wk(10240 + (u % 4) * 1024 + hh * G, G), bank(j), ACT.Exp).then_inc(*act_step(j))

            ln("l3x")
            for g in range(2):
                act.wait_ge(dve_to_act.sem, dve_to_act.next())
                f(wk(g * G, G), wk(g * G, G), ACT.Exp, scale=1.0 / 16).then_inc(*act_step(act_to_dve))
                act.wait_ge(*act_last())
                act.sem_inc(act_to_pe.sem, act_to_pe.give())
            for g in range(2):
                j = J("l3x", "t", g)
                act.wait_ge(*full(j))
                f(wk(1024 + g * G, G), bank(j), ACT.Copy).then_inc(*act_step(j))

            ln("l3f")
            act.wait_ge(dve_to_act.sem, dve_to_act.next())
            f(wk(4096, 128), wk(4096, 128), ACT.Exp).then_inc(*act_step(act_to_dve))
            j = J("l3f", "mt")
            act.wait_ge(*full(j))
            f(wkb(8256, 1024, 0, 16), bank(j, 16).bitcast(BF16), ACT.Copy).then_inc(*act_step(j))
            for m in range(8):
                for g in range(2):
                    j = J("l3f", "h", m, g)
                    act.wait_ge(*full(j))
                    f(wk(m * N + g * G, G), bank(j), ACT.Gelu).then_inc(*act_step(act_to_dve))
                    act.wait_ge(*act_last())
                    act.sem_inc(bank_free[j % BANKS], 1)

        @block.vector
        def _(dve):
            v = nc.vector
            J = lambda *k: job_of[k]

            def ln(layer):
                for b in range(NB):
                    v.bn_stats(sm(b * 6, 6), X[:, b * D:(b + 1) * D]).then_inc(*dve_step())
                dve.wait_ge(*dve_last())
                for b in range(NB):
                    v.bn_aggr(sm(64 + b * 2, 2), sm(b * 6, 6)).then_inc(*dve_step(*([dve_to_act] if b == NB - 1 else [])))
                dve.wait_ge(act_to_dve.sem, act_to_dve.next())
                v.reciprocal(sm(88, 8), sm(80, 8)).then_inc(*dve_step())
                dve.wait_ge(*dve_last())
                for b in range(NB):
                    v.tensor_scalar(XN[:, b * D:(b + 1) * D], X[:, b * D:(b + 1) * D],
                                    sm(64 + 2 * b, 1), sm(88 + b, 1), ALU.subtract, ALU.mult).then_inc(*dve_step(dve_to_pe))
                dve.wait_ge(*dve_last())

            def residual(layer):
                for bp in range(4):
                    j = J(layer, "o", bp)
                    dve.wait_ge(*full(j))
                    x2 = X[:, bp * G:(bp + 1) * G]
                    v.tensor_tensor(x2, bank(j), x2, ALU.add).then_inc(*dve_step(j))
                dve.wait_ge(*dve_last())

            dve.wait_ge(cst_in, 64)
            v.tensor_copy(identb[:, :], cst("ident")).then_inc(*dve_step())
            v.tensor_copy(onesb[:, :], cst("ones")).then_inc(*dve_step())
            for i in range(4):
                v.tensor_copy(causalb[:, i * P:(i + 1) * P], cst("causal")).then_inc(*dve_step())
            v.memset(pad1[:, :], 0.0).then_inc(*dve_step())
            v.memset(pad0[:, :], 0.0).then_inc(*dve_step())
            dve.wait_ge(*dve_last())
            v.tensor_scalar(pad1[0:1, :], mk1[:, :], 0, NEG, ALU.is_equal, ALU.mult).then_inc(*dve_step())
            m8 = mk0[:, :].bitcast(mybir.dt.uint8)
            v.tensor_scalar(pad0[0:1, :], m8, 0, NEG, ALU.is_equal, ALU.mult).then_inc(*dve_step())
            v.tensor_reduce(valid[:, :], r3(m8, P), AX.X, ALU.max).then_inc(*dve_step())
            dve.wait_ge(x_in, 16)
            dve.wait_ge(*dve_last())
            v.tensor_scalar(valid[:, :], valid[:, :], 0.0, None, ALU.not_equal).then_inc(*dve_step())
            dve.wait_ge(*dve_last())

            ln("l0a")
            b3 = lambda ap: r3(ap, P)
            for g in range(2):
                for c in range(2):
                    dve.wait_ge(*freed(J("l0a", "ln", g, c)))
            for c in range(2):
                cv, x_ = wk(7168 + c * N, N), xt(c, 0, N)
                v.tensor_scalar(cv, x_, vec("cw0", c * 3 + 1), vec("cb0", c), ALU.mult, ALU.add).then_inc(*dve_step())
                dve.wait_ge(*dve_last())
                v.scalar_tensor_tensor(b3(cv)[:, :, 1:P], b3(x_)[:, :, 0:P - 1], vec("cw0", c * 3),
                                       b3(cv)[:, :, 1:P], ALU.mult, ALU.add).then_inc(*dve_step())
                dve.wait_ge(*dve_last())
                v.scalar_tensor_tensor(b3(cv)[:, :, 0:P - 1], b3(x_)[:, :, 1:P], vec("cw0", c * 3 + 2),
                                       b3(cv)[:, :, 0:P - 1], ALU.mult, ALU.add).then_inc(*dve_step())
                dve.wait_ge(*dve_last())
            for rc in range(2):
                for g in range(2):
                    gt = wk(1024 + rc * N + g * G, G)
                    ug, vg, cs = wk(3072, G), wk(3584, G), wk(4096, G)
                    dve.wait_ge(act_to_dve.sem, act_to_dve.next())
                    j = J("l0a", "u", rc, g)
                    dve.wait_ge(*full(j))
                    v.scalar_tensor_tensor(ug, bank(j), vec("bu", rc), gt, ALU.add, ALU.mult).then_inc(*dve_step(j))
                    j = J("l0a", "v", rc, g)
                    dve.wait_ge(*full(j))
                    v.scalar_tensor_tensor(vg, bank(j), vec("bv", rc), gt, ALU.add, ALU.mult).then_inc(*dve_step(j))
                    dve.wait_ge(*dve_last())
                    v.tensor_tensor_scan(cs, cst("nf"), ug, 0.0, ALU.mult, ALU.add).then_inc(*dve_step())
                    dve.wait_ge(*dve_last())
                    fin = [dve_to_pe] if (rc, g) == (1, 1) else []
                    v.tensor_tensor(wk(5120 + rc * N + g * G, G), cs, vg, ALU.mult).then_inc(*dve_step(*fin))
                    dve.wait_ge(*dve_last())
            residual("l0a")

            ln("l0x")
            for g in range(2):
                for c in range(2):
                    dve.wait_ge(*freed(J("l0x", "ln", g, c)))
                    dve.wait_ge(*freed(J("pre", "ctx", g, c)))
            wf = wk(12288, G)
            op_, o_, no = wk(12800, N), wk(13824, N), wk(14848, N)
            for c in range(2):
                k, ctxv = xt(c, 0, N), xt(c, 0, N, CT)
                v.scalar_tensor_tensor(r3(wf, P), r3(cst("nf"), P), vec("w", c), cst("first").unsqueeze(1).to_broadcast([P, 4, P]), ALU.mult, ALU.add).then_inc(*dve_step())
                dve.wait_ge(*dve_last())
                for h in range(2):
                    v.tensor_tensor_scan(o_[:, h * G:(h + 1) * G], wf, k[:, h * G:(h + 1) * G],
                                         -1e38, ALU.add, ALU.max).then_inc(*dve_step())
                    dve.wait_ge(*dve_last())
                v.memset(b3(op_)[:, :, 0:1], -1e38).then_inc(*dve_step())
                dve.wait_ge(*dve_last())
                v.tensor_copy(b3(op_)[:, :, 1:P], b3(o_)[:, :, 0:P - 1]).then_inc(*dve_step())
                dve.wait_ge(*dve_last())
                v.scalar_tensor_tensor(no, k, vec("u", c), op_, ALU.add, ALU.max).then_inc(*dve_step())
                dve.wait_ge(*dve_last())
                ea, ee, ea2, ee2 = (wk(4096 + (c * 4 + i) * N, N) for i in range(4))
                v.tensor_tensor(ea, op_, no, ALU.subtract).then_inc(*dve_step(dve_to_act))
                v.scalar_tensor_tensor(ee, k, vec("u", c), no, ALU.add, ALU.subtract).then_inc(*dve_step(dve_to_act))
                v.scalar_tensor_tensor(ea2, op_, vec("w", c), o_, ALU.add, ALU.subtract).then_inc(*dve_step(dve_to_act))
                v.tensor_tensor(ee2, k, o_, ALU.subtract).then_inc(*dve_step(dve_to_act))
                dve.wait_ge(*dve_last())
            for c in range(2):
                ctxv = xt(c, 0, N, CT)
                ea, ee, ea2, ee2 = (wk(4096 + (c * 4 + i) * N, N) for i in range(4))
                for _ in range(4):
                    dve.wait_ge(act_to_dve.sem, act_to_dve.next())
                ps_, qs_ = op_, o_
                v.tensor_tensor(no, ee2, ctxv, ALU.mult).then_inc(*dve_step())
                dve.wait_ge(*dve_last())
                for h in range(2):
                    s = slice(h * G, (h + 1) * G)
                    v.tensor_tensor_scan(ps_[:, s], ea2[:, s], no[:, s], 0.0, ALU.mult, ALU.add).then_inc(*dve_step())
                    dve.wait_ge(*dve_last())
                    v.tensor_tensor_scan(qs_[:, s], ea2[:, s], ee2[:, s], 0.0, ALU.mult, ALU.add).then_inc(*dve_step())
                    dve.wait_ge(*dve_last())
                v.tensor_tensor(b3(ps_)[:, :, 0:P - 1], b3(ea)[:, :, 1:P], b3(ps_)[:, :, 0:P - 1], ALU.mult).then_inc(*dve_step())
                dve.wait_ge(*dve_last())
                v.tensor_tensor(b3(qs_)[:, :, 0:P - 1], b3(ea)[:, :, 1:P], b3(qs_)[:, :, 0:P - 1], ALU.mult).then_inc(*dve_step())
                dve.wait_ge(*dve_last())
                v.tensor_tensor(no, ee, ctxv, ALU.mult).then_inc(*dve_step())
                dve.wait_ge(*dve_last())
                v.tensor_tensor(b3(no)[:, :, 1:P], b3(no)[:, :, 1:P], b3(ps_)[:, :, 0:P - 1], ALU.add).then_inc(*dve_step())
                dve.wait_ge(*dve_last())
                v.tensor_tensor(b3(ee)[:, :, 1:P], b3(ee)[:, :, 1:P], b3(qs_)[:, :, 0:P - 1], ALU.add).then_inc(*dve_step())
                dve.wait_ge(*dve_last())
                v.reciprocal(ee, ee).then_inc(*dve_step())
                dve.wait_ge(*dve_last())
                v.tensor_tensor(wk(c * N, N), no, ee, ALU.mult).then_inc(*dve_step(*([dve_to_pe] if c else [])))
                dve.wait_ge(*dve_last())
            residual("l0x")

            def topk(vals, n, k, width, v8, rl):
                for b in range(NB):
                    v.max(r3(v8, 8)[:, b, :], r3(vals, width)[:, b, 0:n]).then_inc(*dve_step())
                dve.wait_ge(*dve_last())
                v.memset(rl, LOW).then_inc(*dve_step())
                dve.wait_ge(*dve_last())
                v.tensor_copy(r3(rl, 8)[:, :, 0:k], r3(v8, 8)[:, :, 0:k]).then_inc(*dve_step())
                dve.wait_ge(*dve_last())
                for b in range(NB):
                    v.match_replace(r3(vals, width)[:, b, :], r3(rl, 8)[:, b, :],
                                    r3(vals, width)[:, b, :], IMM).then_inc(*dve_step())
                dve.wait_ge(*dve_last())

            def softmax_top(j, n, k, wt, bias=None):
                lg, e_ = wk(4096, NB * n), wk(4096, NB * n)
                dve.wait_ge(*full(j))
                v.tensor_reduce(sm(96, NB), r3(bank(j, P, NB * n), n), AX.X, ALU.max).then_inc(*dve_step())
                dve.wait_ge(*dve_last())
                v.tensor_tensor(r3(lg, n), r3(bank(j, P, NB * n), n),
                                sm(96, NB).unsqueeze(2).to_broadcast([P, NB, n]), ALU.subtract).then_inc(*dve_step(dve_to_act))
                dve.wait_ge(*dve_last())
                dve.sem_inc(bank_free[j % BANKS], 1)
                dve.wait_ge(*dve_last())
                dve.wait_ge(act_to_dve.sem, act_to_dve.next())
                width = n + 8 - k
                vals = wk(4608, NB * width)
                v.memset(vals, LOW).then_inc(*dve_step())
                dve.wait_ge(*dve_last())
                v.tensor_copy(r3(vals, width)[:, :, 0:n], r3(e_, n)).then_inc(*dve_step())
                dve.wait_ge(*dve_last())
                topk(vals, n, k, width, wk(5120, 64), wk(5184, 64))
                v.tensor_scalar(r3(wt, n), r3(vals, width)[:, :, 0:n], IMM, None, ALU.is_equal).then_inc(*dve_step())
                dve.wait_ge(*dve_last())
                return e_

            ln("l0f")
            wt = wk(5376, NB * NE)
            e_ = softmax_top(J("l0f", "r"), NE, 4, wt)
            v.tensor_tensor(wt, wt, e_, ALU.mult).then_inc(*dve_step())
            dve.wait_ge(*dve_last())
            v.tensor_reduce(sm(104, NB), r3(wt, NE), AX.X, ALU.add).then_inc(*dve_step())
            dve.wait_ge(*dve_last())
            v.reciprocal(sm(104, NB), sm(104, NB)).then_inc(*dve_step())
            dve.wait_ge(*dve_last())
            v.tensor_tensor(r3(wt, NE), r3(wt, NE), sm(104, NB).unsqueeze(2).to_broadcast([P, NB, NE]), ALU.mult).then_inc(*dve_step())
            dve.wait_ge(*dve_last())
            for e in range(NE + 1):
                if e < NE:
                    for g in range(2):
                        dve.wait_ge(act_to_dve.sem, act_to_dve.next())
                        j = J("l0f", "up", e, g)
                        dve.wait_ge(*full(j))
                        if e >= 2 and g == 0:
                            dve.wait_ge(*full(J("l0f", "down", e - 2, 3)))
                        v.tensor_tensor(wk((e % 2) * N + g * G, G, 0, EI), bank(j, EI),
                                        wk(2048 + (e % 2) * N + g * G, G, 0, EI), ALU.mult).then_inc(*dve_step(j))
                if e >= 1:
                    f = e - 1
                    dve.wait_ge(*dve_last())
                    for bp in range(4):
                        j = J("l0f", "down", f, bp)
                        dve.wait_ge(*full(j))
                        for i in range(2):
                            b = 2 * bp + i
                            x1 = X[:, b * D:(b + 1) * D]
                            v.scalar_tensor_tensor(x1, bank(j)[:, i * D:(i + 1) * D],
                                                   r3(wt, NE)[:, b, f:f + 1], x1, ALU.mult, ALU.add).then_inc(*dve_step(*([j] if i else [])))
            dve.wait_ge(*dve_last())

            def heads(layer):
                sub = ALU.subtract
                for key in heads_plan():
                    if key[0] == "s":
                        u = key[1]
                        j = J(layer, "s", u)
                        dve.wait_ge(*full(j))
                        mx = sm(704 + (u % 4) * 4, 4)
                        v.tensor_reduce(mx, r3(bank(j), P), AX.X, ALU.max).then_inc(*dve_step())
                        dve.wait_ge(*dve_last())
                        if u >= 3:
                            dve.wait_ge(*full(J(layer, "t", u - 3)))
                        v.tensor_tensor(r3(wk(16384 + (u % 3) * G, G), P), r3(bank(j), P),
                                        mx.unsqueeze(2).to_broadcast([P, 4, P]), sub).then_inc(*dve_step(dve_to_act))
                        dve.wait_ge(*dve_last())
                        dve.sem_inc(bank_free[j % BANKS], 1)
                    elif key[0] == "pv":
                        x = key[1]
                        bp, lo = x // 4, (x // 4 % 2) * G + (x % 4) * P
                        j = J(layer, "pv", x)
                        dve.wait_ge(*full(j))
                        rs = wk(17920, P)
                        v.reciprocal(rs, bank(j)[:, P:2 * P]).then_inc(*dve_step())
                        dve.wait_ge(*dve_last())
                        if bp >= 2:
                            dve.wait_ge(*full(J(layer, "o", bp - 2)))
                        v.tensor_tensor(XT[:, lo:lo + P], bank(j, P, P), rs, ALU.mult).then_inc(*dve_step(j))
                        dve.wait_ge(*dve_last())
                    elif key[0] == "o":
                        j = J(layer, "o", key[1])
                        dve.wait_ge(*full(j))
                        x2 = X[:, key[1] * G:(key[1] + 1) * G]
                        v.tensor_tensor(x2, bank(j), x2, ALU.add).then_inc(*dve_step(j))
                dve.wait_ge(*dve_last())

            ln("l1a")
            dve.wait_ge(*full(J("l1a", "ln", 1, 1)))
            tb = lambda ap: ap.unsqueeze(1).to_broadcast([P, 4, P])
            for c in range(2):
                for g in range(2):
                    for n, dst in (("q", XN[:, c * N + g * G:c * N + (g + 1) * G]), ("k", wk(8192 + (2 * c + g) * G, G))):
                        t = wk(12288, G)
                        j = J("l1a", n, c, g)
                        dve.wait_ge(*full(j))
                        v.tensor_tensor(r3(dst, P), r3(bank(j), P), tb(cst("cos1")), ALU.mult).then_inc(*dve_step(j))
                        j = J("l1a", n + "s", c, g)
                        dve.wait_ge(*full(j))
                        v.tensor_tensor(r3(t, P), r3(bank(j), P), tb(cst("sin1")), ALU.mult).then_inc(*dve_step(j))
                        dve.wait_ge(*dve_last())
                        v.tensor_tensor(dst, dst, t, ALU.add).then_inc(*dve_step(*([dve_to_act] if n == "k" else [])))
                        dve.wait_ge(*dve_last())
            heads("l1a")

            ln("l1x")
            qcos, qsin, kcos, ksin = (sm(128 + i * P, P) for i in range(4))
            v.tensor_scalar(qcos, cst("cosx"), vec("qn"), None, ALU.mult).then_inc(*dve_step())
            v.tensor_scalar(qsin, cst("sinx"), vec("qn"), -1.0, ALU.mult, ALU.mult).then_inc(*dve_step())
            v.tensor_scalar(kcos, cst("cosx"), vec("kn"), None, ALU.mult).then_inc(*dve_step())
            v.tensor_scalar(ksin, cst("sinx"), vec("kn"), -1.0, ALU.mult, ALU.mult).then_inc(*dve_step())
            dve.wait_ge(*dve_last())
            rot = WA[:, 4912:4912 + G]

            def rotate(q, cos, sin):
                h = lambda ap, lo: ap[lo:lo + 64]
                t = r3(rot, P)
                bc = lambda ap, lo: ap[lo:lo + 64, :].unsqueeze(1).to_broadcast([64, 4, P])
                v.tensor_tensor(h(t, 0), h(q, 64), bc(sin, 64), ALU.mult).then_inc(*dve_step())
                v.tensor_tensor(h(t, 64), h(q, 0), bc(sin, 0), ALU.mult).then_inc(*dve_step())
                dve.wait_ge(*dve_last())
                v.tensor_tensor(q, q, tb(cos), ALU.mult).then_inc(*dve_step())
                dve.wait_ge(*dve_last())
                v.tensor_tensor(q, q, t, ALU.add).then_inc(*dve_step())
                dve.wait_ge(*dve_last())

            rootb = WA[:, 4400:4400 + G]
            for g in range(2):
                if g == 1:
                    dve.sem_inc(dve_to_act.sem, dve_to_act.give())
                for kv in range(KV):
                    for _ in range(2):
                        dve.wait_ge(act_to_dve.sem, act_to_dve.next()) if kv == 0 else None
                for kv in range(1, KV + 1):
                    for _ in range(2):
                        if kv < KV:
                            dve.wait_ge(act_to_dve.sem, act_to_dve.next())
                    for i in range(2):
                        dve.wait_ge(act_to_dve.sem, act_to_dve.next())
                        kk = wk(8192 + (kv - 1) * 4 * D, 4 * D).rearrange("p (b t) -> p b t", t=D)[:, :, (1 - i) * P:(2 - i) * P]
                        v.reciprocal(rootb, rootb).then_inc(*dve_step())
                        dve.wait_ge(*dve_last())
                        if i == 0:
                            rotate(kk, kcos, ksin)
                            v.tensor_tensor(kk, kk, r3(rootb, P), ALU.mult).then_inc(*dve_step(*([dve_to_act])))
                            dve.wait_ge(*dve_last())
                        else:
                            v.scalar_tensor_tensor(kk, kk, vec("kn"), r3(rootb, P), ALU.mult, ALU.mult).then_inc(*dve_step(*([dve_to_act] if kv < KV else [])))
                            dve.wait_ge(*dve_last())
                for h in range(XH):
                    dve.wait_ge(act_to_dve.sem, act_to_dve.next())
                    rotate(r3(wk(h * G, G), P), qcos, qsin)
                dve.wait_ge(act_to_dve.sem, act_to_dve.next())
                v.reciprocal(sm(640, 64), sm(640, 64)).then_inc(*dve_step())
                dve.wait_ge(*dve_last())
                v.tensor_scalar(sm(640, 64), sm(640, 64), float(P ** -0.5), None, ALU.mult).then_inc(*dve_step(dve_to_pe))
                dve.wait_ge(*dve_last())
                for u in range(18):
                    base = 704 + (u % 4) * 16
                    if u < 16:
                        for s_ in range(2):
                            j = J("l1x", "s", g, u, s_)
                            dve.wait_ge(*full(j))
                            v.tensor_reduce(sm(base + 2 * s_, 2), r3(bank(j), D), AX.X, ALU.max).then_inc(*dve_step())
                            dve.wait_ge(*dve_last())
                            v.scalar_tensor_tensor(sm(base + 4 + 2 * s_, 2), sm(base + 2 * s_, 2), -1.0,
                                                   sm(640 + (2 * (u % 4) + s_) * 8 + (u // 4) * 2, 2), ALU.mult, ALU.mult).then_inc(*dve_step(dve_to_act))
                        dve.wait_ge(act_to_dve.sem, act_to_dve.next())
                        dve.wait_ge(act_to_dve.sem, act_to_dve.next())
                        v.reciprocal(sm(base + 12, 4), sm(base + 8, 4)).then_inc(*dve_step())
                        dve.wait_ge(*dve_last())
                        for q in range(4):
                            pq = l1x_p(u)[:, q * D:(q + 1) * D]
                            v.tensor_scalar(pq, pq, sm(base + 12 + q, 1), None, ALU.mult).then_inc(*dve_step(*([dve_to_pe] if q == 3 else [])))
                    if 1 <= u <= 16:
                        x = u - 1
                        j = J("l1x", "t", g, x, 0)
                        dve.wait_ge(*full(j))
                        if x >= 2:
                            dve.wait_ge(*full(J("l1x", "pv", g, x - 2)))
                        v.tensor_copy(l1x_pt(x)[:, 0:G], bank(j)).then_inc(*dve_step(j))
                    if u >= 2 and (u - 2) % 4 == 3:
                        b = 4 * g + (u - 2) // 4
                        j = J("l1x", "o", b)
                        dve.wait_ge(*full(j))
                        x1 = X[:, b * D:(b + 1) * D]
                        v.tensor_tensor(x1, bank(j, P, D), x1, ALU.add).then_inc(*dve_step(j))
                dve.wait_ge(*dve_last())

            ln("l1f")
            j = J("l1f", "r")
            dve.wait_ge(*full(j))
            width = 8 + 6
            vals, wt = wk(4608, NB * width), wk(5376, 64)
            v.memset(vals, LOW).then_inc(*dve_step())
            dve.wait_ge(*dve_last())
            v.tensor_tensor(r3(vals, width)[:, :, 0:8], r3(bank(j, P, 64), 8),
                            vec("gate_b").unsqueeze(1).to_broadcast([P, NB, 8]), ALU.add).then_inc(*dve_step(j))
            dve.wait_ge(*dve_last())
            topk(vals, 8, 2, width, wk(5120, 64), wk(5184, 64))
            v.tensor_scalar(r3(wt, 8), r3(vals, width)[:, :, 0:8], IMM, 0.5, ALU.is_equal, ALU.mult).then_inc(*dve_step())
            dve.wait_ge(*dve_last())
            dve.wait_ge(eb_in, 16)
            for n in range(32 + 2):
                if n < 32:
                    e, bp = n // 4, n % 4
                    j = J("l1f", "e", e, bp)
                    dve.wait_ge(*full(j))
                    v.tensor_tensor(r3(wk((n % 4) * G, G), D), r3(bank(j), D),
                                    expert_b[:, e * D:(e + 1) * D].unsqueeze(1).to_broadcast([P, 2, D]), ALU.add).then_inc(*dve_step(dve_to_act))
                    dve.wait_ge(*dve_last())
                    dve.sem_inc(bank_free[j % BANKS], 1)
                if n >= 2:
                    m = n - 2
                    dve.wait_ge(act_to_dve.sem, act_to_dve.next())
                    x2 = X[:, (m % 4) * G:(m % 4 + 1) * G]
                    v.tensor_tensor(x2, x2, wk((m % 4) * G, G), ALU.add).then_inc(*dve_step())
                    dve.wait_ge(*dve_last())

            def conv(j, dst, taps, bias):
                dve.wait_ge(*full(j))
                p, d = r3(bank(j), P), r3(dst, P)
                v.tensor_scalar(dst, bank(j), vec(taps[0], taps[1] + 3), vec(bias[0], bias[1]), ALU.mult, ALU.add).then_inc(*dve_step())
                dve.wait_ge(*dve_last())
                for k in (1, 2, 3):
                    v.scalar_tensor_tensor(d[:, :, k:P], p[:, :, 0:P - k], vec(taps[0], taps[1] + 3 - k),
                                           d[:, :, k:P], ALU.mult, ALU.add).then_inc(*dve_step(*([dve_to_act] if k == 3 else [])))
                    dve.wait_ge(*dve_last())
                dve.sem_inc(bank_free[j % BANKS], 1)

            ln("l2a")
            b8 = lambda ap, m: ap.unsqueeze(2).to_broadcast([P, ap.shape[1], m])
            wo = W(WB, W_L2A, "out")
            dve.wait_ge(wb_in, 32)
            for cc in range(4):
                v.tensor_scalar(wo[:, cc * D:(cc + 1) * D], wo[:, cc * D:(cc + 1) * D], vec("nw2", cc), None, ALU.mult).then_inc(*dve_step())
            j = J("l2a", "dt")
            dve.wait_ge(*full(j))
            raw, dt, am = wk(14336, 64), wk(14464, 64), sm(160, 64)
            dt = sm(224, 64)
            v.tensor_tensor(r3(raw, 8), r3(bank(j, P, 64), 8), vec("dt_bias").unsqueeze(1).to_broadcast([P, NB, 8]), ALU.add).then_inc(*dve_step(dve_to_act))
            dve.wait_ge(*dve_last())
            dve.sem_inc(bank_free[j % BANKS], 1)
            dve.wait_ge(*dve_last())
            dve.wait_ge(act_to_dve.sem, act_to_dve.next())
            v.scalar_tensor_tensor(dt, raw, 0.0, wk(14400, 64), ALU.max, ALU.add).then_inc(*dve_step())
            dve.wait_ge(*dve_last())
            dve.wait_ge(act_to_dve.sem, act_to_dve.next())
            v.scalar_tensor_tensor(r3(am, 8), r3(dt, 8), -1.0, sm(128, 8).unsqueeze(1).to_broadcast([P, NB, 8]), ALU.mult, ALU.mult).then_inc(*dve_step())
            dve.wait_ge(*dve_last())
            for g in range(2):
                for cc in range(6):
                    conv(J("l2a", "c", cc, g), wk(cc * N + g * G, G), ("cw2", cc * 4), ("cb2", cc))
            for b in range(NB + 1):
                if b < NB:
                    if b >= 2:
                        dve.wait_ge(*full(J("l2a", "seg", b - 2, 1)))
                    v.tensor_tensor(r3(XN[:, (b % 2) * 1024:(b % 2 + 1) * 1024], P), b8(am[:, b * 8:(b + 1) * 8], P),
                                    cst("tri").unsqueeze(1).to_broadcast([P, 8, P]), ALU.mult).then_inc(*dve_step(decay_steps))
                if b >= 1:
                    x = b - 1
                    if x == 0:
                        dve.wait_ge(*freed(J("l2a", "x", NB - 1)))
                    xs, e_ = wk(6144 + x * G, G), wk(14336 + (x % 2) * 1024, 1024)
                    cbm = wk(17408 + (x % 2) * P, P)
                    j = J("l2a", "cb", x)
                    dve.wait_ge(*full(j))
                    v.tensor_tensor(cbm, bank(j, P, P), cst("tri"), ALU.mult).then_inc(*dve_step(j))
                    if x >= 2:
                        dve.wait_ge(*full(J("l2a", "y", x - 2)))
                    v.tensor_tensor(r3(wk(16384 + (x % 2) * G, G), 64), r3(xs, 64), b8(dt[:, x * 8:(x + 1) * 8], 64), ALU.mult).then_inc(*dve_step())
                    dve.wait_ge(*dve_last())
                    dve.wait_ge(*freed(J("l2a", "seg", x, 0)))
                    dve.wait_ge(*freed(J("l2a", "seg", x, 1)))
                    v.tensor_tensor(r3(e_, P), r3(e_, P), cbm.unsqueeze(1).to_broadcast([P, 8, P]), ALU.mult).then_inc(*dve_step(decayed_scores))
                    v.tensor_tensor(r3(xs, 64), r3(xs, 64), b8(vec("D2"), 64), ALU.mult).then_inc(*dve_step())
                    dve.wait_ge(*dve_last())
                    j = J("l2a", "y", x)
                    dve.wait_ge(*full(j))
                    v.tensor_tensor(xs, bank(j), xs, ALU.add).then_inc(*dve_step(j))
                    dve.wait_ge(*dve_last())
                    dve.wait_ge(*freed(J("l2a", "z", x)))
                    v.tensor_tensor(wk(10240 + x * G, G), wk(10240 + x * G, G), xs, ALU.mult).then_inc(*dve_step(gated_y))
                    dve.wait_ge(*dve_last())
                    dve.sem_inc(dve_to_act.sem, dve_to_act.give())
                    dve.wait_ge(*dve_last())
            dve.wait_ge(act_to_dve.sem, act_to_dve.next())
            v.reciprocal(sm(152, 8), sm(152, 8)).then_inc(*dve_step())
            dve.wait_ge(*dve_last())

            def scaled_residual(layer, at):
                for b in range(NB):
                    j = J(layer, "o", b)
                    dve.wait_ge(*full(j))
                    x1 = X[:, b * D:(b + 1) * D]
                    v.scalar_tensor_tensor(x1, bank(j, P, D), sm(at + b, 1), x1, ALU.mult, ALU.add).then_inc(*dve_step(j))
                dve.wait_ge(*dve_last())

            scaled_residual("l2a", 152)

            ln("l2x")
            v.tensor_tensor(r3(X[:, :], D), r3(X[:, :], D), vec("b_o").unsqueeze(1).to_broadcast([P, NB, D]), ALU.add).then_inc(*dve_step())
            dve.wait_ge(*dve_last())
            heads("l2x")

            MAGIC = float(3 << 22)
            ln("l2f")
            dve.wait_ge(*dve_last())
            dve.sem_inc(dve_to_act.sem, dve_to_act.give())
            v.tensor_reduce(sm(160, 8), r3(XN[:, :], D), AX.X, ALU.max, apply_absolute_value=True).then_inc(*dve_step())
            dve.wait_ge(*dve_last())
            j = J("l2f", "ws")
            dve.wait_ge(*full(j))
            wm, wr = sm(128 + 8, 3), sm(128 + 11, 3)
            v.tensor_scalar(wm, bank(j, P, 3), 1.0 / (D * 1024), 1e-5, ALU.mult, ALU.max).then_inc(*dve_step(j))
            dve.wait_ge(*dve_last())
            v.reciprocal(wr, wm).then_inc(*dve_step())
            dve.wait_ge(*dve_last())

            def activation_scales(out_scale):
                dve.wait_ge(act_to_dve.sem, act_to_dve.next())
                v.reciprocal(sm(152, 8), sm(152, 8)).then_inc(*dve_step())
                dve.wait_ge(*dve_last())
                v.tensor_tensor(sm(160, 8), sm(160, 8), sm(152, 8), ALU.mult).then_inc(*dve_step())
                dve.wait_ge(*dve_last())
                v.tensor_scalar(sm(160, 8), sm(160, 8), 1e-5, None, ALU.max).then_inc(*dve_step())
                dve.wait_ge(*dve_last())
                v.reciprocal(sm(168, 8), sm(160, 8)).then_inc(*dve_step())
                dve.wait_ge(*dve_last())
                v.tensor_scalar(sm(168, 8), sm(168, 8), 127.0, None, ALU.mult).then_inc(*dve_step())
                dve.wait_ge(*dve_last())
                v.reciprocal(sm(176, 8), sm(168, 8)).then_inc(*dve_step())
                dve.wait_ge(*dve_last())
                v.tensor_tensor(sm(168, 8), sm(168, 8), sm(152, 8), ALU.mult).then_inc(*dve_step())
                dve.wait_ge(*dve_last())

            activation_scales(176)
            v.tensor_scalar(sm(184, 8), sm(176, 8), wm[:, 0:1], None, ALU.mult).then_inc(*dve_step())
            v.tensor_scalar(sm(192, 8), sm(176, 8), wm[:, 1:2], None, ALU.mult).then_inc(*dve_step(dve_to_act))
            for b in range(NB):
                xb = XN[:, b * D:(b + 1) * D]
                v.tensor_scalar(xb, xb, sm(168 + b, 1), MAGIC, ALU.mult, ALU.add).then_inc(*dve_step())
            dve.wait_ge(*dve_last())
            v.tensor_scalar(XN[:, :], XN[:, :], MAGIC - 128.0, MAGIC + 127.0, ALU.max, ALU.min).then_inc(*dve_step())
            dve.wait_ge(*dve_last())
            v.tensor_scalar(wkb(8192, 2048), XN[:, :], MAGIC, None, ALU.subtract).then_inc(*dve_step(dve_to_pe))
            dve.wait_ge(*dve_last())
            dve.wait_ge(wb_in, 48)
            for i, n in enumerate(("gate", "up", "down")):
                wx_ = W(WB, W_L2F, n)
                v.tensor_scalar(wx_, wx_, wr[:, i:i + 1], MAGIC, ALU.mult, ALU.add).then_inc(*dve_step())
                dve.wait_ge(*dve_last())
                v.tensor_scalar(wx_, wx_, MAGIC - 1.0, MAGIC + 1.0, ALU.max, ALU.min).then_inc(*dve_step())
                dve.wait_ge(*dve_last())
                v.tensor_scalar(wkb(11264, 6144)[:, i * 2048:(i + 1) * 2048], wx_, MAGIC, None, ALU.subtract).then_inc(*dve_step(*([dve_to_pe] if i == 2 else [])))
                dve.wait_ge(*dve_last())
            for b in range(NB):
                for h in range(2):
                    dve.wait_ge(act_to_dve.sem, act_to_dve.next())
                    j = J("l2f", "up", b, h)
                    dve.wait_ge(*full(j))
                    v.scalar_tensor_tensor(wk(b * 1024 + h * G, G), bank(j), sm(192 + b, 1), wk(10240 + h * G, G),
                                           ALU.mult, ALU.mult).then_inc(*dve_step(j))
            dve.wait_ge(*dve_last())
            dve.sem_inc(dve_to_act.sem, dve_to_act.give())
            v.tensor_reduce(sm(160, 8), r3(wk(0, 8192), 1024), AX.X, ALU.max, apply_absolute_value=True).then_inc(*dve_step())
            dve.wait_ge(*dve_last())
            activation_scales(176)
            v.tensor_scalar(sm(200, 8), sm(176, 8), wm[:, 2:3], None, ALU.mult).then_inc(*dve_step())
            dve.wait_ge(*dve_last())
            for b in range(NB):
                hb = wk(b * 1024, 1024)
                v.tensor_scalar(hb, hb, sm(168 + b, 1), MAGIC, ALU.mult, ALU.add).then_inc(*dve_step())
                dve.wait_ge(*dve_last())
                v.tensor_scalar(hb, hb, MAGIC - 128.0, MAGIC + 127.0, ALU.max, ALU.min).then_inc(*dve_step())
                dve.wait_ge(*dve_last())
                v.tensor_scalar(wkb(14336, 8192)[:, b * 1024:(b + 1) * 1024], hb, MAGIC, None, ALU.subtract).then_inc(*dve_step(dve_to_pe))
                dve.wait_ge(*dve_last())
            scaled_residual("l2f", 200)

            ln("l3a")
            raw, dt, rx = wk(13312, 512), wk(14336, 512), wk(14848, 512)
            j = J("l3a", "dt")
            dve.wait_ge(*full(j))
            v.tensor_copy(raw, bank(j)).then_inc(*dve_step(dve_to_act))
            dve.wait_ge(*dve_last())
            dve.sem_inc(bank_free[j % BANKS], 1)
            dve.wait_ge(*dve_last())
            dve.wait_ge(act_to_dve.sem, act_to_dve.next())
            v.scalar_tensor_tensor(dt, raw, 0.0, wk(13824, 512), ALU.max, ALU.add).then_inc(*dve_step())
            dve.wait_ge(*dve_last())
            v.reciprocal(rx, dt).then_inc(*dve_step())
            dve.wait_ge(*dve_last())
            v.tensor_tensor(r3(rx, 64), r3(rx, 64), vec("D3").unsqueeze(1).to_broadcast([P, NB, 64]), ALU.mult).then_inc(*dve_step())
            dve.wait_ge(*dve_last())
            v.tensor_scalar(dt, dt, -1.0, None, ALU.mult).then_inc(*dve_step())
            dve.wait_ge(*dve_last())
            for g in range(2):
                for cc in range(12):
                    conv(J("l3a", "c", cc, g), wk(cc * G, G), ("cw3", cc * 4), ("cb3", cc))
                dve.wait_ge(*full(J("l3a", "x", 4 * g + 3)))
                for i in range(4):
                    b = 4 * g + i
                    v.tensor_tensor(r3(wk(i * G, G), 8), r3(bank(J("l3a", "x", b)), 8), b8(rx[:, b * 64:(b + 1) * 64], 8),
                                    ALU.mult).then_inc(*dve_step(dve_to_act))
                dve.wait_ge(*dve_last())
                dve.sem_inc(dve_to_pe.sem, dve_to_pe.give())

                def decay(u):
                    b, q8 = 4 * g + u // 8, u % 8
                    if u >= 2:
                        dve.wait_ge(*full(J("l3a", "seg", g, u - 2, 1)))
                    v.tensor_tensor(r3(XN[:, (u % 2) * 1024:(u % 2 + 1) * 1024], P), b8(dt[:, b * 64 + q8 * 8:b * 64 + q8 * 8 + 8], P),
                                    cst("tri").unsqueeze(1).to_broadcast([P, 8, P]), ALU.mult).then_inc(*dve_step(decay_steps))

                def scores(u):
                    e_ = wk(10240 + (u % 4) * 1024, 1024)
                    dve.wait_ge(*freed(J("l3a", "seg", g, u, 0)))
                    dve.wait_ge(*freed(J("l3a", "seg", g, u, 1)))
                    cbm = wk(16384 + (u % 2) * G + (u % 8 // 2) * P, P)
                    v.tensor_tensor(r3(e_, P), r3(e_, P), cbm.unsqueeze(1).to_broadcast([P, 8, P]), ALU.mult).then_inc(*dve_step(decayed_scores))

                def outp(b):
                    j = J("l3a", "o", b)
                    dve.wait_ge(*full(j))
                    x1 = X[:, b * D:(b + 1) * D]
                    v.tensor_tensor(x1, bank(j, P, D), x1, ALU.add).then_inc(*dve_step(j))

                decay(0)
                for t in range(18):
                    if t < 16:
                        decay(2 * t + 1)
                        for par in range(2 if t % 4 == 0 else 0):
                            j = J("l3a", "cb", g, t // 4, par)
                            dve.wait_ge(*full(j))
                            dve.wait_ge(*dve_last())
                            v.tensor_tensor(r3(wk(16384 + par * G, G), P), r3(bank(j), P),
                                            cst("tri").unsqueeze(1).to_broadcast([P, 4, P]), ALU.mult).then_inc(*dve_step(j))
                        if t % 4 == 0:
                            dve.wait_ge(*dve_last())
                        scores(2 * t)
                    if t >= 2:
                        p = t - 2
                        i, cc = p // 4, p % 4
                        j = J("l3a", "y", g, p)
                        dve.wait_ge(*full(j))
                        if p == 0:
                            dve.wait_ge(*freed(J("l3a", "z", 4 * g + 3)))
                        v.tensor_tensor(wk(17408 + (i % 2) * G + cc * P, P), bank(j, P, P), wk(8192 + cc * G + i * P, P),
                                        ALU.mult).then_inc(*dve_step(j))
                    if t < 16:
                        if t < 15:
                            decay(2 * t + 2)
                        scores(2 * t + 1)
                    if t >= 6 and (t - 6) % 4 == 0:
                        outp(4 * g + (t - 6) // 4)
                outp(4 * g + 3)
                dve.wait_ge(*dve_last())

            ln("l3x")
            for g in range(2):
                j = J("l3x", "s", g)
                dve.wait_ge(*full(j))
                v.tensor_reduce(sm(128 + 4 * g, 4), r3(bank(j), P), AX.X, ALU.max).then_inc(*dve_step())
                dve.wait_ge(*dve_last())
                v.tensor_tensor(r3(wk(g * G, G), P), r3(bank(j), P), b8(sm(128 + 4 * g, 4), P), ALU.subtract).then_inc(*dve_step(dve_to_act))
                dve.wait_ge(*dve_last())
                dve.sem_inc(bank_free[j % BANKS], 1)
            j = J("l3x", "val")
            dve.wait_ge(*full(j))
            v.tensor_copy(sm(136, 8), bank(j, P, 8)).then_inc(*dve_step(j))
            for g in range(2):
                dve.wait_ge(act_to_dve.sem, act_to_dve.next())
                v.tensor_reduce(sm(144 + 4 * g, 4), r3(wk(g * G, G), P), AX.X, ALU.add).then_inc(*dve_step())
                dve.wait_ge(*dve_last())
            v.reciprocal(sm(144, 8), sm(144, 8)).then_inc(*dve_step())
            dve.wait_ge(*dve_last())
            v.tensor_tensor(sm(144, 8), sm(144, 8), sm(136, 8), ALU.mult).then_inc(*dve_step())
            dve.wait_ge(*dve_last())
            for bp in range(4):
                j = J("l3x", "o", bp)
                dve.wait_ge(*full(j))
                for i in range(2):
                    b = 2 * bp + i
                    x1 = X[:, b * D:(b + 1) * D]
                    v.scalar_tensor_tensor(x1, bank(j)[:, i * D:(i + 1) * D], sm(144 + b, 1), x1, ALU.mult, ALU.add).then_inc(*dve_step(*([j] if i else [])))
            dve.wait_ge(*dve_last())

            ln("l3f")
            j = J("l3f", "r")
            dve.wait_ge(*full(j))
            lg = wk(4096, 128)
            v.tensor_tensor(r3(lg, 16), r3(bank(j, P, 128), 16), vec("br").unsqueeze(1).to_broadcast([P, NB, 16]), ALU.add).then_inc(*dve_step(j))
            dve.wait_ge(*dve_last())
            v.tensor_reduce(sm(128, 8), r3(lg, 16), AX.X, ALU.max).then_inc(*dve_step())
            dve.wait_ge(*dve_last())
            v.tensor_tensor(r3(lg, 16), r3(lg, 16), b8(sm(128, 8), 16), ALU.subtract).then_inc(*dve_step(dve_to_act))
            dve.wait_ge(*dve_last())
            dve.wait_ge(act_to_dve.sem, act_to_dve.next())
            width = 16 + 4
            vals = wk(4608, NB * width)
            v.memset(vals, LOW).then_inc(*dve_step())
            dve.wait_ge(*dve_last())
            v.tensor_copy(r3(vals, width)[:, :, 0:16], r3(lg, 16)).then_inc(*dve_step())
            dve.wait_ge(*dve_last())
            topk(vals, 16, 4, width, wk(5120, 64), wk(5184, 64))
            v.tensor_copy(r3(wkb(8768, 1024, 0, 16), 64), cst("ident", 0, 16)[:, 0:16].unsqueeze(2).to_broadcast([16, 16, 64])).then_inc(*dve_step())
            v.tensor_scalar(r3(wkb(8192, 128), 16), r3(vals, width)[:, :, 0:16], IMM, None, ALU.is_equal).then_inc(*dve_step(dve_to_pe))
            dve.wait_ge(*dve_last())
            for m in range(8):
                for g in range(2):
                    dve.wait_ge(act_to_dve.sem, act_to_dve.next())
                    j = J("l3f", "m", m, g)
                    dve.wait_ge(*full(j))
                    t = wk(m * N + g * G, G)
                    v.tensor_tensor(t, bank(j), t, ALU.mult).then_inc(*dve_step(j))
            residual("l3f")
            dve.sem_inc(x_final, 1)


def _cols(w):
    w = np.asarray(w)
    if w.shape[0] < P:
        w = np.concatenate([w, np.zeros((P - w.shape[0], w.shape[1]), w.dtype)])
    return w.reshape(-1, P, w.shape[1]).transpose(1, 0, 2).reshape(P, -1)


def _row(v):
    return np.broadcast_to(np.asarray(v).reshape(1, -1), (P, np.asarray(v).size))


def _chan(v):
    v = np.asarray(v)
    return _cols(v.reshape(v.shape[0], -1))


def _constants():
    i = np.arange(P)
    c = {}
    c["ident"] = np.eye(P)
    c["tri"] = (i[:, None] <= i[None, :]) * 1.0
    c["strict"] = (i[:, None] > i[None, :]) * 1.0
    c["ones"] = np.ones((P, P))
    c["causal"] = np.where(i[None, :] > i[:, None], NEG, 0.0)
    th = (1.0 / 10000.0 ** (2.0 * np.arange(4) / 8)).astype(np.float32)
    ang = (np.arange(P, dtype=np.float32)[:, None] * th[None, :]).astype(np.float32)
    d = i % 8
    c["cos1"] = np.cos(ang[:, d // 2]).T
    c["sin1"] = np.sin(ang[:, d // 2]).T * np.where(d % 2 == 0, -1.0, 1.0)[:, None]
    inv = (1.0 / 10000.0 ** (np.arange(0, P, 2, dtype=np.float32) / P)).astype(np.float32)
    ang = (np.arange(P, dtype=np.float32)[:, None] * inv[None, :]).astype(np.float32)
    c["cosx"] = np.cos(ang[:, i % 64]).T
    c["sinx"] = np.sin(ang[:, i % 64]).T * np.where(i < 64, -1.0, 1.0)[:, None]
    t = np.arange(G) % P
    c["nf"] = np.broadcast_to((t > 0) * 1.0, (P, G))
    c["first"] = np.broadcast_to(np.where(i > 0, 0.0, -1e38), (P, P))
    c["blk"] = ((i[:, None] // 8) % 4 == np.arange(4)[None, :]) * 1.0
    return np.concatenate([c[k] for k in CST], axis=1).astype(np.float32)


def _layout(z):
    swap = np.arange(D).reshape(-1, 2)[:, ::-1].reshape(-1)
    half = np.concatenate([np.arange(64, 128), np.arange(0, 64)])
    krep = (np.arange(8)[:, None, None] * 8 + np.zeros((1, 4, 1), int) + np.arange(8)[None, None, :]).reshape(-1)
    v = {
        "bu": _chan(z["L0_attn_bu"]), "bv": _chan(z["L0_attn_bv"]), "bg1": _chan(z["L0_attn_bg1"]),
        "bg2": _chan(z["L0_attn_bg2"]), "cw0": _chan(z["L0_attn_conv_w"]), "cb0": _chan(z["L0_attn_conv_b"]),
        "w": _chan(z["L0_xattn_w"]), "u": _chan(z["L0_xattn_u"]), "rw0": _cols(z["L0_ffn_router_w"].T),
        "qn": _chan(z["L1_xattn_q_norm_w"]), "kn": _chan(z["L1_xattn_k_norm_w"]),
        "qns": _chan(z["L1_xattn_q_norm_w"][half]), "kns": _chan(z["L1_xattn_k_norm_w"][half]),
        "cw2": _chan(z["L2_attn_conv_w"]), "cb2": _chan(z["L2_attn_conv_b"]), "nw2": _chan(z["L2_attn_norm_w"]),
        "cw3": _chan(z["L3_attn_conv1d_weight"]), "cb3": _chan(z["L3_attn_conv1d_bias"]),
        "gate_b": _row(z["L1_ffn_gate_b"]), "dt_bias": _row(z["L2_attn_dt_bias"]), "A_log": _row(z["L2_attn_A_log"]),
        "D2": _row(z["L2_attn_D_param"]), "D3": _row(z["L3_attn_D"]), "br": _row(z["L3_ffn_br"]),
        "z_bias": _chan(z["L3_attn_z_bias"]), "b_o": _row(z["L2_xattn_b_o"]),
        "eps5": _row([1e-5]), "eps6": _row([1e-6]), "one": _row([1.0]), "zero": _row([0.0]),
    }
    for name, n in VEC.items():
        assert v[name].shape == (P, n), (name, v[name].shape)
    o = {"x": z["x"], "ctx": z["ctx_2048"], "cst": _constants(),
         "vec": np.concatenate([v[k] for k in VEC], axis=1).astype(np.float32)}
    cat = lambda *l: np.concatenate(l, axis=1)
    o["l0a"] = cat(_cols(z["L0_attn_Wu"].T), _cols(z["L0_attn_Wv"].T), _cols(z["L0_attn_Wg1"].T),
                   _cols(z["L0_attn_Wg2"].T))
    o["l0f"] = cat(*[cat(_cols(z["L0_ffn_gate_w"][e].T), _cols(z["L0_ffn_up_w"][e].T), _cols(z["L0_ffn_down_w"][e].T))
                     for e in range(NE)])
    q, k = z["L1_attn_Wq"], z["L1_attn_Wk"][:, krep]
    o["l1a"] = cat(_cols(q), _cols(q[:, swap]), _cols(k), _cols(k[:, swap]), _cols(z["L1_attn_Wv"]), _cols(z["L1_attn_Wo"]))
    o["l1x"] = cat(*[_cols(z["L1_xattn_" + n]) for n in ("wq", "wk", "wv", "wk_ctx", "wv_ctx", "wo")])
    o["l1f"] = cat(_cols(z["L1_ffn_gate_w"]), *[_cols(z["L1_ffn_expert_w"][e]) for e in range(8)])
    o["eb"] = _row(z["L1_ffn_expert_b"])
    o["l2a"] = cat(_cols(z["L2_attn_W_in"]), _cols(z["L2_attn_W_out"]))
    o["l2x"] = cat(_cols(z["L2_xattn_w_q"].T), _cols(z["L2_xattn_w_k"].T[:, krep]), _cols(z["L2_xattn_w_v"].T), _cols(z["L2_xattn_w_o"].T))
    o["l2f"] = cat(_cols(z["L2_ffn_w_gate"].T), _cols(z["L2_ffn_w_up"].T), _cols(z["L2_ffn_w_down"].T))
    o["l3a"] = cat(_cols(z["L3_attn_in_proj_w"].T), _cols(z["L3_attn_out_proj_w"].T))
    o["l3f"] = cat(_cols(z["L3_ffn_Wr"].T), _cols(z["L3_ffn_W1"].T), _cols(z["L3_ffn_W2"].T))
    o["m1"] = z["mask_BxS2_if1"].reshape(1, -1)
    o["m0"] = z["mask_BxS2_bk0"].reshape(1, -1).view(np.int32)
    return {n: np.ascontiguousarray(t) for n, t in o.items()}


def kernel(**inputs):
    import concourse.bacc as bacc
    from concourse.bass_utils import run_bass_kernel_spmd

    laid = _layout({k: np.asarray(t) for k, t in inputs.items()})
    nc = bacc.Bacc("TRN2", target_bir_lowering=False, num_devices=1)
    aps = {n: nc.dram_tensor(f"in_{n}", t.shape, mybir.dt.from_np(t.dtype), kind="ExternalInput").ap()
           for n, t in laid.items()}
    out = nc.dram_tensor("out_0", (NB, P, D), F32, kind="ExternalOutput").ap()
    build(nc, aps, out)
    r = run_bass_kernel_spmd(nc, [{f"in_{n}": t for n, t in laid.items()}], core_ids=[0])
    return r.results[0]["out_0"]
```

```python
from contextlib import ExitStack

import numpy as np
import concourse.bass as bass
from concourse import mybir

P = 128
NB = 8
D = 256
N = NB * P
G = 512
BANKS = 8
NEG = -1e30
LOW, IMM = -3.0e38, -3.3e38

ALU = mybir.AluOpType
ACT = mybir.ActivationFunctionType
AX = mybir.AxisListType
F32 = mybir.dt.float32
BF16 = mybir.dt.bfloat16

CST = dict(ident=128, tri=128, strict=128, ones=128, causal=128, cos1=128, sin1=128,
           cosx=128, sinx=128, nf=512, first=128, blk=4)
VEC = dict(bu=2, bv=2, bg1=1, bg2=2, cw0=6, cb0=2, w=2, u=2, rw0=64, qn=1, kn=1, qns=1, kns=1,
           cw2=24, cb2=6, nw2=4, cw3=48, cb3=12, gate_b=8, dt_bias=8, A_log=8, D2=8, D3=64,
           br=16, z_bias=4, b_o=256, eps5=1, eps6=1, one=1, zero=1)
W_L0A = dict(WuT=512, WvT=512, g1T=128, g2T=256)
W_EXP = dict(gate=192, up=192, down=256)
W_L1A = dict(q=512, qs=512, k=512, ks=512, v=128, o=512)
W_L1X = dict(q=4096, k=1024, v=1024, kc=1024, vc=1024, o=4096)
W_L1F = dict(gate=16, e=4096)
W_L2A = dict(inp=2 * 1288, out=1024)
W_L2X = dict(q=512, k=512, v=128, o=512)
W_L2F = dict(gate=2048, up=2048, down=2048)
W_L3A = dict(inp=2 * 2112, out=1024)
W_L3F = dict(r=32, w1=2048, w2=2048)
NE = 32
EI = 96
EXP_COLS = sum(W_EXP.values())
KV, XH = 4, 16
EXP_CHUNK = 4
EXP_SLOTS = 4
ARENA_A = 5632
ARENA_B = 12288
V_WINDOWS = sum(W_L1A.values())


def offsets(sizes):
    at, out = 0, {}
    for name, n in sizes.items():
        out[name] = (at, at + n)
        at += n
    return out, at


def plans():
    ln = [("ln", g, c) for g in range(2) for c in range(2)]
    out = [("o", bp) for bp in range(4)]
    p = {}
    p["pre"] = [("ctx", g, c) for g in range(2) for c in range(2)]
    p["l0a"] = ln + [("h", g) for g in range(2)] + \
        [(k, rc, g) for rc in range(2) for g in range(2) for k in ("gate", "u", "v")] + out
    p["l0x"] = ln + out
    l = list(ln) + [("r",)]
    for e in range(NE + 1):
        if e < NE:
            l += [(k, e, g) for g in range(2) for k in ("gate", "up")]
        if e >= 1:
            l += [("down", e - 1, bp) for bp in range(4)]
    p["l0f"] = l
    p["l1a"] = ln + [(k, c, g) for c in range(2) for g in range(2) for k in ("q", "qs", "k", "ks")] + \
        [("v",)] + heads_plan()
    l = list(ln)
    for t in range(-4, 35):
        w, r = t // 4 + 1, t % 4
        if 0 <= t < 32:
            l += [("s", t, 0), ("s", t, 1)]
        if w < 8:
            l += [[("k", w), ("kc", w), ("q", w, 0), ("q", w, 1)], [("k2", w), ("kc2", w), ("rq", w, 0)],
                  [("q", w, 2), ("q", w, 3)], [("rq", w, 1)]][r]
            if w % 4 == 0:
                l += [("v", w // 4, r), ("vc", w // 4, r)]
        if 1 <= t < 33:
            l += [("t", t - 1, 0), ("t", t - 1, 1)]
        if 2 <= t < 34:
            l += [("pv", t - 2)]
        if 3 <= t:
            l += [("o", t - 3)]
    p["l1x"] = l
    p["l1f"] = ln + [("r",)] + [("e", e, bp) for e in range(8) for bp in range(4)]
    l = ln + [("dt",)] + [("c", cc, g) for g in range(2) for cc in range(6)] + [("z", b) for b in range(NB)] + \
        [("x", b) for b in range(NB)]
    for b in range(NB + 1):
        if b < NB:
            l += [("seg", b, 0), ("seg", b, 1), ("cb", b)]
        if b >= 1:
            l += [("y", b - 1)]
    for b in range(NB + 1):
        if b < NB:
            l += [("yt", b)]
        if b >= 1:
            l += [("o", b - 1)]
    p["l2a"] = l
    p["l2x"] = ln + [(k, c, g) for c in range(2) for g in range(2) for k in ("q", "k")] + [("v",), ("mask", 0), ("mask", 1)] + heads_plan()
    l = [("ws",)] + [("qt", g, c) for g in range(2) for c in range(2)] + \
        [(k, b, h) for b in range(NB) for h in range(2) for k in ("gate", "up")]
    for b in range(NB + 1):
        if b < NB:
            l += [("ht", b)]
        if b >= 1:
            l += [("o", b - 1)]
    p["l2f"] = l
    l = ln + [("dt",)]
    for g in range(2):
        l += [("c", cc, g) for cc in range(12)] + [("z", 4 * g + i) for i in range(4)] + [("x", 4 * g + i) for i in range(4)]
        for t in range(18):
            if t < 16:
                if t % 4 == 0:
                    l += [("cb", g, t // 4, 0), ("cb", g, t // 4, 1)]
                l += [("seg", g, u, hh) for u in (2 * t, 2 * t + 1) for hh in range(2)]
            if 1 <= t < 17:
                l += [("y", g, t - 1)]
            if t >= 5 and (t - 5) % 4 == 0:
                l += [("o", 4 * g + (t - 5) // 4)]
    p["l3a"] = l
    p["l3x"] = ln + [("val",), ("s", 0), ("s", 1), ("t", 0), ("t", 1)] + out
    p["l3f"] = ln + [("r",), ("mt",)] + [(k, m, g) for m in range(8) for g in range(2) for k in ("h", "m")] + \
        [("o", bp) for bp in range(4)]
    return p


def heads_plan():
    l = []
    for u in range(NB * 8 + 4):
        if u < NB * 8:
            l += [("s", u)]
        if 2 <= u < NB * 8 + 2:
            l += [("t", u - 2)]
        if u >= 7 and (u - 7) % 4 == 0:
            l += [("pv", (u - 7) // 4)]
        if u >= 20 and (u - 20) % 16 == 0:
            l += [("o", (u - 20) // 16)]
    return l + [("o", 3)]


def build(nc, a, out):
    plan = plans()
    job_of, at = {}, 0
    for layer, keys in plan.items():
        for key in keys:
            job_of[(layer,) + key] = at
            at += 1

    with ExitStack() as ctx:
        def sb(name, cols, dt=F32):
            return ctx.enter_context(nc.sbuf_tensor(name, [P, cols], dt))

        def sem(name):
            return ctx.enter_context(nc.semaphore(name))

        cst_at, ncst = offsets(CST)
        vec_at, nvec = offsets(VEC)
        cst_t, vec_t = sb("cst", ncst), sb("vec", nvec)
        X = sb("X", NB * D)
        XN = sb("XN", NB * D)
        XT = sb("XT", 2 * N)
        C = sb("C", NB * D)
        CT = sb("CT", 2 * N)
        WA, WB = sb("WA", ARENA_A), sb("WB", ARENA_B)
        identb, causalb, onesb = sb("identb", P, BF16), sb("causalb", 4 * P, BF16), sb("onesb", P, BF16)
        small = sb("small", 832)
        WORK = 18432
        work = sb("work", WORK)
        PS = ctx.enter_context(nc.psum_tensor("PS", [P, BANKS * G], F32))

        def cst(name, p0=0, p1=P):
            return cst_t[p0:p1, slice(*cst_at[name])]

        def vec(name, i=None, n=1, p0=0, p1=P):
            lo, hi = vec_at[name]
            return vec_t[p0:p1, lo:hi] if i is None else vec_t[p0:p1, lo + i:lo + i + n]

        mk1 = ctx.enter_context(nc.sbuf_tensor("mk1", [1, N], mybir.dt.int32))
        mk0 = ctx.enter_context(nc.sbuf_tensor("mk0", [1, N // 4], mybir.dt.int32))
        pad1 = ctx.enter_context(nc.sbuf_tensor("pad1", [P, N], BF16))
        pad0 = ctx.enter_context(nc.sbuf_tensor("pad0", [P, N], BF16))
        valid = ctx.enter_context(nc.sbuf_tensor("valid", [1, NB], F32))

        bank_full = [sem(f"bank_full{i}") for i in range(BANKS)]
        bank_free = [sem(f"bank_free{i}") for i in range(BANKS)]
        cst_in, x_in, ctx_in = sem("cst_in"), sem("x_in"), sem("ctx_in")
        windows_zero = sem("windows_zero")
        expert_b, eb_in = WB[:, 8192:8192 + 8 * D], sem("eb_in")
        wa_in, wb_in = sem("wa_in"), sem("wb_in")
        exp_in = [sem(f"exp_in{i}") for i in range(EXP_SLOTS)]
        y_out = sem("y_out")
        x_final = sem("x_final")

        class Handoff:
            def __init__(self, name):
                self.sem, self.given, self.taken = sem(name), 0, 0

            def give(self):
                self.given += 1
                return 1

            def next(self):
                self.taken += 1
                return self.taken

        act_to_pe, dve_to_pe = Handoff("act_to_pe"), Handoff("dve_to_pe")
        act_to_dve, dve_to_act = Handoff("act_to_dve"), Handoff("dve_to_act")
        decay_steps, decayed_scores, gated_y = Handoff("decay_steps"), Handoff("decayed_scores"), Handoff("gated_y")

        def stepper(name):
            own, latest = Handoff(name), []

            def step(to=own):
                if isinstance(to, int):
                    latest[:] = [bank_free[to % BANKS], to // BANKS + 1]
                else:
                    to.give()
                    latest[:] = [to.sem, to.given]
                return latest[0], 1

            return step, lambda: tuple(latest)

        dve_step, dve_last = stepper("dve_own")
        act_step, act_last = stepper("act_own")

        def bank(j, rows=P, cols=G):
            return PS[0:rows, (j % BANKS) * G:(j % BANKS) * G + cols]

        def full(j):
            return bank_full[j % BANKS], j // BANKS + 1

        def freed(j):
            return bank_free[j % BANKS], j // BANKS + 1

        block = ctx.enter_context(nc.Block())

        def r3(ap, b):
            return ap.rearrange("p (a b) -> p a b", b=b)

        def xt(c, lo, hi, T=None):
            return (T or XT)[:, c * N + lo:c * N + hi]

        sm = lambda lo, n: small[:, lo:lo + n]

        def W(arena, sizes, name, lo=0, hi=None, p1=P, base=0):
            a0, a1 = offsets(sizes)[0][name]
            hi = a1 - a0 if hi is None else hi
            return arena[0:p1, base + a0 + lo:base + a0 + hi]

        def wk(lo, n, p0=0, p1=P):
            return work[p0:p1, lo:lo + n]

        def wkb(lo, n, p0=0, p1=P):
            return work[p0:p1, lo:lo + n // 2].bitcast(BF16)

        def ew(e, name, lo, hi, p1=P):
            return W(WB, W_EXP, name, lo, hi, p1, base=(e % (EXP_CHUNK * EXP_SLOTS)) * EXP_COLS)

        v_windows, ones_window = WA[:, V_WINDOWS:V_WINDOWS + 2072], WA[:, V_WINDOWS + 2072:V_WINDOWS + 2128]

        masks = WA[:, V_WINDOWS + 2128:V_WINDOWS + 2128 + N // 2].bitcast(BF16)

        def l3a_x(i):
            return wk(6144, 2048) if i == 3 else WB[:, 4128 + i * 2048:4128 + (i + 1) * 2048]

        def l1x_p(u):
            return wk(16384, 1024) if u % 2 == 0 else XN[:, 0:1024]

        def l1x_pt(u):
            return wk(17408, 1024) if u % 2 == 0 else XN[:, 1024:2048]

        def l1x_q(w, hh):
            return wk((w % 2) * 2048 + hh * G, G)

        def l1x_sq(i):
            return wk(4096 + i * G, G)

        def l1x_k(w, kc):
            return r3(wk(8192 + (w % 2) * 1024, 1024), D)[:, :, kc * P:(kc + 1) * P]

        def l1x_v(g, i, kc):
            return wk((12288 + i * 1024 if g == 0 else 6144 + i * 1024 if i < 2 else 8192 + i * 1024) + kc * G, G)

        l1x_root = [WA[:, 4400:4400 + G], C[:, 3 * G:4 * G]]

        @block.sync
        def _(sp):
            J = lambda *k: job_of[k]
            last = lambda layer: job_of[(layer,) + plan[layer][-1]]
            sp.dma_start(r3(X[:, :], D), a["x"].rearrange("b t d -> t b d")).then_inc(x_in, 16)
            sp.dma_start(cst_t[:, :], a["cst"]).then_inc(cst_in, 16)
            sp.dma_start(vec_t[:, :], a["vec"]).then_inc(cst_in, 16)
            sp.dma_start(r3(C[:, :], D), a["ctx"].rearrange("b t d -> t b d")).then_inc(ctx_in, 16)

            def load(arena, name, s):
                sp.dma_start(arena[:, 0:a[name].shape[1]], a[name]).then_inc(s, 16)

            def experts(c):
                s = c % EXP_SLOTS
                n = EXP_CHUNK * EXP_COLS
                sp.dma_start(WB[:, s * n:(s + 1) * n], a["l0f"][:, c * n:(c + 1) * n]).then_inc(exp_in[s], 16)

            sp.dma_start(mk1[:, :], a["m1"]).then_inc(cst_in, 16)
            sp.dma_start(mk0[:, :], a["m0"]).then_inc(cst_in, 16)
            load(WA, "l0a", wa_in)
            for c in range(EXP_SLOTS):
                experts(c)
            for c in range(EXP_SLOTS, NE // EXP_CHUNK):
                sp.wait_ge(*full(J("l0f", "down", (c - EXP_SLOTS + 1) * EXP_CHUNK - 1, 3)))
                experts(c)
                if c == EXP_SLOTS:
                    load(WA, "l1a", wa_in)
            sp.wait_ge(*full(last("l0f")))
            load(WB, "l1x", wb_in)
            sp.wait_ge(*full(last("l1a")))
            load(WA, "l1f", wa_in)
            sp.wait_ge(*full(last("l1x")))
            sp.dma_start(expert_b, a["eb"]).then_inc(eb_in, 16)
            load(WB, "l2a", wb_in)
            sp.dma_start(r3(C[:, :], D), a["ctx"].rearrange("b t d -> t b d")).then_inc(ctx_in, 16)
            for layer, free_by, arena, s in (("l2x", "l1f", WA, wa_in), ("l2f", "l2a", WB, wb_in),
                                             ("l3a", "l2x", WA, wa_in), ("l3f", "l2f", WB, wb_in)):
                sp.wait_ge(*full(last(free_by)))
                load(arena, layer, s)
            sp.wait_ge(x_final, 1)
            sp.dma_start(out.rearrange("b t d -> t b d"), r3(X[:, :], D)).then_inc(y_out, 16)
            sp.wait_ge(y_out, 16)

        @block.gpsimd
        def _(pool):
            both = WA[:, V_WINDOWS:V_WINDOWS + 2072 + 56]
            nc.gpsimd.memset(both, 0.0).then_inc(windows_zero, 1)
            pool.wait_ge(*full(job_of[("l1f",) + plan["l1f"][-1]]))
            nc.gpsimd.memset(both, 0.0).then_inc(windows_zero, 1)
            pool.wait_ge(*freed(job_of[("l2f",) + plan["l2f"][-1]]))
            for i in range(4):
                nc.gpsimd.memset(l3a_x(i), 0.0).then_inc(windows_zero, 1)

        @block.tensor
        def _(pe):
            opened = [0]

            def begin(*key):
                j = opened[0]
                assert job_of[key] == j, (key, job_of[key], j)
                if j >= BANKS:
                    pe.wait_ge(bank_free[j % BANKS], j // BANKS)
                return bank(j)

            def end(ins):
                ins.then_inc(bank_full[opened[0] % BANKS], 1)
                opened[0] += 1

            mm = lambda o, l, r, s, e: nc.tensor.matmul(o, l, r, start=s, stop=e)
            J = lambda *k: job_of[k]

            def transposes(layer, tag, source, ready):
                for g in range(2):
                    for c in range(2):
                        o = begin(layer, tag, g, c)
                        for i in range(4):
                            b = 4 * g + i
                            if ready and c == 0:
                                pe.wait_ge(dve_to_pe.sem, dve_to_pe.next())
                            ins = nc.tensor.transpose(o[:, i * P:(i + 1) * P],
                                                      source[:, b * D + c * P:b * D + (c + 1) * P], cst("ident"))
                        end(ins)

            def ln(layer):
                transposes(layer, "ln", XN, True)

            def need_xt(layer, g):
                pe.wait_ge(*freed(J(layer, "ln", g, 0)))
                pe.wait_ge(*freed(J(layer, "ln", g, 1)))

            def from_xt(o, cols, g, w, T=None):
                for c in range(2):
                    ins = mm(o, w(c), xt(c, g * G, (g + 1) * G, T), c == 0, c == 1)
                return ins

            pe.wait_ge(cst_in, 64)
            pe.wait_ge(ctx_in, 16)
            transposes("pre", "ctx", C, False)

            def heads(layer, wo, pad):
                kbd = r3(wk(0, 8 * N), N)
                for key in heads_plan():
                    o = begin(layer, *key)
                    if key[0] == "s":
                        b, kv = key[1] // 8, key[1] % 8
                        c, r = kv // 4, 32 * (kv % 4)
                        if pad is None:
                            mm(o, identb[:, :], causalb[:, :], True, False)
                        else:
                            mm(r3(o, P), identb[:, :], pad[:, b * P:(b + 1) * P].unsqueeze(1).to_broadcast([P, 4, P]), True, False)
                        end(mm(r3(o, P), XN[r:r + 32, c * N + b * P:c * N + (b + 1) * P],
                               kbd[r:r + 32, 4 * c:4 * c + 4, b * P:(b + 1) * P], False, True))
                    elif key[0] == "t":
                        pe.wait_ge(act_to_pe.sem, act_to_pe.next())
                        for i in range(4):
                            ins = nc.tensor.transpose(o[:, i * P:(i + 1) * P],
                                                      wk(16384 + (key[1] % 3) * G + i * P, P), cst("ident"))
                        end(ins)
                    elif key[0] == "pv":
                        x = key[1]
                        pe.wait_ge(*freed(J(layer, "t", 4 * x + 3)))
                        for part in range(2):
                            for k in range(4):
                                u = 4 * x + k
                                for h in range(4):
                                    window = v_windows[:, u * 32 + 24 - 8 * h:u * 32 + 56 - 8 * h] if part == 0 else ones_window[:, 24 - 8 * h:56 - 8 * h]
                                    ins = mm(o[32 * k:32 * k + 32, part * P:(part + 1) * P], window,
                                             wk(8192 + (u % 16) * G + h * P, P), h == 0, h == 3)
                        end(ins)
                    else:
                        bp = key[1]
                        for x in range(4):
                            pe.wait_ge(*freed(J(layer, "pv", 4 * bp + x)))
                        for i in range(2):
                            for c in range(2):
                                lo = (bp % 2) * G + (2 * i + c) * P
                                ins = mm(o[:, i * D:(i + 1) * D], XT[:, lo:lo + P],
                                         wo[:, c * D:(c + 1) * D], c == 0, c == 1)
                        end(ins)

            def values(layer, wv, T):
                o = begin(layer, "v")
                for b in range(NB):
                    for c in range(2):
                        ins = mm(o[:, b * 64:(b + 1) * 64], xt(c, b * P, (b + 1) * P, T), wv[:, c * 64:(c + 1) * 64], c == 0, c == 1)
                end(ins)

            ln("l0a")
            pe.wait_ge(wa_in, 16)
            w = lambda n, *k, **kw: W(WA, W_L0A, n, *k, **kw)
            for g in range(2):
                o = begin("l0a", "h", g)
                need_xt("l0a", g)
                end(from_xt(o[0:64, :], 64, g, lambda c: w("g1T", c * 64, c * 64 + 64)))
            for rc in range(2):
                for g in range(2):
                    o = begin("l0a", "gate", rc, g)
                    pe.wait_ge(*freed(J("l0a", "h", g)))
                    end(mm(o, w("g2T", rc * P, rc * P + P, p1=64), wk(0 + g * G, G, 0, 64), True, True))
                    for n in ("u", "v"):
                        o = begin("l0a", n, rc, g)
                        end(from_xt(o, P, g, lambda c: w("WuT" if n == "u" else "WvT", c * D + rc * P, c * D + rc * P + P)))
            for bp in range(4):
                o = begin("l0a", "o", bp)
                if bp == 0:
                    pe.wait_ge(dve_to_pe.sem, dve_to_pe.next())
                for i in range(2):
                    b = 2 * bp + i
                    oo = o[:, i * D:(i + 1) * D]
                    for rc in range(2):
                        mm(oo, wk(5120 + rc * N + b * P, P), w("WuT", rc * D, rc * D + D), rc == 0, False)
                    for c in range(2):
                        ins = mm(oo[:, c * P:(c + 1) * P], wk(7168 + c * N + b * P, P), cst("ident"), False, c == 1)
                end(ins)

            ln("l0x")
            for bp in range(4):
                o = begin("l0x", "o", bp)
                if bp == 0:
                    pe.wait_ge(dve_to_pe.sem, dve_to_pe.next())
                for i in range(2):
                    for c in range(2):
                        b = 2 * bp + i
                        ins = nc.tensor.transpose(o[:, i * D + c * P:i * D + (c + 1) * P],
                                                  wk(c * N + b * P, P), cst("ident"))
                end(ins)

            ln("l0f")
            o = begin("l0f", "r")
            pe.wait_ge(cst_in, 64)
            need_xt("l0f", 0)
            need_xt("l0f", 1)
            for b in range(NB):
                for c in range(2):
                    ins = mm(o[:, b * NE:(b + 1) * NE], xt(c, b * P, (b + 1) * P), vec("rw0", c * NE, NE), c == 0, c == 1)
            end(ins)
            for e in range(NE + 1):
                if e < NE:
                    ch = e // EXP_CHUNK
                    if e % EXP_CHUNK == 0:
                        pe.wait_ge(exp_in[ch % EXP_SLOTS], 16 * (ch // EXP_SLOTS + 1))
                    for g in range(2):
                        for n in ("gate", "up"):
                            o = begin("l0f", n, e, g)
                            end(from_xt(o[0:EI, :], EI, g, lambda c: ew(e, n, c * EI, (c + 1) * EI)))
                if e >= 1:
                    f = e - 1
                    for bp in range(4):
                        o = begin("l0f", "down", f, bp)
                        pe.wait_ge(*freed(J("l0f", "up", f, bp // 2)))
                        for i in range(2):
                            b = 2 * bp + i
                            ins = mm(o[:, i * D:(i + 1) * D], wk((f % 2) * N + b * P, P, 0, EI),
                                     ew(f, "down", 0, D, EI), True, True)
                        end(ins)

            ln("l1a")
            pe.wait_ge(wa_in, 32)
            w1 = lambda n, *k, **kw: W(WA, W_L1A, n, *k, **kw)
            for c in range(2):
                for g in range(2):
                    for n in ("q", "qs", "k", "ks"):
                        o = begin("l1a", n, c, g)
                        need_xt("l1a", g)
                        end(from_xt(o, P, g, lambda cc: w1(n, cc * D + c * P, cc * D + c * P + P)))
            values("l1a", w1("v"), XT)
            pe.wait_ge(act_to_pe.sem, act_to_pe.next())
            pe.wait_ge(act_to_pe.sem, act_to_pe.next())
            heads("l1a", w1("o"), None)

            ln("l1x")
            pe.wait_ge(wb_in, 16)
            wx = lambda n, *k, **kw: W(WB, W_L1X, n, *k, **kw)
            for t in range(-4, 35):
                w, r = t // 4 + 1, t % 4
                if 0 <= t < 32:
                    if r == 0:
                        pe.wait_ge(dve_to_pe.sem, dve_to_pe.next())
                    for s_ in range(2):
                        o = begin("l1x", "s", t, s_)
                        for i in range(2):
                            mm(o[:, i * D:(i + 1) * D], l1x_q(t // 4, 2 * s_ + i)[:, r * P:(r + 1) * P],
                               wk(8192 + (t // 4 % 2) * 1024 + r * D, D), True, False)
                            ins = mm(o[:, i * D + P:(i + 1) * D], identb[:, :], causalb[:, 0:P], False, True)
                        end(ins)
                if w < 8:
                    g, kv = w // 4, w % 4
                    if kv == 0 and r == 0:
                        need_xt("l1x", g)
                    if r == 0:
                        for n, T in (("k", XT), ("kc", CT)):
                            o = begin("l1x", n, w)
                            end(from_xt(o, P, g, lambda c: wx(n, c * G + kv * P, c * G + kv * P + P), T))
                    if r == 1:
                        for i, n in enumerate(("k", "kc")):
                            o = begin("l1x", n + "2", w)
                            pe.wait_ge(*freed(J("l1x", n, w)))
                            end(mm(o, cst("ones"), l1x_sq(i), True, True))
                    for hh in ((0, 1), (), (2, 3), ())[r]:
                        o = begin("l1x", "q", w, hh)
                        h = 4 * kv + hh
                        end(from_xt(o, P, g, lambda c: wx("q", c * 2048 + h * P, c * 2048 + h * P + P)))
                    if r % 2 == 1:
                        o = begin("l1x", "rq", w, r // 2)
                        for i in range(2):
                            pe.wait_ge(*freed(J("l1x", "q", w, 2 * (r // 2) + i)))
                            for b in range(4):
                                ins = mm(o[:, b * 2 + i:b * 2 + i + 1], l1x_sq(2 + i)[:, b * P:(b + 1) * P],
                                         cst("ones")[:, 0:1], True, True)
                        end(ins)
                    if kv == 0:
                        b = 4 * g + r
                        for n, T in (("v", XT), ("vc", CT)):
                            o = begin("l1x", n, g, r)
                            for c in range(2):
                                ins = mm(o, xt(c, b * P, (b + 1) * P, T), wx(n, c * G, c * G + G), c == 0, c == 1)
                            end(ins)
                if 1 <= t < 33:
                    x = t - 1
                    pe.wait_ge(dve_to_pe.sem, dve_to_pe.next())
                    for kc in range(2):
                        o = begin("l1x", "t", x, kc)
                        for j in range(4):
                            ins = nc.tensor.transpose(o[:, j * P:(j + 1) * P],
                                                      l1x_p(x)[:, j * D + kc * P:j * D + (kc + 1) * P], cst("ident"))
                        end(ins)
                if 2 <= t < 34:
                    x = t - 2
                    g, kv, b = x // 16, x // 4 % 4, x % 4
                    o = begin("l1x", "pv", x)
                    if kv == 0:
                        pe.wait_ge(*freed(J("l1x", "v", g, b)))
                        pe.wait_ge(*freed(J("l1x", "vc", g, b)))
                    for kc in range(2):
                        pe.wait_ge(*freed(J("l1x", "t", x, kc)))
                        ins = mm(o, l1x_v(g, b, kc)[:, kv * P:(kv + 1) * P], l1x_pt(x)[:, kc * G:(kc + 1) * G], kc == 0, kc == 1)
                    end(ins)
                if 3 <= t:
                    x = t - 3
                    o = begin("l1x", "o", x)
                    pe.wait_ge(*freed(J("l1x", "pv", x)))
                    for hh in range(4):
                        h = 4 * (x // 4 % 4) + hh
                        ins = mm(o[:, 0:D], C[:, (x % 3) * G + hh * P:(x % 3) * G + (hh + 1) * P],
                                 wx("o", h * D, h * D + D), hh == 0, hh == 3)
                    end(ins)

            ln("l1f")
            pe.wait_ge(wa_in, 48)
            wf_ = lambda n, *k, **kw: W(WA, W_L1F, n, *k, **kw)
            o = begin("l1f", "r")
            need_xt("l1f", 0)
            need_xt("l1f", 1)
            for b in range(NB):
                for c in range(2):
                    ins = mm(o[:, b * 8:(b + 1) * 8], xt(c, b * P, (b + 1) * P), wf_("gate", c * 8, c * 8 + 8), c == 0, c == 1)
            end(ins)
            for e in range(8):
                for bp in range(4):
                    o = begin("l1f", "e", e, bp)
                    for i in range(2):
                        b = 2 * bp + i
                        for c in range(2):
                            ins = mm(o[:, i * D:(i + 1) * D], xt(c, b * P, (b + 1) * P),
                                     wf_("e", (2 * e + c) * D, (2 * e + c) * D + D), c == 0, c == 1)
                    end(ins)

            def project(layer, n, wt_, stride, lo, rows, b):
                o = begin(layer, n, b)
                for c in range(2):
                    ins = mm(o, xt(c, b * P, (b + 1) * P), wt_[:, c * stride + lo:c * stride + lo + rows], c == 0, c == 1)
                end(ins)

            ln("l2a")
            pe.wait_ge(wb_in, 32)
            wi, wo = W(WB, W_L2A, "inp"), W(WB, W_L2A, "out")
            o = begin("l2a", "dt")
            need_xt("l2a", 0)
            need_xt("l2a", 1)
            for b in range(NB):
                for c in range(2):
                    ins = mm(o[:, b * 8:(b + 1) * 8], xt(c, b * P, (b + 1) * P), wi[:, c * 1288 + 1280:c * 1288 + 1288], c == 0, c == 1)
            end(ins)
            for g in range(2):
                for cc in range(6):
                    o = begin("l2a", "c", cc, g)
                    end(from_xt(o, P, g, lambda c: wi[:, c * 1288 + 512 + cc * P:c * 1288 + 512 + (cc + 1) * P]))
            for b in range(NB):
                project("l2a", "z", wi, 1288, 0, 512, b)
            for b in range(NB):
                o = begin("l2a", "x", b)
                if b % 4 == 0:
                    pe.wait_ge(act_to_pe.sem, act_to_pe.next())
                for cc in range(4):
                    ins = nc.tensor.transpose(o[:, cc * P:(cc + 1) * P], wk(cc * N + b * P, P), cst("ident"))
                end(ins)
            for b in range(NB + 1):
                if b < NB:
                    pe.wait_ge(decay_steps.sem, decay_steps.next())
                    for hh in range(2):
                        o = begin("l2a", "seg", b, hh)
                        end(mm(o, cst("strict"), XN[:, (b % 2) * 1024 + hh * G:(b % 2) * 1024 + (hh + 1) * G], True, True))
                    o = begin("l2a", "cb", b)
                    end(mm(o[:, 0:P], wk(4 * N + b * P, P), wk(5 * N + b * P, P), True, True))
                if b >= 1:
                    x = b - 1
                    pe.wait_ge(decayed_scores.sem, decayed_scores.next())
                    o = begin("l2a", "y", x)
                    for h in range(8):
                        ins = mm(o[:, h * 64:(h + 1) * 64], wk(14336 + (x % 2) * 1024 + h * P, P),
                                 wk(16384 + (x % 2) * G + h * 64, 64), True, True)
                    end(ins)
            for b in range(NB + 1):
                if b < NB:
                    pe.wait_ge(gated_y.sem, gated_y.next())
                    o = begin("l2a", "yt", b)
                    for cc in range(4):
                        ins = nc.tensor.transpose(o[:, cc * P:(cc + 1) * P], wk(10240 + b * G + cc * P, P), cst("ident"))
                    end(ins)
                if b >= 1:
                    o = begin("l2a", "o", b - 1)
                    pe.wait_ge(*freed(J("l2a", "yt", b - 1)))
                    for cc in range(4):
                        ins = mm(o[:, 0:D], XT[:, ((b - 1) % 4) * G + cc * P:((b - 1) % 4) * G + (cc + 1) * P],
                                 wo[:, cc * D:(cc + 1) * D], cc == 0, cc == 3)
                    end(ins)

            ln("l2x")
            pe.wait_ge(wa_in, 64)
            w2 = lambda n, *k, **kw: W(WA, W_L2X, n, *k, **kw)
            for c in range(2):
                for g in range(2):
                    need_xt("l2x", g)
                    for n, T in (("q", XT), ("k", CT)):
                        o = begin("l2x", n, c, g)
                        end(from_xt(o, P, g, lambda cc: w2(n, cc * D + c * P, cc * D + c * P + P), T))
            values("l2x", w2("v"), CT)
            pe.wait_ge(act_to_pe.sem, act_to_pe.next())
            pe.wait_ge(act_to_pe.sem, act_to_pe.next())
            for g in range(2):
                o = begin("l2x", "mask", g)
                for i in range(4):
                    ins = mm(o[:, i * P:(i + 1) * P], onesb[:, :], pad1[:, (4 * g + i) * P:(4 * g + i + 1) * P], True, True)
                end(ins)
            for g in range(2):
                pe.wait_ge(*freed(J("l2x", "mask", g)))
            heads("l2x", w2("o"), masks)

            o = begin("l2f", "ws")
            pe.wait_ge(act_to_pe.sem, act_to_pe.next())
            end(mm(o[:, 0:3], cst("ones"), sm(128, 3), True, True))
            for _ in range(NB):
                pe.wait_ge(dve_to_pe.sem, dve_to_pe.next())
            pe.wait_ge(dve_to_pe.sem, dve_to_pe.next())
            for g in range(2):
                for c in range(2):
                    o = begin("l2f", "qt", g, c).bitcast(BF16)
                    for i in range(4):
                        b = 4 * g + i
                        ins = nc.tensor.transpose(o[:, i * P:(i + 1) * P],
                                                  wkb(8192, 2048)[:, b * D + c * P:b * D + (c + 1) * P], identb[:, :])
                    end(ins)
            pe.wait_ge(dve_to_pe.sem, dve_to_pe.next())
            wq = wkb(11264, 6144)
            for b in range(NB):
                for h in range(2):
                    for i, n in enumerate(("gate", "up")):
                        o = begin("l2f", n, b, h)
                        for c in range(2):
                            pe.wait_ge(*freed(J("l2f", "qt", b // 4, c)))
                            ins = mm(o, wkb(9216, 2048)[:, c * N + b * P:c * N + (b + 1) * P],
                                     wq[:, i * 2048 + c * 1024 + h * G:i * 2048 + c * 1024 + (h + 1) * G], c == 0, c == 1)
                        end(ins)
            for b in range(NB + 1):
                if b < NB:
                    pe.wait_ge(dve_to_pe.sem, dve_to_pe.next())
                    o = begin("l2f", "ht", b).bitcast(BF16)
                    for m in range(8):
                        ins = nc.tensor.transpose(o[:, m * P:(m + 1) * P], wkb(14336, 8192)[:, b * 1024 + m * P:b * 1024 + (m + 1) * P],
                                                  identb[:, :])
                    end(ins)
                if b >= 1:
                    o = begin("l2f", "o", b - 1)
                    pe.wait_ge(*freed(J("l2f", "ht", b - 1)))
                    ht = XT[:, :].bitcast(BF16)
                    for m in range(8):
                        ins = mm(o[:, 0:D], ht[:, ((b - 1) % 4) * 1024 + m * P:((b - 1) % 4) * 1024 + (m + 1) * P],
                                 wq[:, 4096 + m * D:4096 + (m + 1) * D], m == 0, m == 7)
                    end(ins)

            ln("l3a")
            pe.wait_ge(wa_in, 80)
            wi, wo = W(WA, W_L3A, "inp"), W(WA, W_L3A, "out")
            o = begin("l3a", "dt")
            need_xt("l3a", 0)
            need_xt("l3a", 1)
            for b in range(NB):
                for c in range(2):
                    ins = mm(o[:, b * 64:(b + 1) * 64], xt(c, b * P, (b + 1) * P), wi[:, c * 2112 + 2048:c * 2112 + 2112], c == 0, c == 1)
            end(ins)
            for g in range(2):
                for cc in range(12):
                    o = begin("l3a", "c", cc, g)
                    end(from_xt(o, P, g, lambda c: wi[:, c * 2112 + cc * P:c * 2112 + (cc + 1) * P]))
                for cc in range(4):
                    o = begin("l3a", "z", 4 * g + cc)
                    end(from_xt(o, P, g, lambda c: wi[:, c * 2112 + 1536 + cc * P:c * 2112 + 1536 + (cc + 1) * P]))
                pe.wait_ge(act_to_pe.sem, act_to_pe.next())
                for i in range(4):
                    o = begin("l3a", "x", 4 * g + i)
                    for cc in range(4):
                        ins = nc.tensor.transpose(o[:, cc * P:(cc + 1) * P], wk(cc * G + i * P, P), cst("ident"))
                    end(ins)

                for t in range(18):
                    if t < 16:
                        i = t // 4
                        for par in range(2 if t % 4 == 0 else 0):
                            o = begin("l3a", "cb", g, i, par)
                            for m in range(4):
                                src = lambda part: work[64 * par:64 * par + 64, (part + m) * G + i * P:(part + m) * G + (i + 1) * P]
                                ins = mm(o[:, m * P:(m + 1) * P], src(4), src(8), True, True)
                            end(ins)
                        for u in (2 * t, 2 * t + 1):
                            pe.wait_ge(decay_steps.sem, decay_steps.next())
                            for hh in range(2):
                                o = begin("l3a", "seg", g, u, hh)
                                end(mm(o, cst("strict"), XN[:, (u % 2) * 1024 + hh * G:(u % 2) * 1024 + (hh + 1) * G], True, True))
                    if 1 <= t < 17:
                        i, cc = (t - 1) // 4, (t - 1) % 4
                        if t == 1:
                            pe.wait_ge(dve_to_pe.sem, dve_to_pe.next())
                            pe.wait_ge(*freed(J("l3a", "x", 4 * g + 3)))
                        o = begin("l3a", "y", g, t - 1)
                        mm(o[:, 0:P], wk(i * G + cc * P, P), cst("ident"), True, False)
                        for x in (2 * t - 2, 2 * t - 1):
                            pe.wait_ge(decayed_scores.sem, decayed_scores.next())
                            for h in range(8):
                                q = 32 * (2 * (x % 2) + h // 4)
                                ins = mm(o[q:q + 32, 0:P], l3a_x(i)[:, ((x % 8) * 8 + h) * 32:((x % 8) * 8 + h + 1) * 32],
                                         wk(10240 + (x % 4) * 1024 + h * P, P), False, h % 4 == 3)
                        end(ins)
                    if t >= 5 and (t - 5) % 4 == 0:
                        i = (t - 5) // 4
                        b = 4 * g + i
                        o = begin("l3a", "o", b)
                        for cc in range(4):
                            pe.wait_ge(*freed(J("l3a", "y", g, 4 * i + cc)))
                            ins = mm(o[:, 0:D], wk(17408 + (b % 2) * G + cc * P, P), wo[:, cc * D:(cc + 1) * D], cc == 0, cc == 3)
                        end(ins)

            ln("l3x")
            o = begin("l3x", "val")
            end(mm(o[:, 0:NB], cst("ones", 0, 1), valid[:, :], True, True))
            for g in range(2):
                o = begin("l3x", "s", g)
                need_xt("l3x", g)
                for i in range(4):
                    b = 4 * g + i
                    oo = o[:, i * P:(i + 1) * P]
                    for c in range(2):
                        mm(oo, xt(c, b * P, (b + 1) * P), xt(c, b * P, (b + 1) * P, CT), c == 0, False)
                    ins = mm(oo, onesb[:, :], pad0[:, b * P:(b + 1) * P], False, True)
                end(ins)
            pe.wait_ge(ctx_in, 32)
            for g in range(2):
                pe.wait_ge(act_to_pe.sem, act_to_pe.next())
                o = begin("l3x", "t", g)
                for i in range(4):
                    ins = nc.tensor.transpose(o[:, i * P:(i + 1) * P], wk(g * G + i * P, P), cst("ident"))
                end(ins)
            for bp in range(4):
                o = begin("l3x", "o", bp)
                pe.wait_ge(*freed(J("l3x", "t", bp // 2)))
                for i in range(2):
                    b = 2 * bp + i
                    ins = mm(o[:, i * D:(i + 1) * D], wk(1024 + b * P, P), C[:, b * D:(b + 1) * D], True, True)
                end(ins)

            ln("l3f")
            pe.wait_ge(wb_in, 64)
            w3 = lambda n, *k, **kw: W(WB, W_L3F, n, *k, **kw)
            o = begin("l3f", "r")
            need_xt("l3f", 0)
            need_xt("l3f", 1)
            for b in range(NB):
                for c in range(2):
                    ins = mm(o[:, b * 16:(b + 1) * 16], xt(c, b * P, (b + 1) * P), w3("r", c * 16, c * 16 + 16), c == 0, c == 1)
            end(ins)
            o = begin("l3f", "mt").bitcast(BF16)
            pe.wait_ge(dve_to_pe.sem, dve_to_pe.next())
            for b in range(NB):
                ins = nc.tensor.transpose(o[0:16, b * P:(b + 1) * P], wkb(8192, 128)[:, b * 16:(b + 1) * 16], identb[:, :])
            end(ins)
            for m in range(8):
                for g in range(2):
                    o = begin("l3f", "h", m, g)
                    end(from_xt(o, P, g, lambda c: w3("w1", c * 1024 + m * P, c * 1024 + m * P + P)))
                    o = begin("l3f", "m", m, g)
                    pe.wait_ge(*freed(J("l3f", "mt")))
                    end(mm(o, wkb(8768, 1024, 0, 16)[:, 2 * m * 64:(2 * m + 2) * 64], wkb(8256, 1024, 0, 16)[:, g * G:(g + 1) * G], True, True))
            for bp in range(4):
                o = begin("l3f", "o", bp)
                for i in range(2):
                    b = 2 * bp + i
                    for m in range(8):
                        pe.wait_ge(*freed(J("l3f", "m", m, b // 4)))
                        ins = mm(o[:, i * D:(i + 1) * D], wk(m * N + b * P, P), w3("w2", m * D, m * D + D), m == 0, m == 7)
                end(ins)

        @block.scalar
        def _(act):
            J = lambda *k: job_of[k]
            f = nc.scalar.activation

            def evac(layer, tag, T, *to):
                for g in range(2):
                    for c in range(2):
                        j = J(layer, tag, g, c)
                        act.wait_ge(*full(j))
                        f(xt(c, g * G, (g + 1) * G, T), bank(j), ACT.Copy).then_inc(*act_step(j))

            def ln(layer, *to):
                for g in range(2):
                    act.wait_ge(dve_to_act.sem, dve_to_act.next())
                    f(sm(80 + 4 * g, 4), sm(64 + 8 * g, 8).rearrange("p (b s) -> p b s", s=2)[:, :, 1], ACT.Sqrt,
                      bias=vec("eps5")).then_inc(*act_step(act_to_dve))
                evac(layer, "ln", XT, *to)

            act.wait_ge(cst_in, 64)
            evac("pre", "ctx", CT)

            ln("l0a")
            for g in range(2):
                j = J("l0a", "h", g)
                act.wait_ge(*full(j))
                f(wk(g * G, G, 0, 64), bank(j, 64), ACT.Relu, bias=vec("bg1", 0, p1=64)).then_inc(*act_step(j))
            for rc in range(2):
                for g in range(2):
                    j = J("l0a", "gate", rc, g)
                    act.wait_ge(*full(j))
                    f(wk(1024 + rc * N + g * G, G), bank(j), ACT.Sigmoid, bias=vec("bg2", rc)).then_inc(*act_step(act_to_dve))
                    act.wait_ge(*act_last())
                    act.sem_inc(bank_free[j % BANKS], 1)

            ln("l0x")
            for c in range(2):
                for i in range(2):
                    for k in range(2):
                        act.wait_ge(dve_to_act.sem, dve_to_act.next())
                        t = wk(4096 + (c * 4 + i * 2 + k) * N, N)
                        f(t, t, ACT.Exp).then_inc(*act_step(act_to_dve))

            ln("l0f")
            act.wait_ge(dve_to_act.sem, dve_to_act.next())
            f(wk(4096, 256), wk(4096, 256), ACT.Exp).then_inc(*act_step(act_to_dve))
            for e in range(NE):
                for g in range(2):
                    j = J("l0f", "gate", e, g)
                    act.wait_ge(*full(j))
                    if e >= 2:
                        act.wait_ge(*freed(J("l0f", "up", e - 2, g)))
                    f(wk(2048 + (e % 2) * N + g * G, G, 0, EI), bank(j, EI), ACT.Silu).then_inc(*act_step(act_to_dve))
                    act.wait_ge(*act_last())
                    act.sem_inc(bank_free[j % BANKS], 1)

            def values(layer):
                j = J(layer, "v")
                act.wait_ge(windows_zero, 1 if layer == "l1a" else 2)
                act.wait_ge(*full(j))
                f(ones_window[:, 24:32], cst("ones")[:, 0:8], ACT.Copy).then_inc(*act_step())
                act.wait_ge(*act_last())
                f(r3(v_windows[:, 24:24 + 2048], 32)[:, :, 0:8], r3(bank(j), 8), ACT.Copy).then_inc(*act_step(act_to_pe))
                act.wait_ge(*act_last())
                act.sem_inc(bank_free[j % BANKS], 1)

            def block_keys(layer, c, g, src, *to):
                for i in range(4):
                    f(wk((4 * c + i) * N + g * G, G), src, ACT.Copy, scale=cst("blk")[:, i:i + 1]).then_inc(*act_step(*(to if i == 3 else ())))

            def heads(layer):
                for key in heads_plan():
                    if key[0] == "t":
                        u = key[1]
                        j = J(layer, "t", u)
                        act.wait_ge(*full(j))
                        if u >= 16:
                            act.wait_ge(*full(J(layer, "pv", (u - 16) // 4)))
                        f(wk(8192 + (u % 16) * G, G), bank(j), ACT.Copy).then_inc(*act_step(j))
                    elif key[0] == "s":
                        act.wait_ge(dve_to_act.sem, dve_to_act.next())
                        t = wk(16384 + (key[1] % 3) * G, G)
                        f(t, t, ACT.Exp, scale=float(8 ** -0.5)).then_inc(*act_step(act_to_pe))

            ln("l1a")
            for c in range(2):
                for g in range(2):
                    act.wait_ge(dve_to_act.sem, dve_to_act.next())
                    block_keys("l1a", c, g, wk(8192 + (2 * c + g) * G, G))
            values("l1a")
            act.sem_inc(act_to_pe.sem, act_to_pe.give())
            heads("l1a")

            ln("l1x")
            for t in range(-4, 34):
                w, r = t // 4 + 1, t % 4
                if 0 <= t < 32:
                    for s_ in range(2):
                        j = J("l1x", "s", t, s_)
                        act.wait_ge(dve_to_act.sem, dve_to_act.next())
                        if s_ == 0 and t >= 2:
                            act.wait_ge(*full(J("l1x", "t", t - 2, 1)))
                        for i in range(2):
                            q = 2 * s_ + i
                            f(l1x_p(t)[:, q * D:(q + 1) * D], bank(j)[:, i * D:(i + 1) * D], ACT.Exp,
                              bias=sm(704 + (t % 4) * 16 + 4 + q, 1), scale=sm(640 + (t // 4 % 4) * 16 + s_ * 8 + r * 2 + i, 1),
                              accum_out=sm(704 + (t % 4) * 16 + 8 + q, 1)).then_inc(*act_step(*([act_to_dve] if i == 1 else [])))
                        act.wait_ge(*act_last())
                        act.sem_inc(bank_free[j % BANKS], 1)
                if w < 8:
                    if r == 0:
                        for i, n in enumerate(("k", "kc")):
                            j = J("l1x", n, w)
                            act.wait_ge(*full(j))
                            if w >= 1:
                                act.wait_ge(*full(J("l1x", "kc2", w - 1)))
                            if w >= 2:
                                act.wait_ge(*full(J("l1x", "s", 4 * w - 5, 1)))
                            f(l1x_k(w, 1 - i), r3(bank(j), P), ACT.Copy).then_inc(*act_step())
                            f(l1x_sq(i), bank(j), ACT.Square).then_inc(*act_step(act_to_dve))
                            act.wait_ge(*act_last())
                            act.sem_inc(bank_free[j % BANKS], 1)
                    for i, n in enumerate(("k2", "kc2") if r == 1 else ()):
                        j = J("l1x", n, w)
                        act.wait_ge(*full(j))
                        f(l1x_root[i], bank(j), ACT.Sqrt, bias=vec("eps6"), scale=1.0 / P).then_inc(*act_step(act_to_dve))
                        act.wait_ge(*act_last())
                        act.sem_inc(bank_free[j % BANKS], 1)
                    for hh in ((0, 1), (), (2, 3), ())[r]:
                        j = J("l1x", "q", w, hh)
                        act.wait_ge(*full(j))
                        if hh >= 2:
                            act.wait_ge(*full(J("l1x", "rq", w, 0)))
                        elif w >= 1:
                            act.wait_ge(*full(J("l1x", "rq", w - 1, 1)))
                        f(l1x_q(w, hh), bank(j), ACT.Copy).then_inc(*act_step())
                        f(l1x_sq(2 + hh % 2), bank(j), ACT.Square).then_inc(*act_step(act_to_dve))
                        act.wait_ge(*act_last())
                        act.sem_inc(bank_free[j % BANKS], 1)
                    if r % 2 == 1:
                        j = J("l1x", "rq", w, r // 2)
                        act.wait_ge(*full(j))
                        f(sm(640 + (w % 4) * 16 + (r // 2) * 8, 8), bank(j, P, 8), ACT.Sqrt, bias=vec("eps6"), scale=1.0 / P).then_inc(*act_step(act_to_dve))
                        act.wait_ge(*act_last())
                        act.sem_inc(bank_free[j % BANKS], 1)
                    if w % 4 == 0:
                        for kc, n in ((1, "v"), (0, "vc")):
                            j = J("l1x", n, w // 4, r)
                            act.wait_ge(*full(j))
                            f(l1x_v(w // 4, r, kc), bank(j), ACT.Copy).then_inc(*act_step(j))
                if 1 <= t < 33:
                    x = t - 1
                    j = J("l1x", "t", x, 1)
                    act.wait_ge(*full(j))
                    if x >= 2:
                        act.wait_ge(*full(J("l1x", "pv", x - 2)))
                    f(l1x_pt(x)[:, G:2 * G], bank(j), ACT.Copy).then_inc(*act_step(j))
                if 2 <= t:
                    x = t - 2
                    j = J("l1x", "pv", x)
                    act.wait_ge(*full(j))
                    if x >= 3:
                        act.wait_ge(*full(J("l1x", "o", x - 3)))
                    f(C[:, (x % 3) * G:(x % 3 + 1) * G], bank(j), ACT.Copy).then_inc(*act_step(j))

            ln("l1f")
            for e in range(8):
                for bp in range(4):
                    t = wk(((4 * e + bp) % 4) * G, G)
                    act.wait_ge(dve_to_act.sem, dve_to_act.next())
                    for i in range(2):
                        f(t[:, i * D:(i + 1) * D], t[:, i * D:(i + 1) * D], ACT.Relu,
                          scale=wk(5376, 64)[:, (2 * bp + i) * 8 + e:(2 * bp + i) * 8 + e + 1]).then_inc(*act_step(*([act_to_dve] if i else [])))

            def own_tap(j, dst, tap, bias):
                act.wait_ge(*full(j))
                f(dst, bank(j), ACT.Identity, scale=tap, bias=bias).then_inc(*act_step(act_to_dve))

            def softplus(lo, n):
                act.wait_ge(dve_to_act.sem, dve_to_act.next())
                f(wk(lo + n, n), wk(lo, n), ACT.Abs).then_inc(*act_step())
                act.wait_ge(*act_last())
                f(wk(lo + n, n), wk(lo + n, n), ACT.Exp, scale=-1.0).then_inc(*act_step())
                act.wait_ge(*act_last())
                f(wk(lo + n, n), wk(lo + n, n), ACT.Ln, bias=vec("one")).then_inc(*act_step(act_to_dve))

            ln("l2a")
            softplus(14336, 64)
            act.wait_ge(*act_last())
            f(sm(128, 8), vec("A_log"), ACT.Exp).then_inc(*act_step(act_to_dve))
            for g in range(2):
                for cc in range(7):
                    if cc < 6:
                        own_tap(J("l2a", "c", cc, g), wk(cc * N + g * G, G), vec("cw2", cc * 4 + 3), vec("cb2", cc))
                    if cc >= 1:
                        act.wait_ge(dve_to_act.sem, dve_to_act.next())
                        t = wk((cc - 1) * N + g * G, G)
                        f(t, t, ACT.Silu).then_inc(*act_step(*([act_to_pe] if cc == 6 else [])))
            for b in range(NB):
                j = J("l2a", "z", b)
                act.wait_ge(*full(j))
                f(wk(10240 + b * G, G), bank(j), ACT.Silu).then_inc(*act_step(j))
            for b in range(NB):
                j = J("l2a", "x", b)
                act.wait_ge(*full(j))
                f(wk(6144 + b * G, G), bank(j), ACT.Copy).then_inc(*act_step(j))
            for b in range(NB):
                for hh in range(2):
                    j = J("l2a", "seg", b, hh)
                    act.wait_ge(*full(j))
                    if b >= 2:
                        act.wait_ge(*full(J("l2a", "y", b - 2)))
                    f(wk(14336 + (b % 2) * 1024 + hh * G, G), bank(j), ACT.Exp).then_inc(*act_step(j))
            for b in range(NB):
                act.wait_ge(dve_to_act.sem, dve_to_act.next())
                if b == 0:
                    act.wait_ge(*full(J("l2a", "y", NB - 1)))
                act.wait_ge(*act_last())
                f(wk(14336 + (b % 2) * G, G), wk(10240 + b * G, G), ACT.Square, accum_out=sm(144 + b, 1)).then_inc(*act_step())
            act.wait_ge(*act_last())
            f(sm(152, 8), sm(144, 8), ACT.Sqrt, bias=vec("eps5"), scale=1.0 / 512).then_inc(*act_step(act_to_dve))
            for b in range(NB):
                j = J("l2a", "yt", b)
                act.wait_ge(*full(j))
                if b >= 4:
                    act.wait_ge(*full(J("l2a", "o", b - 4)))
                f(XT[:, (b % 4) * G:(b % 4 + 1) * G], bank(j), ACT.Copy).then_inc(*act_step(j))

            ln("l2x")
            for c in range(2):
                for g in range(2):
                    j = J("l2x", "q", c, g)
                    act.wait_ge(*full(j))
                    f(XN[:, c * N + g * G:c * N + (g + 1) * G], bank(j), ACT.Copy).then_inc(*act_step(j))
                    j = J("l2x", "k", c, g)
                    act.wait_ge(*full(j))
                    block_keys("l2x", c, g, bank(j), j)
            values("l2x")
            act.sem_inc(act_to_pe.sem, act_to_pe.give())
            heads("l2x")

            act.wait_ge(wb_in, 48)
            for i, n in enumerate(("gate", "up", "down")):
                f(wk(0, 2048), W(WB, W_L2F, n), ACT.Abs, accum_out=sm(128 + i, 1)).then_inc(*act_step(*([act_to_pe] if i == 2 else [])))
                act.wait_ge(*act_last())
            for g in range(2):
                act.wait_ge(dve_to_act.sem, dve_to_act.next())
                f(sm(80 + 4 * g, 4), sm(64 + 8 * g, 8).rearrange("p (b s) -> p b s", s=2)[:, :, 1], ACT.Sqrt,
                  bias=vec("eps5")).then_inc(*act_step(act_to_dve))
            act.wait_ge(dve_to_act.sem, dve_to_act.next())
            for b in range(NB):
                f(wk(b * D, D), XN[:, b * D:(b + 1) * D], ACT.Square, accum_out=sm(144 + b, 1)).then_inc(*act_step())
            act.wait_ge(*act_last())
            f(sm(152, 8), sm(144, 8), ACT.Sqrt, bias=vec("eps6"), scale=1.0 / D).then_inc(*act_step(act_to_dve))
            for g in range(2):
                for c in range(2):
                    j = J("l2f", "qt", g, c)
                    act.wait_ge(*full(j))
                    f(wkb(9216, 2048)[:, c * N + g * G:c * N + (g + 1) * G], bank(j).bitcast(BF16)[:, 0:G], ACT.Copy).then_inc(*act_step(j))
            act.wait_ge(dve_to_act.sem, dve_to_act.next())

            def squares(b):
                act.wait_ge(dve_to_act.sem, dve_to_act.next())
                f(wk(8192, 1024), wk(b * 1024, 1024), ACT.Square, accum_out=sm(144 + b, 1)).then_inc(*act_step())
                act.wait_ge(*act_last())

            for b in range(NB):
                for h in range(2):
                    j = J("l2f", "gate", b, h)
                    act.wait_ge(*full(j))
                    if b >= 1:
                        act.wait_ge(*freed(J("l2f", "up", b - 1, h)))
                    f(wk(10240 + h * G, G), bank(j), ACT.Silu, scale=sm(184 + b, 1)).then_inc(*act_step(act_to_dve))
                    act.wait_ge(*act_last())
                    act.sem_inc(bank_free[j % BANKS], 1)
                if b >= 1:
                    squares(b - 1)
            squares(NB - 1)
            f(sm(152, 8), sm(144, 8), ACT.Sqrt, bias=vec("eps6"), scale=1.0 / 1024).then_inc(*act_step(act_to_dve))
            for b in range(NB):
                j = J("l2f", "ht", b)
                act.wait_ge(*full(j))
                if b >= 4:
                    act.wait_ge(*full(J("l2f", "o", b - 4)))
                f(XT[:, (b % 4) * G:(b % 4 + 1) * G].bitcast(BF16), bank(j).bitcast(BF16), ACT.Copy).then_inc(*act_step(j))

            ln("l3a")
            softplus(13312, 512)
            for g in range(2):
                for cc in range(13):
                    if cc < 12:
                        own_tap(J("l3a", "c", cc, g), wk(cc * G, G), vec("cw3", cc * 4 + 3), vec("cb3", cc))
                    if cc >= 1:
                        act.wait_ge(dve_to_act.sem, dve_to_act.next())
                        t = wk((cc - 1) * G, G)
                        f(t, t, ACT.Silu).then_inc(*act_step(*([act_to_pe] if cc == 12 else [])))
                for cc in range(4):
                    j = J("l3a", "z", 4 * g + cc)
                    act.wait_ge(*full(j))
                    f(wk(8192 + cc * G, G), bank(j), ACT.Silu, bias=vec("z_bias", cc)).then_inc(*act_step(j))
                if g == 0:
                    act.wait_ge(windows_zero, 6)
                for i in range(4):
                    j = J("l3a", "x", 4 * g + i)
                    act.wait_ge(dve_to_act.sem, dve_to_act.next())
                    for c in range(4):
                        f(l3a_x(i).rearrange("p (a c w) -> p a c w", c=4, w=32)[:, :, c, c * 8:c * 8 + 8],
                          bank(j).rearrange("p (a c w) -> p a c w", c=4, w=8)[:, :, c, :], ACT.Copy).then_inc(*act_step(*([j] if c == 3 else [])))
                for u in range(32):
                    for hh in range(2):
                        j = J("l3a", "seg", g, u, hh)
                        act.wait_ge(*full(j))
                        if u >= 4:
                            act.wait_ge(*full(J("l3a", "y", g, (u - 4) // 2)))
                        f(wk(10240 + (u % 4) * 1024 + hh * G, G), bank(j), ACT.Exp).then_inc(*act_step(j))

            ln("l3x")
            for g in range(2):
                act.wait_ge(dve_to_act.sem, dve_to_act.next())
                f(wk(g * G, G), wk(g * G, G), ACT.Exp, scale=1.0 / 16).then_inc(*act_step(act_to_dve))
                act.wait_ge(*act_last())
                act.sem_inc(act_to_pe.sem, act_to_pe.give())
            for g in range(2):
                j = J("l3x", "t", g)
                act.wait_ge(*full(j))
                f(wk(1024 + g * G, G), bank(j), ACT.Copy).then_inc(*act_step(j))

            ln("l3f")
            act.wait_ge(dve_to_act.sem, dve_to_act.next())
            f(wk(4096, 128), wk(4096, 128), ACT.Exp).then_inc(*act_step(act_to_dve))
            j = J("l3f", "mt")
            act.wait_ge(*full(j))
            f(wkb(8256, 1024, 0, 16), bank(j, 16).bitcast(BF16), ACT.Copy).then_inc(*act_step(j))
            for m in range(8):
                for g in range(2):
                    j = J("l3f", "h", m, g)
                    act.wait_ge(*full(j))
                    f(wk(m * N + g * G, G), bank(j), ACT.Gelu).then_inc(*act_step(act_to_dve))
                    act.wait_ge(*act_last())
                    act.sem_inc(bank_free[j % BANKS], 1)

        @block.vector
        def _(dve):
            v = nc.vector
            J = lambda *k: job_of[k]

            def ln(layer):
                for g in range(2):
                    for b in range(4 * g, 4 * g + 4):
                        v.bn_stats(sm(b * 6, 6), X[:, b * D:(b + 1) * D]).then_inc(*dve_step())
                    dve.wait_ge(*dve_last())
                    for b in range(4 * g, 4 * g + 4):
                        v.bn_aggr(sm(64 + b * 2, 2), sm(b * 6, 6)).then_inc(*dve_step(*([dve_to_act] if b == 4 * g + 3 else [])))
                for g in range(2):
                    dve.wait_ge(act_to_dve.sem, act_to_dve.next())
                    v.reciprocal(sm(88 + 4 * g, 4), sm(80 + 4 * g, 4)).then_inc(*dve_step())
                    dve.wait_ge(*dve_last())
                    for b in range(4 * g, 4 * g + 4):
                        v.tensor_scalar(XN[:, b * D:(b + 1) * D], X[:, b * D:(b + 1) * D],
                                        sm(64 + 2 * b, 1), sm(88 + b, 1), ALU.subtract, ALU.mult).then_inc(*dve_step(dve_to_pe))
                dve.wait_ge(*dve_last())

            def residual(layer):
                for bp in range(4):
                    j = J(layer, "o", bp)
                    dve.wait_ge(*full(j))
                    x2 = X[:, bp * G:(bp + 1) * G]
                    v.tensor_tensor(x2, bank(j), x2, ALU.add).then_inc(*dve_step(j))
                dve.wait_ge(*dve_last())

            dve.wait_ge(cst_in, 64)
            v.tensor_copy(identb[:, :], cst("ident")).then_inc(*dve_step())
            v.tensor_copy(onesb[:, :], cst("ones")).then_inc(*dve_step())
            for i in range(4):
                v.tensor_copy(causalb[:, i * P:(i + 1) * P], cst("causal")).then_inc(*dve_step())
            v.memset(pad1[:, :], 0.0).then_inc(*dve_step())
            v.memset(pad0[:, :], 0.0).then_inc(*dve_step())
            dve.wait_ge(*dve_last())
            v.tensor_scalar(pad1[0:1, :], mk1[:, :], 0, NEG, ALU.is_equal, ALU.mult).then_inc(*dve_step())
            m8 = mk0[:, :].bitcast(mybir.dt.uint8)
            v.tensor_scalar(pad0[0:1, :], m8, 0, NEG, ALU.is_equal, ALU.mult).then_inc(*dve_step())
            v.tensor_reduce(valid[:, :], r3(m8, P), AX.X, ALU.max).then_inc(*dve_step())
            dve.wait_ge(x_in, 16)
            dve.wait_ge(*dve_last())
            v.tensor_scalar(valid[:, :], valid[:, :], 0.0, None, ALU.not_equal).then_inc(*dve_step())
            dve.wait_ge(*dve_last())

            ln("l0a")
            b3 = lambda ap: r3(ap, P)
            for g in range(2):
                for c in range(2):
                    dve.wait_ge(*freed(J("l0a", "ln", g, c)))
            for c in range(2):
                cv, x_ = wk(7168 + c * N, N), xt(c, 0, N)
                v.tensor_scalar(cv, x_, vec("cw0", c * 3 + 1), vec("cb0", c), ALU.mult, ALU.add).then_inc(*dve_step())
                dve.wait_ge(*dve_last())
                v.scalar_tensor_tensor(b3(cv)[:, :, 1:P], b3(x_)[:, :, 0:P - 1], vec("cw0", c * 3),
                                       b3(cv)[:, :, 1:P], ALU.mult, ALU.add).then_inc(*dve_step())
                dve.wait_ge(*dve_last())
                v.scalar_tensor_tensor(b3(cv)[:, :, 0:P - 1], b3(x_)[:, :, 1:P], vec("cw0", c * 3 + 2),
                                       b3(cv)[:, :, 0:P - 1], ALU.mult, ALU.add).then_inc(*dve_step())
                dve.wait_ge(*dve_last())
            for rc in range(2):
                for g in range(2):
                    gt = wk(1024 + rc * N + g * G, G)
                    ug, vg, cs = wk(3072, G), wk(3584, G), wk(4096, G)
                    dve.wait_ge(act_to_dve.sem, act_to_dve.next())
                    j = J("l0a", "u", rc, g)
                    dve.wait_ge(*full(j))
                    v.scalar_tensor_tensor(ug, bank(j), vec("bu", rc), gt, ALU.add, ALU.mult).then_inc(*dve_step(j))
                    j = J("l0a", "v", rc, g)
                    dve.wait_ge(*full(j))
                    v.scalar_tensor_tensor(vg, bank(j), vec("bv", rc), gt, ALU.add, ALU.mult).then_inc(*dve_step(j))
                    dve.wait_ge(*dve_last())
                    v.tensor_tensor_scan(cs, cst("nf"), ug, 0.0, ALU.mult, ALU.add).then_inc(*dve_step())
                    dve.wait_ge(*dve_last())
                    fin = [dve_to_pe] if (rc, g) == (1, 1) else []
                    v.tensor_tensor(wk(5120 + rc * N + g * G, G), cs, vg, ALU.mult).then_inc(*dve_step(*fin))
                    dve.wait_ge(*dve_last())
            residual("l0a")

            ln("l0x")
            for g in range(2):
                for c in range(2):
                    dve.wait_ge(*freed(J("l0x", "ln", g, c)))
                    dve.wait_ge(*freed(J("pre", "ctx", g, c)))
            wf = wk(12288, G)
            op_, o_, no = wk(12800, N), wk(13824, N), wk(14848, N)
            for c in range(2):
                k, ctxv = xt(c, 0, N), xt(c, 0, N, CT)
                v.scalar_tensor_tensor(r3(wf, P), r3(cst("nf"), P), vec("w", c), cst("first").unsqueeze(1).to_broadcast([P, 4, P]), ALU.mult, ALU.add).then_inc(*dve_step())
                dve.wait_ge(*dve_last())
                for h in range(2):
                    v.tensor_tensor_scan(o_[:, h * G:(h + 1) * G], wf, k[:, h * G:(h + 1) * G],
                                         -1e38, ALU.add, ALU.max).then_inc(*dve_step())
                    dve.wait_ge(*dve_last())
                v.memset(b3(op_)[:, :, 0:1], -1e38).then_inc(*dve_step())
                dve.wait_ge(*dve_last())
                v.tensor_copy(b3(op_)[:, :, 1:P], b3(o_)[:, :, 0:P - 1]).then_inc(*dve_step())
                dve.wait_ge(*dve_last())
                v.scalar_tensor_tensor(no, k, vec("u", c), op_, ALU.add, ALU.max).then_inc(*dve_step())
                dve.wait_ge(*dve_last())
                ea, ee, ea2, ee2 = (wk(4096 + (c * 4 + i) * N, N) for i in range(4))
                v.tensor_tensor(ea, op_, no, ALU.subtract).then_inc(*dve_step(dve_to_act))
                v.scalar_tensor_tensor(ee, k, vec("u", c), no, ALU.add, ALU.subtract).then_inc(*dve_step(dve_to_act))
                v.scalar_tensor_tensor(ea2, op_, vec("w", c), o_, ALU.add, ALU.subtract).then_inc(*dve_step(dve_to_act))
                v.tensor_tensor(ee2, k, o_, ALU.subtract).then_inc(*dve_step(dve_to_act))
                dve.wait_ge(*dve_last())
            for c in range(2):
                ctxv = xt(c, 0, N, CT)
                ea, ee, ea2, ee2 = (wk(4096 + (c * 4 + i) * N, N) for i in range(4))
                for _ in range(4):
                    dve.wait_ge(act_to_dve.sem, act_to_dve.next())
                ps_, qs_ = op_, o_
                v.tensor_tensor(no, ee2, ctxv, ALU.mult).then_inc(*dve_step())
                dve.wait_ge(*dve_last())
                for h in range(2):
                    s = slice(h * G, (h + 1) * G)
                    v.tensor_tensor_scan(ps_[:, s], ea2[:, s], no[:, s], 0.0, ALU.mult, ALU.add).then_inc(*dve_step())
                    dve.wait_ge(*dve_last())
                    v.tensor_tensor_scan(qs_[:, s], ea2[:, s], ee2[:, s], 0.0, ALU.mult, ALU.add).then_inc(*dve_step())
                    dve.wait_ge(*dve_last())
                v.tensor_tensor(b3(ps_)[:, :, 0:P - 1], b3(ea)[:, :, 1:P], b3(ps_)[:, :, 0:P - 1], ALU.mult).then_inc(*dve_step())
                dve.wait_ge(*dve_last())
                v.tensor_tensor(b3(qs_)[:, :, 0:P - 1], b3(ea)[:, :, 1:P], b3(qs_)[:, :, 0:P - 1], ALU.mult).then_inc(*dve_step())
                dve.wait_ge(*dve_last())
                v.tensor_tensor(no, ee, ctxv, ALU.mult).then_inc(*dve_step())
                dve.wait_ge(*dve_last())
                v.tensor_tensor(b3(no)[:, :, 1:P], b3(no)[:, :, 1:P], b3(ps_)[:, :, 0:P - 1], ALU.add).then_inc(*dve_step())
                dve.wait_ge(*dve_last())
                v.tensor_tensor(b3(ee)[:, :, 1:P], b3(ee)[:, :, 1:P], b3(qs_)[:, :, 0:P - 1], ALU.add).then_inc(*dve_step())
                dve.wait_ge(*dve_last())
                v.reciprocal(ee, ee).then_inc(*dve_step())
                dve.wait_ge(*dve_last())
                v.tensor_tensor(wk(c * N, N), no, ee, ALU.mult).then_inc(*dve_step(*([dve_to_pe] if c else [])))
                dve.wait_ge(*dve_last())
            residual("l0x")

            def topk(vals, n, k, width, v8, rl):
                for b in range(NB):
                    v.max(r3(v8, 8)[:, b, :], r3(vals, width)[:, b, 0:n]).then_inc(*dve_step())
                dve.wait_ge(*dve_last())
                v.memset(rl, LOW).then_inc(*dve_step())
                dve.wait_ge(*dve_last())
                v.tensor_copy(r3(rl, 8)[:, :, 0:k], r3(v8, 8)[:, :, 0:k]).then_inc(*dve_step())
                dve.wait_ge(*dve_last())
                for b in range(NB):
                    v.match_replace(r3(vals, width)[:, b, :], r3(rl, 8)[:, b, :],
                                    r3(vals, width)[:, b, :], IMM).then_inc(*dve_step())
                dve.wait_ge(*dve_last())

            def softmax_top(j, n, k, wt, bias=None):
                lg, e_ = wk(4096, NB * n), wk(4096, NB * n)
                dve.wait_ge(*full(j))
                v.tensor_reduce(sm(96, NB), r3(bank(j, P, NB * n), n), AX.X, ALU.max).then_inc(*dve_step())
                dve.wait_ge(*dve_last())
                v.tensor_tensor(r3(lg, n), r3(bank(j, P, NB * n), n),
                                sm(96, NB).unsqueeze(2).to_broadcast([P, NB, n]), ALU.subtract).then_inc(*dve_step(dve_to_act))
                dve.wait_ge(*dve_last())
                dve.sem_inc(bank_free[j % BANKS], 1)
                dve.wait_ge(*dve_last())
                dve.wait_ge(act_to_dve.sem, act_to_dve.next())
                width = n + 8 - k
                vals = wk(4608, NB * width)
                v.memset(vals, LOW).then_inc(*dve_step())
                dve.wait_ge(*dve_last())
                v.tensor_copy(r3(vals, width)[:, :, 0:n], r3(e_, n)).then_inc(*dve_step())
                dve.wait_ge(*dve_last())
                topk(vals, n, k, width, wk(5120, 64), wk(5184, 64))
                v.tensor_scalar(r3(wt, n), r3(vals, width)[:, :, 0:n], IMM, None, ALU.is_equal).then_inc(*dve_step())
                dve.wait_ge(*dve_last())
                return e_

            ln("l0f")
            wt = wk(5376, NB * NE)
            e_ = softmax_top(J("l0f", "r"), NE, 4, wt)
            v.tensor_tensor(wt, wt, e_, ALU.mult).then_inc(*dve_step())
            dve.wait_ge(*dve_last())
            v.tensor_reduce(sm(104, NB), r3(wt, NE), AX.X, ALU.add).then_inc(*dve_step())
            dve.wait_ge(*dve_last())
            v.reciprocal(sm(104, NB), sm(104, NB)).then_inc(*dve_step())
            dve.wait_ge(*dve_last())
            v.tensor_tensor(r3(wt, NE), r3(wt, NE), sm(104, NB).unsqueeze(2).to_broadcast([P, NB, NE]), ALU.mult).then_inc(*dve_step())
            dve.wait_ge(*dve_last())
            for e in range(NE + 1):
                if e < NE:
                    for g in range(2):
                        dve.wait_ge(act_to_dve.sem, act_to_dve.next())
                        j = J("l0f", "up", e, g)
                        dve.wait_ge(*full(j))
                        if e >= 2 and g == 0:
                            dve.wait_ge(*full(J("l0f", "down", e - 2, 3)))
                        v.tensor_tensor(wk((e % 2) * N + g * G, G, 0, EI), bank(j, EI),
                                        wk(2048 + (e % 2) * N + g * G, G, 0, EI), ALU.mult).then_inc(*dve_step(j))
                if e >= 1:
                    f = e - 1
                    dve.wait_ge(*dve_last())
                    for bp in range(4):
                        j = J("l0f", "down", f, bp)
                        dve.wait_ge(*full(j))
                        for i in range(2):
                            b = 2 * bp + i
                            x1 = X[:, b * D:(b + 1) * D]
                            v.scalar_tensor_tensor(x1, bank(j)[:, i * D:(i + 1) * D],
                                                   r3(wt, NE)[:, b, f:f + 1], x1, ALU.mult, ALU.add).then_inc(*dve_step(*([j] if i else [])))
            dve.wait_ge(*dve_last())

            def heads(layer):
                sub = ALU.subtract
                for key in heads_plan():
                    if key[0] == "s":
                        u = key[1]
                        j = J(layer, "s", u)
                        dve.wait_ge(*full(j))
                        mx = sm(704 + (u % 4) * 4, 4)
                        v.tensor_reduce(mx, r3(bank(j), P), AX.X, ALU.max).then_inc(*dve_step())
                        dve.wait_ge(*dve_last())
                        if u >= 3:
                            dve.wait_ge(*full(J(layer, "t", u - 3)))
                        v.tensor_tensor(r3(wk(16384 + (u % 3) * G, G), P), r3(bank(j), P),
                                        mx.unsqueeze(2).to_broadcast([P, 4, P]), sub).then_inc(*dve_step(dve_to_act))
                        dve.wait_ge(*dve_last())
                        dve.sem_inc(bank_free[j % BANKS], 1)
                    elif key[0] == "pv":
                        x = key[1]
                        bp, lo = x // 4, (x // 4 % 2) * G + (x % 4) * P
                        j = J(layer, "pv", x)
                        dve.wait_ge(*full(j))
                        rs = wk(17920, P)
                        v.reciprocal(rs, bank(j)[:, P:2 * P]).then_inc(*dve_step())
                        dve.wait_ge(*dve_last())
                        if bp >= 2:
                            dve.wait_ge(*full(J(layer, "o", bp - 2)))
                        v.tensor_tensor(XT[:, lo:lo + P], bank(j, P, P), rs, ALU.mult).then_inc(*dve_step(j))
                        dve.wait_ge(*dve_last())
                    elif key[0] == "o":
                        j = J(layer, "o", key[1])
                        dve.wait_ge(*full(j))
                        x2 = X[:, key[1] * G:(key[1] + 1) * G]
                        v.tensor_tensor(x2, bank(j), x2, ALU.add).then_inc(*dve_step(j))
                dve.wait_ge(*dve_last())

            ln("l1a")
            dve.wait_ge(*full(J("l1a", "ln", 1, 1)))
            tb = lambda ap: ap.unsqueeze(1).to_broadcast([P, 4, P])
            for c in range(2):
                for g in range(2):
                    for n, dst in (("q", XN[:, c * N + g * G:c * N + (g + 1) * G]), ("k", wk(8192 + (2 * c + g) * G, G))):
                        t = wk(12288, G)
                        j = J("l1a", n, c, g)
                        dve.wait_ge(*full(j))
                        v.tensor_tensor(r3(dst, P), r3(bank(j), P), tb(cst("cos1")), ALU.mult).then_inc(*dve_step(j))
                        j = J("l1a", n + "s", c, g)
                        dve.wait_ge(*full(j))
                        v.tensor_tensor(r3(t, P), r3(bank(j), P), tb(cst("sin1")), ALU.mult).then_inc(*dve_step(j))
                        dve.wait_ge(*dve_last())
                        v.tensor_tensor(dst, dst, t, ALU.add).then_inc(*dve_step(*([dve_to_act] if n == "k" else [])))
                        dve.wait_ge(*dve_last())
            heads("l1a")

            ln("l1x")
            qcos, qsin, kcos, ksin = (sm(128 + i * P, P) for i in range(4))
            v.tensor_scalar(qcos, cst("cosx"), vec("qn"), None, ALU.mult).then_inc(*dve_step())
            v.tensor_scalar(qsin, cst("sinx"), vec("qn"), -1.0, ALU.mult, ALU.mult).then_inc(*dve_step())
            v.tensor_scalar(kcos, cst("cosx"), vec("kn"), None, ALU.mult).then_inc(*dve_step())
            v.tensor_scalar(ksin, cst("sinx"), vec("kn"), -1.0, ALU.mult, ALU.mult).then_inc(*dve_step())
            dve.wait_ge(*dve_last())
            rot = WA[:, 4912:4912 + G]

            def rotate(q, cos, sin):
                h = lambda ap, lo: ap[lo:lo + 64]
                t = r3(rot, P)
                bc = lambda ap, lo: ap[lo:lo + 64, :].unsqueeze(1).to_broadcast([64, 4, P])
                v.tensor_tensor(h(t, 0), h(q, 64), bc(sin, 64), ALU.mult).then_inc(*dve_step())
                v.tensor_tensor(h(t, 64), h(q, 0), bc(sin, 0), ALU.mult).then_inc(*dve_step())
                dve.wait_ge(*dve_last())
                v.tensor_tensor(q, q, tb(cos), ALU.mult).then_inc(*dve_step())
                dve.wait_ge(*dve_last())
                v.tensor_tensor(q, q, t, ALU.add).then_inc(*dve_step())
                dve.wait_ge(*dve_last())

            def prepare(w, r):
                for _ in range(2 if r == 0 else 0):
                    dve.wait_ge(act_to_dve.sem, act_to_dve.next())
                for hh in ((0, 1), (), (2, 3), ())[r]:
                    dve.wait_ge(act_to_dve.sem, act_to_dve.next())
                    rotate(r3(l1x_q(w, hh), P), qcos, qsin)
                if r == 2:
                    dve.sem_inc(dve_to_pe.sem, dve_to_pe.give())
                for i in range(2 if r == 1 else 0):
                    dve.wait_ge(act_to_dve.sem, act_to_dve.next())
                    kk, root = l1x_k(w, 1 - i), l1x_root[i]
                    v.reciprocal(root, root).then_inc(*dve_step())
                    dve.wait_ge(*dve_last())
                    if i == 0:
                        rotate(kk, kcos, ksin)
                        v.tensor_tensor(kk, kk, r3(root, P), ALU.mult).then_inc(*dve_step())
                    else:
                        v.scalar_tensor_tensor(kk, kk, vec("kn"), r3(root, P), ALU.mult, ALU.mult).then_inc(*dve_step())
                    dve.wait_ge(*dve_last())
                if r % 2 == 1:
                    dve.wait_ge(act_to_dve.sem, act_to_dve.next())
                    rq = sm(640 + (w % 4) * 16 + (r // 2) * 8, 8)
                    v.reciprocal(rq, rq).then_inc(*dve_step())
                    dve.wait_ge(*dve_last())
                    v.tensor_scalar(rq, rq, float(P ** -0.5), None, ALU.mult).then_inc(*dve_step())
                    dve.wait_ge(*dve_last())

            for t in range(-3, 36):
                w, r = (t - 1) // 4 + 1, (t - 1) % 4
                base = 704 + (t % 4) * 16
                if w < 8 and r == 3:
                    prepare(w, r)
                if 0 <= t < 32:
                    for s_ in range(2):
                        j = J("l1x", "s", t, s_)
                        dve.wait_ge(*full(j))
                        v.tensor_reduce(sm(base + 2 * s_, 2), r3(bank(j), D), AX.X, ALU.max).then_inc(*dve_step())
                        dve.wait_ge(*dve_last())
                        v.scalar_tensor_tensor(sm(base + 4 + 2 * s_, 2), sm(base + 2 * s_, 2), -1.0,
                                               sm(640 + (t // 4 % 4) * 16 + s_ * 8 + (t % 4) * 2, 2), ALU.mult, ALU.mult).then_inc(*dve_step(dve_to_act))
                if 4 <= t:
                    x = t - 4
                    b = 4 * (x // 16) + x % 4
                    j = J("l1x", "o", x)
                    dve.wait_ge(*full(j))
                    x1 = X[:, b * D:(b + 1) * D]
                    v.tensor_tensor(x1, bank(j, P, D), x1, ALU.add).then_inc(*dve_step(j))
                if w < 8 and r != 3:
                    prepare(w, r)
                if 0 <= t < 32:
                    dve.wait_ge(act_to_dve.sem, act_to_dve.next())
                    dve.wait_ge(act_to_dve.sem, act_to_dve.next())
                    v.reciprocal(sm(base + 12, 4), sm(base + 8, 4)).then_inc(*dve_step())
                    dve.wait_ge(*dve_last())
                    for q in range(4):
                        pq = l1x_p(t)[:, q * D:(q + 1) * D]
                        v.tensor_scalar(pq, pq, sm(base + 12 + q, 1), None, ALU.mult).then_inc(*dve_step(*([dve_to_pe] if q == 3 else [])))
                if 1 <= t < 33:
                    x = t - 1
                    j = J("l1x", "t", x, 0)
                    dve.wait_ge(*full(j))
                    if x >= 2:
                        dve.wait_ge(*full(J("l1x", "pv", x - 2)))
                    v.tensor_copy(l1x_pt(x)[:, 0:G], bank(j)).then_inc(*dve_step(j))
            dve.wait_ge(*dve_last())

            ln("l1f")
            j = J("l1f", "r")
            dve.wait_ge(*full(j))
            width = 8 + 6
            vals, wt = wk(4608, NB * width), wk(5376, 64)
            v.memset(vals, LOW).then_inc(*dve_step())
            dve.wait_ge(*dve_last())
            v.tensor_tensor(r3(vals, width)[:, :, 0:8], r3(bank(j, P, 64), 8),
                            vec("gate_b").unsqueeze(1).to_broadcast([P, NB, 8]), ALU.add).then_inc(*dve_step(j))
            dve.wait_ge(*dve_last())
            topk(vals, 8, 2, width, wk(5120, 64), wk(5184, 64))
            v.tensor_scalar(r3(wt, 8), r3(vals, width)[:, :, 0:8], IMM, 0.5, ALU.is_equal, ALU.mult).then_inc(*dve_step())
            dve.wait_ge(*dve_last())
            dve.wait_ge(eb_in, 16)
            for n in range(32 + 2):
                if n < 32:
                    e, bp = n // 4, n % 4
                    j = J("l1f", "e", e, bp)
                    dve.wait_ge(*full(j))
                    v.tensor_tensor(r3(wk((n % 4) * G, G), D), r3(bank(j), D),
                                    expert_b[:, e * D:(e + 1) * D].unsqueeze(1).to_broadcast([P, 2, D]), ALU.add).then_inc(*dve_step(dve_to_act))
                    dve.wait_ge(*dve_last())
                    dve.sem_inc(bank_free[j % BANKS], 1)
                if n >= 2:
                    m = n - 2
                    dve.wait_ge(act_to_dve.sem, act_to_dve.next())
                    x2 = X[:, (m % 4) * G:(m % 4 + 1) * G]
                    v.tensor_tensor(x2, x2, wk((m % 4) * G, G), ALU.add).then_inc(*dve_step())
                    dve.wait_ge(*dve_last())

            def conv(j, dst, taps):
                dve.wait_ge(*full(j))
                dve.wait_ge(act_to_dve.sem, act_to_dve.next())
                p, d = r3(bank(j), P), r3(dst, P)
                for k in (1, 2, 3):
                    v.scalar_tensor_tensor(d[:, :, k:P], p[:, :, 0:P - k], vec(taps[0], taps[1] + 3 - k),
                                           d[:, :, k:P], ALU.mult, ALU.add).then_inc(*dve_step(*([dve_to_act] if k == 3 else [])))
                    dve.wait_ge(*dve_last())
                dve.sem_inc(bank_free[j % BANKS], 1)

            ln("l2a")
            b8 = lambda ap, m: ap.unsqueeze(2).to_broadcast([P, ap.shape[1], m])
            wo = W(WB, W_L2A, "out")
            dve.wait_ge(wb_in, 32)
            for cc in range(4):
                v.tensor_scalar(wo[:, cc * D:(cc + 1) * D], wo[:, cc * D:(cc + 1) * D], vec("nw2", cc), None, ALU.mult).then_inc(*dve_step())
            j = J("l2a", "dt")
            dve.wait_ge(*full(j))
            raw, dt, am = wk(14336, 64), wk(14464, 64), sm(160, 64)
            dt = sm(224, 64)
            v.tensor_tensor(r3(raw, 8), r3(bank(j, P, 64), 8), vec("dt_bias").unsqueeze(1).to_broadcast([P, NB, 8]), ALU.add).then_inc(*dve_step(dve_to_act))
            dve.wait_ge(*dve_last())
            dve.sem_inc(bank_free[j % BANKS], 1)
            dve.wait_ge(*dve_last())
            dve.wait_ge(act_to_dve.sem, act_to_dve.next())
            v.scalar_tensor_tensor(dt, raw, 0.0, wk(14400, 64), ALU.max, ALU.add).then_inc(*dve_step())
            dve.wait_ge(*dve_last())
            dve.wait_ge(act_to_dve.sem, act_to_dve.next())
            v.scalar_tensor_tensor(r3(am, 8), r3(dt, 8), -1.0, sm(128, 8).unsqueeze(1).to_broadcast([P, NB, 8]), ALU.mult, ALU.mult).then_inc(*dve_step())
            dve.wait_ge(*dve_last())
            for g in range(2):
                for cc in range(6):
                    conv(J("l2a", "c", cc, g), wk(cc * N + g * G, G), ("cw2", cc * 4))
            for b in range(NB + 2):
                if b < NB:
                    if b >= 2:
                        dve.wait_ge(*full(J("l2a", "seg", b - 2, 1)))
                    v.tensor_tensor(r3(XN[:, (b % 2) * 1024:(b % 2 + 1) * 1024], P), b8(am[:, b * 8:(b + 1) * 8], P),
                                    cst("tri").unsqueeze(1).to_broadcast([P, 8, P]), ALU.mult).then_inc(*dve_step(decay_steps))
                if 1 <= b <= NB:
                    x = b - 1
                    if x == 0:
                        dve.wait_ge(*freed(J("l2a", "x", NB - 1)))
                    xs, e_ = wk(6144 + x * G, G), wk(14336 + (x % 2) * 1024, 1024)
                    cbm = wk(17408 + (x % 2) * P, P)
                    j = J("l2a", "cb", x)
                    dve.wait_ge(*full(j))
                    v.tensor_tensor(cbm, bank(j, P, P), cst("tri"), ALU.mult).then_inc(*dve_step(j))
                    if x >= 2:
                        dve.wait_ge(*full(J("l2a", "y", x - 2)))
                    v.tensor_tensor(r3(wk(16384 + (x % 2) * G, G), 64), r3(xs, 64), b8(dt[:, x * 8:(x + 1) * 8], 64), ALU.mult).then_inc(*dve_step())
                    dve.wait_ge(*dve_last())
                    dve.wait_ge(*freed(J("l2a", "seg", x, 0)))
                    dve.wait_ge(*freed(J("l2a", "seg", x, 1)))
                    v.tensor_tensor(r3(e_, P), r3(e_, P), cbm.unsqueeze(1).to_broadcast([P, 8, P]), ALU.mult).then_inc(*dve_step(decayed_scores))
                    v.tensor_tensor(r3(xs, 64), r3(xs, 64), b8(vec("D2"), 64), ALU.mult).then_inc(*dve_step())
                if b >= 2:
                    x = b - 2
                    xs = wk(6144 + x * G, G)
                    j = J("l2a", "y", x)
                    dve.wait_ge(*full(j))
                    v.tensor_tensor(xs, bank(j), xs, ALU.add).then_inc(*dve_step(j))
                    dve.wait_ge(*dve_last())
                    dve.wait_ge(*freed(J("l2a", "z", x)))
                    v.tensor_tensor(wk(10240 + x * G, G), wk(10240 + x * G, G), xs, ALU.mult).then_inc(*dve_step(gated_y))
                    dve.wait_ge(*dve_last())
                    dve.sem_inc(dve_to_act.sem, dve_to_act.give())
                    dve.wait_ge(*dve_last())
            dve.wait_ge(act_to_dve.sem, act_to_dve.next())
            v.reciprocal(sm(152, 8), sm(152, 8)).then_inc(*dve_step())
            dve.wait_ge(*dve_last())

            def scaled_residual(layer, at):
                for b in range(NB):
                    j = J(layer, "o", b)
                    dve.wait_ge(*full(j))
                    x1 = X[:, b * D:(b + 1) * D]
                    v.scalar_tensor_tensor(x1, bank(j, P, D), sm(at + b, 1), x1, ALU.mult, ALU.add).then_inc(*dve_step(j))
                dve.wait_ge(*dve_last())

            scaled_residual("l2a", 152)

            ln("l2x")
            v.tensor_tensor(r3(X[:, :], D), r3(X[:, :], D), vec("b_o").unsqueeze(1).to_broadcast([P, NB, D]), ALU.add).then_inc(*dve_step())
            dve.wait_ge(*dve_last())
            for g in range(2):
                j = J("l2x", "mask", g)
                dve.wait_ge(*full(j))
                v.tensor_tensor(r3(masks[:, g * G:(g + 1) * G], P), r3(bank(j), P), cst("causal").unsqueeze(1).to_broadcast([P, 4, P]),
                                ALU.add).then_inc(*dve_step(j))
            heads("l2x")

            MAGIC = float(3 << 22)
            ln("l2f")
            dve.wait_ge(*dve_last())
            dve.sem_inc(dve_to_act.sem, dve_to_act.give())
            v.tensor_reduce(sm(160, 8), r3(XN[:, :], D), AX.X, ALU.max, apply_absolute_value=True).then_inc(*dve_step())
            dve.wait_ge(*dve_last())
            j = J("l2f", "ws")
            dve.wait_ge(*full(j))
            wm, wr = sm(128 + 8, 3), sm(128 + 11, 3)
            v.tensor_scalar(wm, bank(j, P, 3), 1.0 / (D * 1024), 1e-5, ALU.mult, ALU.max).then_inc(*dve_step(j))
            dve.wait_ge(*dve_last())
            v.reciprocal(wr, wm).then_inc(*dve_step())
            dve.wait_ge(*dve_last())

            def activation_scales(out_scale):
                dve.wait_ge(act_to_dve.sem, act_to_dve.next())
                v.reciprocal(sm(152, 8), sm(152, 8)).then_inc(*dve_step())
                dve.wait_ge(*dve_last())
                v.tensor_tensor(sm(160, 8), sm(160, 8), sm(152, 8), ALU.mult).then_inc(*dve_step())
                dve.wait_ge(*dve_last())
                v.tensor_scalar(sm(160, 8), sm(160, 8), 1e-5, None, ALU.max).then_inc(*dve_step())
                dve.wait_ge(*dve_last())
                v.reciprocal(sm(168, 8), sm(160, 8)).then_inc(*dve_step())
                dve.wait_ge(*dve_last())
                v.tensor_scalar(sm(168, 8), sm(168, 8), 127.0, None, ALU.mult).then_inc(*dve_step())
                dve.wait_ge(*dve_last())
                v.reciprocal(sm(176, 8), sm(168, 8)).then_inc(*dve_step())
                dve.wait_ge(*dve_last())
                v.tensor_tensor(sm(168, 8), sm(168, 8), sm(152, 8), ALU.mult).then_inc(*dve_step())
                dve.wait_ge(*dve_last())

            activation_scales(176)
            v.tensor_scalar(sm(184, 8), sm(176, 8), wm[:, 0:1], None, ALU.mult).then_inc(*dve_step())
            v.tensor_scalar(sm(192, 8), sm(176, 8), wm[:, 1:2], None, ALU.mult).then_inc(*dve_step(dve_to_act))
            for b in range(NB):
                xb = XN[:, b * D:(b + 1) * D]
                v.tensor_scalar(xb, xb, sm(168 + b, 1), MAGIC, ALU.mult, ALU.add).then_inc(*dve_step())
            dve.wait_ge(*dve_last())
            v.tensor_scalar(XN[:, :], XN[:, :], MAGIC - 128.0, MAGIC + 127.0, ALU.max, ALU.min).then_inc(*dve_step())
            dve.wait_ge(*dve_last())
            v.tensor_scalar(wkb(8192, 2048), XN[:, :], MAGIC, None, ALU.subtract).then_inc(*dve_step(dve_to_pe))
            dve.wait_ge(*dve_last())
            dve.wait_ge(wb_in, 48)
            for i, n in enumerate(("gate", "up", "down")):
                wx_ = W(WB, W_L2F, n)
                v.tensor_scalar(wx_, wx_, wr[:, i:i + 1], MAGIC, ALU.mult, ALU.add).then_inc(*dve_step())
                dve.wait_ge(*dve_last())
                v.tensor_scalar(wx_, wx_, MAGIC - 1.0, MAGIC + 1.0, ALU.max, ALU.min).then_inc(*dve_step())
                dve.wait_ge(*dve_last())
                v.tensor_scalar(wkb(11264, 6144)[:, i * 2048:(i + 1) * 2048], wx_, MAGIC, None, ALU.subtract).then_inc(*dve_step(*([dve_to_pe] if i == 2 else [])))
                dve.wait_ge(*dve_last())
            for b in range(NB):
                for h in range(2):
                    dve.wait_ge(act_to_dve.sem, act_to_dve.next())
                    j = J("l2f", "up", b, h)
                    dve.wait_ge(*full(j))
                    v.scalar_tensor_tensor(wk(b * 1024 + h * G, G), bank(j), sm(192 + b, 1), wk(10240 + h * G, G),
                                           ALU.mult, ALU.mult).then_inc(*dve_step(j))
                dve.wait_ge(*dve_last())
                dve.sem_inc(dve_to_act.sem, dve_to_act.give())
                v.tensor_reduce(sm(160 + b, 1), wk(b * 1024, 1024), AX.X, ALU.max, apply_absolute_value=True).then_inc(*dve_step())
            dve.wait_ge(*dve_last())
            activation_scales(176)
            v.tensor_scalar(sm(200, 8), sm(176, 8), wm[:, 2:3], None, ALU.mult).then_inc(*dve_step())
            dve.wait_ge(*dve_last())
            for b in range(NB):
                hb = wk(b * 1024, 1024)
                v.tensor_scalar(hb, hb, sm(168 + b, 1), MAGIC, ALU.mult, ALU.add).then_inc(*dve_step())
                dve.wait_ge(*dve_last())
                v.tensor_scalar(hb, hb, MAGIC - 128.0, MAGIC + 127.0, ALU.max, ALU.min).then_inc(*dve_step())
                dve.wait_ge(*dve_last())
                v.tensor_scalar(wkb(14336, 8192)[:, b * 1024:(b + 1) * 1024], hb, MAGIC, None, ALU.subtract).then_inc(*dve_step(dve_to_pe))
                dve.wait_ge(*dve_last())
            scaled_residual("l2f", 200)

            ln("l3a")
            raw, dt, rx = wk(13312, 512), wk(14336, 512), wk(14848, 512)
            j = J("l3a", "dt")
            dve.wait_ge(*full(j))
            v.tensor_copy(raw, bank(j)).then_inc(*dve_step(dve_to_act))
            dve.wait_ge(*dve_last())
            dve.sem_inc(bank_free[j % BANKS], 1)
            dve.wait_ge(*dve_last())
            dve.wait_ge(act_to_dve.sem, act_to_dve.next())
            v.scalar_tensor_tensor(dt, raw, 0.0, wk(13824, 512), ALU.max, ALU.add).then_inc(*dve_step())
            dve.wait_ge(*dve_last())
            v.reciprocal(rx, dt).then_inc(*dve_step())
            dve.wait_ge(*dve_last())
            v.tensor_tensor(r3(rx, 64), r3(rx, 64), vec("D3").unsqueeze(1).to_broadcast([P, NB, 64]), ALU.mult).then_inc(*dve_step())
            dve.wait_ge(*dve_last())
            v.tensor_scalar(dt, dt, -1.0, None, ALU.mult).then_inc(*dve_step())
            dve.wait_ge(*dve_last())
            for g in range(2):
                for cc in range(12):
                    conv(J("l3a", "c", cc, g), wk(cc * G, G), ("cw3", cc * 4))
                dve.wait_ge(*full(J("l3a", "x", 4 * g + 3)))
                for i in range(4):
                    b = 4 * g + i
                    v.tensor_tensor(r3(wk(i * G, G), 8), r3(bank(J("l3a", "x", b)), 8), b8(rx[:, b * 64:(b + 1) * 64], 8),
                                    ALU.mult).then_inc(*dve_step(dve_to_act))
                dve.wait_ge(*dve_last())
                dve.sem_inc(dve_to_pe.sem, dve_to_pe.give())

                def decay(u):
                    b, q8 = 4 * g + u // 8, u % 8
                    if u >= 2:
                        dve.wait_ge(*full(J("l3a", "seg", g, u - 2, 1)))
                    v.tensor_tensor(r3(XN[:, (u % 2) * 1024:(u % 2 + 1) * 1024], P), b8(dt[:, b * 64 + q8 * 8:b * 64 + q8 * 8 + 8], P),
                                    cst("tri").unsqueeze(1).to_broadcast([P, 8, P]), ALU.mult).then_inc(*dve_step(decay_steps))

                def scores(u):
                    e_ = wk(10240 + (u % 4) * 1024, 1024)
                    dve.wait_ge(*freed(J("l3a", "seg", g, u, 0)))
                    dve.wait_ge(*freed(J("l3a", "seg", g, u, 1)))
                    cbm = wk(16384 + (u % 2) * G + (u % 8 // 2) * P, P)
                    v.tensor_tensor(r3(e_, P), r3(e_, P), cbm.unsqueeze(1).to_broadcast([P, 8, P]), ALU.mult).then_inc(*dve_step(decayed_scores))

                def outp(b):
                    j = J("l3a", "o", b)
                    dve.wait_ge(*full(j))
                    x1 = X[:, b * D:(b + 1) * D]
                    v.tensor_tensor(x1, bank(j, P, D), x1, ALU.add).then_inc(*dve_step(j))

                decay(0)
                for t in range(18):
                    if t < 16:
                        decay(2 * t + 1)
                        for par in range(2 if t % 4 == 0 else 0):
                            j = J("l3a", "cb", g, t // 4, par)
                            dve.wait_ge(*full(j))
                            dve.wait_ge(*dve_last())
                            v.tensor_tensor(r3(wk(16384 + par * G, G), P), r3(bank(j), P),
                                            cst("tri").unsqueeze(1).to_broadcast([P, 4, P]), ALU.mult).then_inc(*dve_step(j))
                        if t % 4 == 0:
                            dve.wait_ge(*dve_last())
                        scores(2 * t)
                    if t >= 2:
                        p = t - 2
                        i, cc = p // 4, p % 4
                        j = J("l3a", "y", g, p)
                        dve.wait_ge(*full(j))
                        if p == 0:
                            dve.wait_ge(*freed(J("l3a", "z", 4 * g + 3)))
                        v.tensor_tensor(wk(17408 + (i % 2) * G + cc * P, P), bank(j, P, P), wk(8192 + cc * G + i * P, P),
                                        ALU.mult).then_inc(*dve_step(j))
                    if t < 16:
                        if t < 15:
                            decay(2 * t + 2)
                        scores(2 * t + 1)
                    if t >= 6 and (t - 6) % 4 == 0:
                        outp(4 * g + (t - 6) // 4)
                outp(4 * g + 3)
                dve.wait_ge(*dve_last())

            ln("l3x")
            for g in range(2):
                j = J("l3x", "s", g)
                dve.wait_ge(*full(j))
                v.tensor_reduce(sm(128 + 4 * g, 4), r3(bank(j), P), AX.X, ALU.max).then_inc(*dve_step())
                dve.wait_ge(*dve_last())
                v.tensor_tensor(r3(wk(g * G, G), P), r3(bank(j), P), b8(sm(128 + 4 * g, 4), P), ALU.subtract).then_inc(*dve_step(dve_to_act))
                dve.wait_ge(*dve_last())
                dve.sem_inc(bank_free[j % BANKS], 1)
            j = J("l3x", "val")
            dve.wait_ge(*full(j))
            v.tensor_copy(sm(136, 8), bank(j, P, 8)).then_inc(*dve_step(j))
            for g in range(2):
                dve.wait_ge(act_to_dve.sem, act_to_dve.next())
                v.tensor_reduce(sm(144 + 4 * g, 4), r3(wk(g * G, G), P), AX.X, ALU.add).then_inc(*dve_step())
                dve.wait_ge(*dve_last())
            v.reciprocal(sm(144, 8), sm(144, 8)).then_inc(*dve_step())
            dve.wait_ge(*dve_last())
            v.tensor_tensor(sm(144, 8), sm(144, 8), sm(136, 8), ALU.mult).then_inc(*dve_step())
            dve.wait_ge(*dve_last())
            for bp in range(4):
                j = J("l3x", "o", bp)
                dve.wait_ge(*full(j))
                for i in range(2):
                    b = 2 * bp + i
                    x1 = X[:, b * D:(b + 1) * D]
                    v.scalar_tensor_tensor(x1, bank(j)[:, i * D:(i + 1) * D], sm(144 + b, 1), x1, ALU.mult, ALU.add).then_inc(*dve_step(*([j] if i else [])))
            dve.wait_ge(*dve_last())

            ln("l3f")
            j = J("l3f", "r")
            dve.wait_ge(*full(j))
            lg = wk(4096, 128)
            v.tensor_tensor(r3(lg, 16), r3(bank(j, P, 128), 16), vec("br").unsqueeze(1).to_broadcast([P, NB, 16]), ALU.add).then_inc(*dve_step(j))
            dve.wait_ge(*dve_last())
            v.tensor_reduce(sm(128, 8), r3(lg, 16), AX.X, ALU.max).then_inc(*dve_step())
            dve.wait_ge(*dve_last())
            v.tensor_tensor(r3(lg, 16), r3(lg, 16), b8(sm(128, 8), 16), ALU.subtract).then_inc(*dve_step(dve_to_act))
            dve.wait_ge(*dve_last())
            dve.wait_ge(act_to_dve.sem, act_to_dve.next())
            width = 16 + 4
            vals = wk(4608, NB * width)
            v.memset(vals, LOW).then_inc(*dve_step())
            dve.wait_ge(*dve_last())
            v.tensor_copy(r3(vals, width)[:, :, 0:16], r3(lg, 16)).then_inc(*dve_step())
            dve.wait_ge(*dve_last())
            topk(vals, 16, 4, width, wk(5120, 64), wk(5184, 64))
            v.tensor_copy(r3(wkb(8768, 1024, 0, 16), 64), cst("ident", 0, 16)[:, 0:16].unsqueeze(2).to_broadcast([16, 16, 64])).then_inc(*dve_step())
            v.tensor_scalar(r3(wkb(8192, 128), 16), r3(vals, width)[:, :, 0:16], IMM, None, ALU.is_equal).then_inc(*dve_step(dve_to_pe))
            dve.wait_ge(*dve_last())
            for m in range(8):
                for g in range(2):
                    dve.wait_ge(act_to_dve.sem, act_to_dve.next())
                    j = J("l3f", "m", m, g)
                    dve.wait_ge(*full(j))
                    t = wk(m * N + g * G, G)
                    v.tensor_tensor(t, bank(j), t, ALU.mult).then_inc(*dve_step(j))
            residual("l3f")
            dve.sem_inc(x_final, 1)


def _cols(w):
    w = np.asarray(w)
    if w.shape[0] < P:
        w = np.concatenate([w, np.zeros((P - w.shape[0], w.shape[1]), w.dtype)])
    return w.reshape(-1, P, w.shape[1]).transpose(1, 0, 2).reshape(P, -1)


def _row(v):
    return np.broadcast_to(np.asarray(v).reshape(1, -1), (P, np.asarray(v).size))


def _chan(v):
    v = np.asarray(v)
    return _cols(v.reshape(v.shape[0], -1))


def _constants():
    i = np.arange(P)
    c = {}
    c["ident"] = np.eye(P)
    c["tri"] = (i[:, None] <= i[None, :]) * 1.0
    c["strict"] = (i[:, None] > i[None, :]) * 1.0
    c["ones"] = np.ones((P, P))
    c["causal"] = np.where(i[None, :] > i[:, None], NEG, 0.0)
    th = (1.0 / 10000.0 ** (2.0 * np.arange(4) / 8)).astype(np.float32)
    ang = (np.arange(P, dtype=np.float32)[:, None] * th[None, :]).astype(np.float32)
    d = i % 8
    c["cos1"] = np.cos(ang[:, d // 2]).T
    c["sin1"] = np.sin(ang[:, d // 2]).T * np.where(d % 2 == 0, -1.0, 1.0)[:, None]
    inv = (1.0 / 10000.0 ** (np.arange(0, P, 2, dtype=np.float32) / P)).astype(np.float32)
    ang = (np.arange(P, dtype=np.float32)[:, None] * inv[None, :]).astype(np.float32)
    c["cosx"] = np.cos(ang[:, i % 64]).T
    c["sinx"] = np.sin(ang[:, i % 64]).T * np.where(i < 64, -1.0, 1.0)[:, None]
    t = np.arange(G) % P
    c["nf"] = np.broadcast_to((t > 0) * 1.0, (P, G))
    c["first"] = np.broadcast_to(np.where(i > 0, 0.0, -1e38), (P, P))
    c["blk"] = ((i[:, None] // 8) % 4 == np.arange(4)[None, :]) * 1.0
    return np.concatenate([c[k] for k in CST], axis=1).astype(np.float32)


def _layout(z):
    swap = np.arange(D).reshape(-1, 2)[:, ::-1].reshape(-1)
    half = np.concatenate([np.arange(64, 128), np.arange(0, 64)])
    krep = (np.arange(8)[:, None, None] * 8 + np.zeros((1, 4, 1), int) + np.arange(8)[None, None, :]).reshape(-1)
    v = {
        "bu": _chan(z["L0_attn_bu"]), "bv": _chan(z["L0_attn_bv"]), "bg1": _chan(z["L0_attn_bg1"]),
        "bg2": _chan(z["L0_attn_bg2"]), "cw0": _chan(z["L0_attn_conv_w"]), "cb0": _chan(z["L0_attn_conv_b"]),
        "w": _chan(z["L0_xattn_w"]), "u": _chan(z["L0_xattn_u"]), "rw0": _cols(z["L0_ffn_router_w"].T),
        "qn": _chan(z["L1_xattn_q_norm_w"]), "kn": _chan(z["L1_xattn_k_norm_w"]),
        "qns": _chan(z["L1_xattn_q_norm_w"][half]), "kns": _chan(z["L1_xattn_k_norm_w"][half]),
        "cw2": _chan(z["L2_attn_conv_w"]), "cb2": _chan(z["L2_attn_conv_b"]), "nw2": _chan(z["L2_attn_norm_w"]),
        "cw3": _chan(z["L3_attn_conv1d_weight"]), "cb3": _chan(z["L3_attn_conv1d_bias"]),
        "gate_b": _row(z["L1_ffn_gate_b"]), "dt_bias": _row(z["L2_attn_dt_bias"]), "A_log": _row(z["L2_attn_A_log"]),
        "D2": _row(z["L2_attn_D_param"]), "D3": _row(z["L3_attn_D"]), "br": _row(z["L3_ffn_br"]),
        "z_bias": _chan(z["L3_attn_z_bias"]), "b_o": _row(z["L2_xattn_b_o"]),
        "eps5": _row([1e-5]), "eps6": _row([1e-6]), "one": _row([1.0]), "zero": _row([0.0]),
    }
    for name, n in VEC.items():
        assert v[name].shape == (P, n), (name, v[name].shape)
    o = {"x": z["x"], "ctx": z["ctx_2048"], "cst": _constants(),
         "vec": np.concatenate([v[k] for k in VEC], axis=1).astype(np.float32)}
    cat = lambda *l: np.concatenate(l, axis=1)
    o["l0a"] = cat(_cols(z["L0_attn_Wu"].T), _cols(z["L0_attn_Wv"].T), _cols(z["L0_attn_Wg1"].T),
                   _cols(z["L0_attn_Wg2"].T))
    o["l0f"] = cat(*[cat(_cols(z["L0_ffn_gate_w"][e].T), _cols(z["L0_ffn_up_w"][e].T), _cols(z["L0_ffn_down_w"][e].T))
                     for e in range(NE)])
    q, k = z["L1_attn_Wq"], z["L1_attn_Wk"][:, krep]
    o["l1a"] = cat(_cols(q), _cols(q[:, swap]), _cols(k), _cols(k[:, swap]), _cols(z["L1_attn_Wv"]), _cols(z["L1_attn_Wo"]))
    o["l1x"] = cat(*[_cols(z["L1_xattn_" + n]) for n in ("wq", "wk", "wv", "wk_ctx", "wv_ctx", "wo")])
    o["l1f"] = cat(_cols(z["L1_ffn_gate_w"]), *[_cols(z["L1_ffn_expert_w"][e]) for e in range(8)])
    o["eb"] = _row(z["L1_ffn_expert_b"])
    o["l2a"] = cat(_cols(z["L2_attn_W_in"]), _cols(z["L2_attn_W_out"]))
    o["l2x"] = cat(_cols(z["L2_xattn_w_q"].T), _cols(z["L2_xattn_w_k"].T[:, krep]), _cols(z["L2_xattn_w_v"].T), _cols(z["L2_xattn_w_o"].T))
    o["l2f"] = cat(_cols(z["L2_ffn_w_gate"].T), _cols(z["L2_ffn_w_up"].T), _cols(z["L2_ffn_w_down"].T))
    o["l3a"] = cat(_cols(z["L3_attn_in_proj_w"].T), _cols(z["L3_attn_out_proj_w"].T))
    o["l3f"] = cat(_cols(z["L3_ffn_Wr"].T), _cols(z["L3_ffn_W1"].T), _cols(z["L3_ffn_W2"].T))
    o["m1"] = z["mask_BxS2_if1"].reshape(1, -1)
    o["m0"] = z["mask_BxS2_bk0"].reshape(1, -1).view(np.int32)
    return {n: np.ascontiguousarray(t) for n, t in o.items()}


def kernel(**inputs):
    import concourse.bacc as bacc
    from concourse.bass_utils import run_bass_kernel_spmd

    laid = _layout({k: np.asarray(t) for k, t in inputs.items()})
    nc = bacc.Bacc("TRN2", target_bir_lowering=False, num_devices=1)
    aps = {n: nc.dram_tensor(f"in_{n}", t.shape, mybir.dt.from_np(t.dtype), kind="ExternalInput").ap()
           for n, t in laid.items()}
    out = nc.dram_tensor("out_0", (NB, P, D), F32, kind="ExternalOutput").ap()
    build(nc, aps, out)
    r = run_bass_kernel_spmd(nc, [{f"in_{n}": t for n, t in laid.items()}], core_ids=[0])
    return r.results[0]["out_0"]
```
